# Optimizing a Trainium2 kernel written in Bass

```python
import numpy as np
import jax
import jax.numpy as jnp

def _softmax(x, axis=-1):
    return jax.nn.softmax(x, axis=axis)

def _gelu(x):
    return jax.nn.gelu(x, approximate=True)

def _silu(x):
    return jax.nn.silu(x)

def _sigmoid(x):
    return jax.nn.sigmoid(x)

def _layernorm(x, axis=-1, eps=1e-05):
    m = jnp.mean(x, axis=axis, keepdims=True)
    v = jnp.var(x, axis=axis, keepdims=True)
    return (x - m) / jnp.sqrt(v + eps)

def _scatter_add(tgt, idx, src, axis=0):
    return tgt.at[idx].add(src)

def _segment_sum(src, seg, n):
    return jax.ops.segment_sum(src, seg, n)
kernel_name = 'mk_decoder_preln_d1_seqx_r4_e3e38f'

def setup_inputs(seed: int=0):
    np.random.seed(seed)
    _w = jnp.asarray

    def _rec_inputs():
        import jax
        import jax.numpy as jnp
        _rk = jax.random.key(seed)
        x = -0.000125 + 0.9999 * jax.random.normal(jax.random.fold_in(_rk, 1), (8, 112, 512), jnp.float32)
        _lenS = 112 - jax.random.randint(jax.random.fold_in(_rk, 7), (8,), 0, max(1, 112 // 4) + 1, jnp.int32)
        _lenS2 = 375 - jax.random.randint(jax.random.fold_in(_rk, 8), (8,), 0, max(1, 375 // 4) + 1, jnp.int32)
        _ctx_2048P = jax.random.normal(jax.random.fold_in(_rk, 11), (8, 16, 512), jnp.float32)
        _ctx_2048c = jax.random.dirichlet(jax.random.fold_in(_rk, 511), 0.3 * jnp.ones((16,), jnp.float32), (8, 375))
        _ctx_2048t = jnp.einsum('bsk,bkd->bsd', _ctx_2048c, _ctx_2048P)
        _ctx_2048t = _ctx_2048t * jax.lax.rsqrt(jnp.mean(jnp.square(_ctx_2048t)) + 1e-12) * 0.953939
        ctx_2048 = 1.72703e-05 + 1.00003 * (_ctx_2048t + 0.3 * jax.random.normal(jax.random.fold_in(_rk, 611), (8, 375, 512), jnp.float32))
        return (x, ctx_2048)
    x, ctx_2048 = _rec_inputs()

    def _L0_attn_setup():
        import jax, jax.numpy as jnp
        import numpy as np
        DIM = 512
        N_HEADS = 16
        N_KV_HEADS = 4
        WINDOW = 128
        GLOBAL = 64

        def alibi_slopes(num_heads):
            closest_pow2 = 2.0 ** np.floor(np.log2(num_heads))
            base = 2.0 ** (-2.0 ** (-(np.log2(closest_pow2) - 3.0)))
            powers = np.arange(1, 1 + num_heads, dtype=np.float32)
            return jnp.asarray(base ** powers, dtype=jnp.float32)

        def window_allowed(seq_len):
            i = jnp.arange(seq_len)[:, None]
            j = jnp.arange(seq_len)[None, :]
            inside = (j >= i - WINDOW // 2) & (j <= i + WINDOW // 2)
            glob = (i < GLOBAL) | (j < GLOBAL)
            return inside | glob
        key = jax.random.key(seed)
        k1, k2, k3, k4 = jax.random.split(key, 4)
        B, S, D = (2, 512, DIM)
        kv_feat = 2 * D * N_KV_HEADS // N_HEADS
        std = 0.02
        x = jax.random.normal(k1, (B, S, D), dtype=jnp.float32)
        Wq = jax.random.normal(k2, (D, D), dtype=jnp.float32) * std
        Wkv = jax.random.normal(k3, (D, kv_feat), dtype=jnp.float32) * std
        Wo = jax.random.normal(k4, (D, D), dtype=jnp.float32) * std
        bo = jnp.zeros((D,), dtype=jnp.float32)
        return {'x': x, 'Wq': Wq, 'Wkv': Wkv, 'Wo': Wo, 'bo': bo}
    _L0_attn_all = _L0_attn_setup()
    _L0_attn_in = {k: v for k, v in _L0_attn_all.items() if k in ('Wq', 'Wkv', 'Wo', 'bo')}
    del _L0_attn_all

    def _L0_xattn_setup():
        import jax, jax.numpy as jnp
        import numpy as np
        DIM = 512
        NH = 16
        HD = DIM // NH
        EPS = 1e-06
        IMG_LEN = 257

        def rms_norm(x, w, eps=EPS):
            xf = x.astype(jnp.float32)
            y = xf * jax.lax.rsqrt(jnp.mean(xf * xf, axis=-1, keepdims=True) + eps)
            return y.astype(x.dtype) * w

        def linear(x, w, b):
            return jnp.einsum('blc,oc->blo', x, w) + b

        def attention(q, k, v):
            scale = 1.0 / jnp.sqrt(jnp.asarray(HD, q.dtype))
            scores = jnp.einsum('bqhd,bkhd->bhqk', q, k) * scale
            probs = jax.nn.softmax(scores, axis=-1)
            return jnp.einsum('bhqk,bkhd->bqhd', probs, v)
        key = jax.random.key(seed)
        ks = jax.random.split(key, 12)
        B, L = (2, 2048)
        s = 0.02
        inp = {'x': jax.random.normal(ks[0], (B, L, DIM), jnp.float32), 'context': jax.random.normal(ks[1], (B, 769, DIM), jnp.float32), 'q_w': jax.random.normal(ks[2], (DIM, DIM), jnp.float32) * s, 'q_b': jnp.zeros((DIM,), jnp.float32), 'k_w': jax.random.normal(ks[3], (DIM, DIM), jnp.float32) * s, 'k_b': jnp.zeros((DIM,), jnp.float32), 'v_w': jax.random.normal(ks[4], (DIM, DIM), jnp.float32) * s, 'v_b': jnp.zeros((DIM,), jnp.float32), 'k_img_w': jax.random.normal(ks[5], (DIM, DIM), jnp.float32) * s, 'k_img_b': jnp.zeros((DIM,), jnp.float32), 'v_img_w': jax.random.normal(ks[6], (DIM, DIM), jnp.float32) * s, 'v_img_b': jnp.zeros((DIM,), jnp.float32), 'o_w': jax.random.normal(ks[7], (DIM, DIM), jnp.float32) * s, 'o_b': jnp.zeros((DIM,), jnp.float32), 'norm_q_w': jnp.ones((DIM,), jnp.float32), 'norm_k_w': jnp.ones((DIM,), jnp.float32), 'norm_k_img_w': jnp.ones((DIM,), jnp.float32)}
        return inp
    _L0_xattn_all = _L0_xattn_setup()
    _L0_xattn_in = {k: v for k, v in _L0_xattn_all.items() if k in ('q_w', 'q_b', 'k_w', 'k_b', 'v_w', 'v_b', 'k_img_w', 'k_img_b', 'v_img_w', 'v_img_b', 'o_w', 'o_b', 'norm_q_w', 'norm_k_w', 'norm_k_img_w')}
    del _L0_xattn_all

    def _L0_ffn_setup():
        import jax, jax.numpy as jnp
        import numpy as np
        GOLDEN_CENTER = 1.0 / np.e
        GOLDEN_LOWER = 0.5 - np.log(4.0 / 3.0)
        GOLDEN_UPPER = 0.5

        def _golden_weights(x, Wr, temperature):
            inh = jax.nn.sigmoid(x @ Wr / temperature)
            in_zone = (inh >= GOLDEN_LOWER) & (inh <= GOLDEN_UPPER)
            distance = jnp.abs(inh - GOLDEN_CENTER)
            weights = jnp.exp(-distance / 0.1) * in_zone.astype(x.dtype)
            wsum = jnp.sum(weights, axis=-1, keepdims=True)
            no_expert = wsum < 1e-08
            fb = jnp.exp(-distance / 0.3)
            _, top2 = jax.lax.top_k(fb, 2)
            fb_mask = jnp.sum(jax.nn.one_hot(top2, weights.shape[-1], dtype=x.dtype), axis=-2)
            fb_w = fb * fb_mask
            fb_w = fb_w / jnp.maximum(jnp.sum(fb_w, axis=-1, keepdims=True), 1e-08)
            weights = jnp.where(no_expert, fb_w, weights)
            weights = weights / jnp.maximum(jnp.sum(weights, axis=-1, keepdims=True), 1e-08)
            return weights
        key = jax.random.key(seed)
        ks = jax.random.split(key, 5)
        B, T, D, E, F = (2, 512, 512, 8, 512)
        s_in = 1.0 / np.sqrt(D)
        s_f = 1.0 / np.sqrt(F)
        return {'x': jax.random.normal(ks[0], (B, T, D), dtype=jnp.float32), 'Wg': jax.random.normal(ks[1], (E, D, F), dtype=jnp.float32) * s_in, 'Wu': jax.random.normal(ks[2], (E, D, F), dtype=jnp.float32) * s_in, 'Wd': jax.random.normal(ks[3], (E, F, D), dtype=jnp.float32) * s_f, 'Wr': jax.random.normal(ks[4], (D, E), dtype=jnp.float32) * s_in, 'temperature': jnp.ones((1,), dtype=jnp.float32)}
    _L0_ffn_all = _L0_ffn_setup()
    _L0_ffn_in = {k: v for k, v in _L0_ffn_all.items() if k in ('Wg', 'Wu', 'Wd', 'Wr', 'temperature')}
    del _L0_ffn_all
    return {'x': x, 'ctx_2048': ctx_2048, 'L0_attn_Wq': _L0_attn_in['Wq'], 'L0_attn_Wkv': _L0_attn_in['Wkv'], 'L0_attn_Wo': _L0_attn_in['Wo'], 'L0_attn_bo': _L0_attn_in['bo'], 'L0_xattn_q_w': _L0_xattn_in['q_w'], 'L0_xattn_q_b': _L0_xattn_in['q_b'], 'L0_xattn_k_w': _L0_xattn_in['k_w'], 'L0_xattn_k_b': _L0_xattn_in['k_b'], 'L0_xattn_v_w': _L0_xattn_in['v_w'], 'L0_xattn_v_b': _L0_xattn_in['v_b'], 'L0_xattn_k_img_w': _L0_xattn_in['k_img_w'], 'L0_xattn_k_img_b': _L0_xattn_in['k_img_b'], 'L0_xattn_v_img_w': _L0_xattn_in['v_img_w'], 'L0_xattn_v_img_b': _L0_xattn_in['v_img_b'], 'L0_xattn_o_w': _L0_xattn_in['o_w'], 'L0_xattn_o_b': _L0_xattn_in['o_b'], 'L0_xattn_norm_q_w': _L0_xattn_in['norm_q_w'], 'L0_xattn_norm_k_w': _L0_xattn_in['norm_k_w'], 'L0_xattn_norm_k_img_w': _L0_xattn_in['norm_k_img_w'], 'L0_ffn_Wg': _L0_ffn_in['Wg'], 'L0_ffn_Wu': _L0_ffn_in['Wu'], 'L0_ffn_Wd': _L0_ffn_in['Wd'], 'L0_ffn_Wr': _L0_ffn_in['Wr'], 'L0_ffn_temperature': _L0_ffn_in['temperature']}

def reference(x, ctx_2048, L0_attn_Wq, L0_attn_Wkv, L0_attn_Wo, L0_attn_bo, L0_xattn_q_w, L0_xattn_q_b, L0_xattn_k_w, L0_xattn_k_b, L0_xattn_v_w, L0_xattn_v_b, L0_xattn_k_img_w, L0_xattn_k_img_b, L0_xattn_v_img_w, L0_xattn_v_img_b, L0_xattn_o_w, L0_xattn_o_b, L0_xattn_norm_q_w, L0_xattn_norm_k_w, L0_xattn_norm_k_img_w, L0_ffn_Wg, L0_ffn_Wu, L0_ffn_Wd, L0_ffn_Wr, L0_ffn_temperature):
    import jax
    import jax.numpy as jnp

    def _L0_attn_ref(x, Wq, Wkv, Wo, bo):
        import jax, jax.numpy as jnp
        import numpy as np
        DIM = 512
        N_HEADS = 16
        N_KV_HEADS = 4
        WINDOW = 128
        GLOBAL = 64

        def alibi_slopes(num_heads):
            closest_pow2 = 2.0 ** np.floor(np.log2(num_heads))
            base = 2.0 ** (-2.0 ** (-(np.log2(closest_pow2) - 3.0)))
            powers = np.arange(1, 1 + num_heads, dtype=np.float32)
            return jnp.asarray(base ** powers, dtype=jnp.float32)

        def window_allowed(seq_len):
            i = jnp.arange(seq_len)[:, None]
            j = jnp.arange(seq_len)[None, :]
            inside = (j >= i - WINDOW // 2) & (j <= i + WINDOW // 2)
            glob = (i < GLOBAL) | (j < GLOBAL)
            return inside | glob
        B, S, D = x.shape
        H, KVH = (N_HEADS, N_KV_HEADS)
        hd = D // H
        r = H // KVH
        cw = jax.nn.sigmoid(jnp.sum(jnp.abs(x), axis=-1, keepdims=True))
        q = jnp.dot(x * cw, Wq)
        kv = jnp.dot(x, Wkv)
        k, v = jnp.split(kv, 2, axis=-1)
        q = q.reshape(B, S, H, hd).transpose(0, 2, 1, 3)
        k = k.reshape(B, S, KVH, hd).transpose(0, 2, 1, 3)
        v = v.reshape(B, S, KVH, hd).transpose(0, 2, 1, 3)
        k = jnp.repeat(k, r, axis=1)
        v = jnp.repeat(v, r, axis=1)
        scale = 1.0 / jnp.sqrt(jnp.float32(hd))
        qk = jnp.einsum('bhid,bhjd->bhij', q, k) * scale
        pos = jnp.arange(S)
        dist = -jnp.abs(pos[:, None] - pos[None, :]).astype(jnp.float32)
        qk = qk + alibi_slopes(H)[None, :, None, None] * dist[None, None, :, :]
        allowed = window_allowed(S)
        qk = jnp.where(allowed[None, None, :, :], -1000000000.0, qk)
        attn = jax.nn.softmax(qk, axis=-1)
        out = jnp.einsum('bhij,bhjd->bhid', attn, v)
        out = out.transpose(0, 2, 1, 3).reshape(B, S, D)
        return jnp.dot(out, Wo) + bo

    def _L0_xattn_ref(x, context, q_w, q_b, k_w, k_b, v_w, v_b, k_img_w, k_img_b, v_img_w, v_img_b, o_w, o_b, norm_q_w, norm_k_w, norm_k_img_w):
        import jax, jax.numpy as jnp
        import numpy as np
        DIM = 512
        NH = 16
        HD = DIM // NH
        EPS = 1e-06
        IMG_LEN = 257

        def rms_norm(x, w, eps=EPS):
            xf = x.astype(jnp.float32)
            y = xf * jax.lax.rsqrt(jnp.mean(xf * xf, axis=-1, keepdims=True) + eps)
            return y.astype(x.dtype) * w

        def linear(x, w, b):
            return jnp.einsum('blc,oc->blo', x, w) + b

        def attention(q, k, v):
            scale = 1.0 / jnp.sqrt(jnp.asarray(HD, q.dtype))
            scores = jnp.einsum('bqhd,bkhd->bhqk', q, k) * scale
            probs = jax.nn.softmax(scores, axis=-1)
            return jnp.einsum('bhqk,bkhd->bqhd', probs, v)
        B, L, _ = x.shape
        ctx_img = context[:, :IMG_LEN]
        ctx_txt = context[:, IMG_LEN:]
        q = rms_norm(linear(x, q_w, q_b), norm_q_w).reshape(B, L, NH, HD)
        k = rms_norm(linear(ctx_txt, k_w, k_b), norm_k_w).reshape(B, -1, NH, HD)
        v = linear(ctx_txt, v_w, v_b).reshape(B, -1, NH, HD)
        k_img = rms_norm(linear(ctx_img, k_img_w, k_img_b), norm_k_img_w).reshape(B, -1, NH, HD)
        v_img = linear(ctx_img, v_img_w, v_img_b).reshape(B, -1, NH, HD)
        img_x = attention(q, k_img, v_img)
        txt_x = attention(q, k, v)
        out = (txt_x + img_x).reshape(B, L, DIM)
        return linear(out, o_w, o_b)

    def _L0_ffn_ref(x, Wg, Wu, Wd, Wr, temperature):
        import jax, jax.numpy as jnp
        import numpy as np
        GOLDEN_CENTER = 1.0 / np.e
        GOLDEN_LOWER = 0.5 - np.log(4.0 / 3.0)
        GOLDEN_UPPER = 0.5

        def _golden_weights(x, Wr, temperature):
            inh = jax.nn.sigmoid(x @ Wr / temperature)
            in_zone = (inh >= GOLDEN_LOWER) & (inh <= GOLDEN_UPPER)
            distance = jnp.abs(inh - GOLDEN_CENTER)
            weights = jnp.exp(-distance / 0.1) * in_zone.astype(x.dtype)
            wsum = jnp.sum(weights, axis=-1, keepdims=True)
            no_expert = wsum < 1e-08
            fb = jnp.exp(-distance / 0.3)
            _, top2 = jax.lax.top_k(fb, 2)
            fb_mask = jnp.sum(jax.nn.one_hot(top2, weights.shape[-1], dtype=x.dtype), axis=-2)
            fb_w = fb * fb_mask
            fb_w = fb_w / jnp.maximum(jnp.sum(fb_w, axis=-1, keepdims=True), 1e-08)
            weights = jnp.where(no_expert, fb_w, weights)
            weights = weights / jnp.maximum(jnp.sum(weights, axis=-1, keepdims=True), 1e-08)
            return weights
        weights = _golden_weights(x, Wr, temperature)
        gate = jnp.einsum('btd,edf->betf', x, Wg)
        up = jnp.einsum('btd,edf->betf', x, Wu)
        h = jax.nn.silu(gate) * up
        e_out = jnp.einsum('betf,efd->betd', h, Wd)
        out = jnp.einsum('bte,betd->btd', weights, e_out)
        return out
    x = x + _L0_attn_ref(_layernorm(x, axis=-1), L0_attn_Wq, L0_attn_Wkv, L0_attn_Wo, L0_attn_bo)
    x = x + _L0_xattn_ref(_layernorm(x, axis=-1), ctx_2048, L0_xattn_q_w, L0_xattn_q_b, L0_xattn_k_w, L0_xattn_k_b, L0_xattn_v_w, L0_xattn_v_b, L0_xattn_k_img_w, L0_xattn_k_img_b, L0_xattn_v_img_w, L0_xattn_v_img_b, L0_xattn_o_w, L0_xattn_o_b, L0_xattn_norm_q_w, L0_xattn_norm_k_w, L0_xattn_norm_k_img_w)
    x = x + _L0_ffn_ref(_layernorm(x, axis=-1), L0_ffn_Wg, L0_ffn_Wu, L0_ffn_Wd, L0_ffn_Wr, L0_ffn_temperature)
    return x

_drawn_inputs = setup_inputs


def setup_inputs(seed=0):
    import zlib

    import numpy as np

    out = dict(_drawn_inputs(seed))
    spreads = {'L0_attn_bo': (0.0, 0.1),
     'L0_xattn_q_b': (0.0, 0.1),
     'L0_xattn_k_b': (0.0, 0.417),
     'L0_xattn_v_b': (0.0, 0.1),
     'L0_xattn_k_img_b': (0.0, 0.566),
     'L0_xattn_v_img_b': (0.0, 0.1),
     'L0_xattn_o_b': (0.0, 0.1),
     'L0_xattn_norm_q_w': (1.0, 0.2),
     'L0_xattn_norm_k_w': (1.0, 0.546),
     'L0_xattn_norm_k_img_w': (1.0, 0.593)}
    factors = {}
    for name, (base, spread) in spreads.items():
        noise = np.random.default_rng([zlib.crc32(name.encode()), seed]).standard_normal(out[name].shape)
        drawn = base * np.exp(spread * noise) if base else spread * noise
        out[name] = jnp.asarray(drawn.astype(out[name].dtype))
    for name, factor in factors.items():
        out[name] = (out[name] * factor).astype(out[name].dtype)
    return out
```

```python
from contextlib import ExitStack

import numpy as np

import concourse.bass as bass
from concourse import mybir

F32 = mybir.dt.float32
F32R = mybir.dt.float32r
ALU = mybir.AluOpType
ACT = mybir.ActivationFunctionType
AX = mybir.AxisListType

P = 128
B, S, D = 8, 112, 512
C = D // P
NH, HD = 16, 32
G = 4
R = NH // G
IMG, CTX = 257, 375
TXT = CTX - IMG
IMGP = IMG + 1
KEYS = IMGP + TXT
TILE = [P, P, KEYS - 2 * P]
CKEYS = 3 * P
TB = 4
TXTN = TB * TXT
HALF = B // 2 * S
E, F = 8, 512
FC = F // P
NT = B * S // P
NTOK = B * S
PART = [(0, 4 * P), (4 * P, 3 * P)]
WINDOW_SIDE, GLOBAL = 64, 64
LN_EPS, RMS_EPS = 1e-5, 1e-6
WRP = 72
ZONE_MID = float(1.0 / np.e)
ZONE_LO = float(np.float32(0.5 - np.log(4.0 / 3.0)))
ZONE_HI = 0.5
QB, KB, KIB, VB, VIB, NQ, NK, NKI, TEMP = (C * i for i in range(9))
NCOLS = TEMP + 1

assert S - 1 - GLOBAL <= WINDOW_SIDE


def due(value):
    return not isinstance(value, int) or value > 0


class Count:

    def __init__(self):
        self.base, self.n = 0, 0

    def next(self):
        self.n += 1
        return self.base + self.n

    def enter(self, i, first, per):
        self.start, self.per = self.base + self.n, per
        self.base, self.n = self.start + (i - first) * per, 0

    def leave(self, rounds):
        assert self.n == self.per, (self.n, self.per)
        self.base, self.n = self.start + rounds * self.per, 0


def decoder(nc, x, ctxT, ctx_txt, ctx_last, wkv, wo_attn, bo8, wkT, wkiT, wvT, wviT, wqT, woT, ob, cols,
            wg, wu, wd, wr, out):
    with ExitStack() as ctx:
        base = 16640
        end = 229368

        def at(name, offset, shape, dt=F32):
            size = int(np.prod(shape[1:])) * 4
            assert base + offset + size <= end and offset % 32 == 0, (name, offset, size)
            return nc.alloc_sbuf_tensor_at(name, list(shape), dt, offset=base + offset)

        def pair(name, offset, shape):
            size = int(np.prod(shape[1:])) * 4
            return at(name + "_hi", offset, shape, F32R), at(name + "_lo", offset + size, shape, F32R)

        def sem(name):
            return ctx.enter_context(nc.semaphore(name))

        ident = at("ident", 0, [P, P])
        ones = at("ones", 512, [P, P])
        col = at("col", 1024, [P, NCOLS])
        wr_raw = at("wr_raw", 1184, [P, C, E])
        qscale = at("qscale", 1312, [P, C])
        vbsum = at("vbsum", 1328 + 16, [P, C])
        stats = at("stats", 1536, [S, B, 6])
        mv = at("mv", 1728, [S, B, 2])
        lnx, lnr0, lna, rstd = (at(n, 1792 + 32 * i, [S, B]) for i, n in enumerate(("lnx", "lnr0", "lna", "rstd")))
        rm = at("rm", 1920, [S, B])
        meanT = at("meanT", 1952, [P, C, B])
        vT = at("vT", 2080, [P, B])
        vrep = at("vrep", 2112, [P, G, B])
        mcorr = at("mcorr", 2240, [P, B])
        vlast = at("vlast", 2496, [B, D])
        tril = at("tril", 5120, [P, E, E])
        zT = at("zT", 1536, [E, NTOK])
        KT0, VV0, QF0 = 5376, 5376 + 48128, 5376 + 48128 + 49152
        KT = at("KT", KT0, [P, C, B, KEYS])
        VV = at("VV", VV0, [P, B, 3, D])
        wk_hi, wk_lo = pair("wk", VV0, [P, C, D])
        txt_raw = [at(f"txt_raw{t}", VV0 + 16384 + 7552 * t, [P, C, TXTN]) for t in range(2)]
        txt_hi, txt_lo = pair("txt", VV0 + 31488, [P, C, TXTN])
        A0 = QF0
        wki_hi, wki_lo = pair("wki", A0, [P, C, D])
        wv_hi, wv_lo = pair("wv", A0 + 16384, [P, C, D])
        wvi_hi, wvi_lo = pair("wvi", A0 + 32768, [P, C, D])
        woA = at("woA", A0 + 32768, [P, G, D])
        wvA = at("wvA", A0 + 40960, [P, C, P])
        rep = at("rep", A0 + 43008, [P, G, R, HD])
        o8 = at("o8", A0 + 45056, [B, D])
        CT0 = A0 + 49152
        ctx_hi, ctx_lo = zip(*(pair(f"ctx{i}", CT0 + 12288 * i, [P, C, CKEYS]) for i in range(2)))
        w_slot = [at(f"w_slot{i}", CT0 + 8192 * i, [P, C, D]) for i in range(2)]
        ctx_raw = [at(f"ctx_raw{i}", CT0 + 24576 + 6144 * i, [P, C, CKEYS]) for i in range(2)]
        wk_raw = at("wk_raw", CT0 + 24576, [P, C, D])
        KS0 = CT0 + 36864
        ksq, ksum, kx, kr0, ka = (at(n, KS0 + 1504 * i, [P, KEYS]) for i, n in enumerate(("ksq", "ksum", "kx", "kr0", "ka")))
        sel = at("sel", CT0 + 16384, [B, B, S])
        QF = at("QF", QF0, [P, C, NTOK])
        X1 = QF0 + 14336
        xt1_hi, xt1_lo = pair("xt1", X1, [P, C, NTOK])
        wq_hi, wq_lo = pair("wq", X1 + 28672, [P, C, D])
        qsq, qsum, qx, qr0, qa = (at(n, X1 + 45056 + 1792 * i, [P, HALF]) for i, n in enumerate(("qsq", "qsum", "qx", "qr0", "qa")))
        xn1 = [at(f"xn1_{i}", X1 + 54016 + 2048 * i, [S, D]) for i in range(2)]
        wq_raw = at("wq_raw", X1 + 58112, [P, C, D])
        ob_sb = at("ob_sb", X1 + 66304, [S, D])
        prob = [at(f"prob{i}", X1 + 6016 * i, [S, R, KEYS]) for i in range(4)]
        a1 = X1 + 24064
        pt_hi, pt_lo = zip(*(pair(f"pt{i}", a1 + 3584 * i, [P, R * S]) for i in range(2)))
        ks_hi, ks_lo = zip(*(pair(f"ks{i}", a1 + 7168 + 3008 * i, [P, KEYS]) for i in range(2)))
        vs_hi, vs_lo = zip(*(pair(f"vs{i}", a1 + 13184 + 3072 * i, [P, 3, P]) for i in range(2)))
        qs_hi, qs_lo = zip(*(pair(f"qs{i}", a1 + 19328 + 896 * i, [P, S]) for i in range(2)))
        nmax, psums, prec = (at(n, a1 + 21120 + 128 * i, [S, G, R, 2]) for i, n in enumerate(("nmax", "psums", "prec")))
        wo_hi, wo_lo = pair("wo", a1 + 21504, [P, C, D])
        wo_raw = at("wo_raw", a1 + 37888, [P, C, D])
        ot_hi, ot_lo = zip(*(pair(f"ot{i}", X1 + 3584 * i, [P, C, S]) for i in range(2)))
        xn2 = [at(f"xn2_{i}", a1 + 46080 + 2048 * i, [S, D]) for i in range(2)]
        X0 = end - base - 16384
        X = at("X", X0 // 32 * 32, [S, B, D])
        w0 = KT0
        xt_hi, xt_lo = pair("xt", w0 + 49152, [P, C, NTOK])
        acc = at("acc", w0 + 77824, [P, NT, D])
        h_hi, h_lo = pair("h", w0 + 92160, [P, FC, NTOK])
        e_raw = [at(f"e_raw{i}", w0 + 120832 + 8192 * i, [P, C, D]) for i in range(3)]
        eg, eu, ed = ([pair(f"{n}{i}", w0 + (0, 145408)[i] + 16384 * k, [P, C, D]) for i in range(2)]
                      for k, n in enumerate(("eg", "eu", "ed")))
        M0 = w0 + 194560
        silu = [at(f"silu{i}", M0 + 2048 * i, [P, 4 * P]) for i in range(2)]
        hf = [at(f"hf{i}", M0 + 4096 + 2048 * i, [P, 4 * P]) for i in range(2)]
        r0 = M0 + 8192
        wr_hi, wr_lo = pair("wr", r0, [P, C, WRP])
        rank2 = at("rank2", r0, [P, NT, E, E])
        (z, inh, dist, zone, fb, rnk, wtok) = (at(n, r0 + 2304 + 224 * i, [P, NT, E])
                                               for i, n in enumerate(("z", "inh", "dist", "zone", "fb", "rnk", "wtok")))
        s1, s2 = (at(n, r0 + 3872 + 32 * i, [P, NT]) for i, n in enumerate(("s1", "s2")))
        ps = ctx.enter_context(nc.psum_tensor("ps", [P, 8, 512], F32))

        (d_wk, d_x, d_small, d_attn, d_wq, d_ob, d_wo, d_acc, d_wr, d_out, d_vl) = (
            sem(n) for n in ("d_wk", "d_x", "d_small", "d_attn", "d_wq", "d_ob", "d_wo", "d_acc", "d_wr", "d_out", "d_vl"))
        d_txt = [sem(f"d_txt{t}") for t in range(2)]
        d_w = [sem(f"d_w{i}") for i in range(2)]
        d_ctx = [sem(f"d_ctx{i}") for i in range(2)]
        d_e = [sem(f"d_e{k}") for k in range(3)]
        const_ones = sem("const_ones")
        const_ident = sem("const_ident")
        const_sel = sem("const_sel")
        dve_own = sem("dve_own")
        pool_own = sem("pool_own")
        act_own = sem("act_own")
        wk_hi_done = sem("wk_hi_done")
        wk_lo_done = sem("wk_lo_done")
        txt_hi_done = sem("txt_hi_done")
        txt_lo_done = sem("txt_lo_done")
        ktxt_mm = sem("ktxt_mm")
        k_evac = sem("k_evac")
        ln0_x = sem("ln0_x")
        ln0_r = sem("ln0_r")
        ln0_done = sem("ln0_done")
        a1_mm = sem("a1_mm")
        a1_done = sem("a1_done")
        a2_mm = sem("a2_mm")
        a2_done = sem("a2_done")
        a3_mm = sem("a3_mm")
        a3_done = sem("a3_done")
        a4_mm = sem("a4_mm")
        a4_done = sem("a4_done")
        a5_mm = sem("a5_mm")
        x1_done = sem("x1_done")
        ln1_x = sem("ln1_x")
        ln1_r = sem("ln1_r")
        w_hi_done = sem("w_hi_done")
        w_lo_done = sem("w_lo_done")
        ctx_hi_done = sem("ctx_hi_done")
        ctx_lo_done = sem("ctx_lo_done")
        v_mm = sem("v_mm")
        v_evac = sem("v_evac")
        k_sum = sem("k_sum")
        ss_mm = sem("ss_mm")
        kx_done = sem("kx_done")
        kr_done = sem("kr_done")
        k_fin = sem("k_fin")
        vl_mm = sem("vl_mm")
        vl_done = sem("vl_done")
        wq_hi_done = sem("wq_hi_done")
        wq_lo_done = sem("wq_lo_done")
        xn1_done = sem("xn1_done")
        x1t_mm = sem("x1t_mm")
        xt1_hi_done = sem("xt1_hi_done")
        xt1_lo_done = sem("xt1_lo_done")
        q_mm = sem("q_mm")
        q_evac = sem("q_evac")
        q_sum = sem("q_sum")
        qss_mm = sem("qss_mm")
        qx_done = sem("qx_done")
        qr_done = sem("qr_done")
        q_fin = sem("q_fin")
        sk_hi = sem("sk_hi")
        sk_klo = sem("sk_klo")
        sk_qlo = sem("sk_qlo")
        s_mm = sem("s_mm")
        max_done = sem("max_done")
        exp_done = sem("exp_done")
        rec_done = sem("rec_done")
        norm_done = sem("norm_done")
        t_mm = sem("t_mm")
        pt_hi_done = sem("pt_hi_done")
        pt_lo_done = sem("pt_lo_done")
        vs_hi_done = sem("vs_hi_done")
        vs_lo_done = sem("vs_lo_done")
        pv_mm = sem("pv_mm")
        diag_done = sem("diag_done")
        wo_hi_done = sem("wo_hi_done")
        wo_lo_done = sem("wo_lo_done")
        ot_hi_done = sem("ot_hi_done")
        ot_lo_done = sem("ot_lo_done")
        o_mm = sem("o_mm")
        x2_done = sem("x2_done")
        ln2_x = sem("ln2_x")
        ln2_r = sem("ln2_r")
        xn2_done = sem("xn2_done")
        x2t_mm = sem("x2t_mm")
        xt_hi_done = sem("xt_hi_done")
        xt_lo_done = sem("xt_lo_done")
        wr_hi_done = sem("wr_hi_done")
        wr_lo_done = sem("wr_lo_done")
        z_mm = sem("z_mm")
        zt_done = sem("zt_done")
        zz_mm = sem("zz_mm")
        z_done = sem("z_done")
        r_act = sem("r_act")
        r_dve = sem("r_dve")
        e_hi_done = sem("e_hi_done")
        e_lo_done = sem("e_lo_done")
        gate_mm = sem("gate_mm")
        up_mm = sem("up_mm")
        silu_done = sem("silu_done")
        hf_done = sem("hf_done")
        h_hi_done = sem("h_hi_done")
        h_lo_done = sem("h_lo_done")
        down_mm = sem("down_mm")
        acc_done = sem("acc_done")

        ds = bass.ds

        def row(t, b):
            return t[:, ds(b, 1), :].rearrange("p a n -> p (a n)")

        def mm3(pe, o, wh, wl, xh, xl, first, last):
            pe.matmul(o, wh, xh, start=first, stop=False)
            pe.matmul(o, wh, xl, start=False, stop=False)
            return pe.matmul(o, wl, xh, start=False, stop=last)

        def f(t):
            return t.bitcast(F32)

        def pairs(eng, i_first, i_last, body):
            with eng.Fori(i_first, i_last) as i:
                for par in range(2):
                    body(2 * i + par, i, par)

        n_acc = 1 + sum(1 for i in range(1, NTOK) if i % S == 0 or i % P == 0)
        block = ctx.enter_context(nc.Block())

        @block.sync
        def _(sp):
            sp.dma_start(wk_raw[:], wkT).then_inc(d_wk, 16)
            sp.dma_start(txt_raw[0][:], ctx_txt[0]).then_inc(d_txt[0], 16)
            sp.dma_start(X[:], x.rearrange("b q d -> q b d")).then_inc(d_x, 16)
            sp.dma_start(col[:], cols).then_inc(d_small, 16)
            sp.dma_start(wr_raw[:], wr.rearrange("(c p) e -> p c e", p=P)).then_inc(d_wr, 16)
            sp.dma_start(txt_raw[1][:], ctx_txt[1]).then_inc(d_txt[1], 16)
            sp.dma_start(wvA[:], wkv.rearrange("(c p) n -> p c n", p=P)[:, :, P:2 * P]).then_inc(d_attn, 16)
            sp.dma_start(woA[:], wo_attn.rearrange("(g p) n -> p g n", p=P)).then_inc(d_attn, 16)
            sp.dma_start(o8[:], bo8).then_inc(d_attn, 16)
            sp.dma_start(w_slot[0][:], wkiT).then_inc(d_w[0], 16)
            sp.dma_start(w_slot[1][:], wvT).then_inc(d_w[1], 16)
            sp.wait_ge(w_lo_done, 1)
            sp.dma_start(w_slot[0][:], wviT).then_inc(d_w[0], 16)
            sp.wait_ge(wk_lo_done, 1)

            def load_ctx(b, i, par):
                if due(b - 1):
                    sp.wait_ge(ctx_lo_done, b - 1)
                sp.dma_start(ctx_raw[par][:], ctxT[ds(b, 1)].rearrange("a p c n -> (a p) c n")).then_inc(d_ctx[par], 16)

            load_ctx(0, 0, 0)
            load_ctx(1, 0, 1)
            pairs(sp, 1, B // 2, load_ctx)
            if due(B - 1):
                sp.wait_ge(ctx_lo_done, B - 1)
            sp.dma_start(ctx_raw[0][:, :, 0:P], ctx_last).then_inc(d_ctx[0], 16)
            sp.wait_ge(vl_mm, 1)
            sp.dma_start(wq_raw[:], wqT).then_inc(d_wq, 16)
            sp.dma_start(ob_sb[:], ob).then_inc(d_ob, 16)
            sp.wait_ge(vl_done, 1)
            sp.wait_ge(v_evac, 3 * B)
            for b in range(B):
                sp.dma_start(VV[0:1, b, 2, :], vlast[b:b + 1, :]).then_inc(d_vl, 16)
            sp.wait_ge(q_fin, 8)
            sp.dma_start(wo_raw[:], woT).then_inc(d_wo, 16)
            sp.wait_ge(pv_mm, 3 * B * G)

            def load_e(e, i, par):
                for k, w in enumerate((wg, wu, wd)):
                    if due(3 * e + k - 2):
                        sp.wait_ge(e_lo_done, 3 * e + k - 2)
                    sp.dma_start(e_raw[k][:], w[ds(e, 1)].rearrange("a (c p) n -> p (a c) n", p=P)).then_inc(d_e[k], 16)

            load_e(0, 0, 0)
            load_e(1, 0, 1)
            sp.wait_ge(x2_done, B)
            flat = 0
            while flat < NTOK:
                b, s = divmod(flat, S)
                t, p = divmod(flat, P)
                n = min(S - s, P - p)
                sp.dma_start(acc[p:p + n, t, :], X[s:s + n, b, :]).then_inc(d_acc, 16)
                flat += n
            pairs(sp, 1, E // 2, load_e)
            for j in range(NT):
                if due(NT * (E - 1) + j + 1):
                    sp.wait_ge(acc_done, NT * (E - 1) + j + 1)
                sp.dma_start(out[j * P:(j + 1) * P, :], acc[:, j, :]).then_inc(d_out, 16)
            sp.wait_ge(d_out, 16 * NT)

        @block.tensor
        def _(pe):
            def ktxt(u):
                t, c = divmod(u, C)
                pe.wait_ge(wk_lo_done, 1)
                pe.wait_ge(txt_lo_done, t + 1)
                if due(u - 3):
                    pe.wait_ge(k_evac, u - 3)
                for k in range(C):
                    mm = mm3(pe, ps[:, c, 0:TXTN], wk_hi[:, k, c * P:(c + 1) * P], wk_lo[:, k, c * P:(c + 1) * P],
                             txt_hi[:, k, :], txt_lo[:, k, :], k == 0, k == C - 1)
                mm.then_inc(ktxt_mm, 1)

            for u in range(4):
                ktxt(u)
            pe.wait_ge(ln0_done, 1)
            pe.wait_ge(const_ones, 1)
            for b in range(B):
                for c in range(C):
                    pe.matmul(ps[:, 4, c * B + b:c * B + b + 1], X[:, b, c * P:(c + 1) * P], rstd[:, b:b + 1],
                              start=True, stop=True)
            pe.matmul(ps[:, 4, 64:64 + B], ones[0:S, :], rm[:, :], start=True, stop=True).then_inc(a1_mm, 1)
            ktxt(4)
            pe.wait_ge(a1_done, 1)
            pe.wait_ge(d_attn, 48)
            for c in range(C):
                mm = pe.matmul(ps[:, 5, 0:B], wvA[:, c, :], meanT[:, c, :], start=(c == 0), stop=(c == C - 1))
            mm.then_inc(a2_mm, 1)
            ktxt(5)
            pe.wait_ge(a2_done, 2)
            for g in range(G):
                mm = pe.matmul(ps[:, 6, g * B:(g + 1) * B], rep[:, g, :, :].rearrange("p r d -> p (r d)"), vT[:, :],
                               start=True, stop=True)
            mm.then_inc(a3_mm, 1)
            ktxt(6)
            pe.wait_ge(a3_done, 1)
            for g in range(G):
                mm = pe.matmul(ps[0:B, 7, :], vrep[:, g, :], woA[:, g, :], start=(g == 0), stop=(g == G - 1))
            mm.then_inc(a4_mm, 1)
            ktxt(7)
            pe.wait_ge(a4_done, 1)
            pe.wait_ge(const_sel, 1)
            for b in range(B):
                if due(b - 3):
                    pe.wait_ge(x1_done, b - 3)
                pe.matmul(ps[0:S, 4 + b % 4, :], sel[:, b, :], o8[:, :], start=True, stop=True).then_inc(a5_mm, 1)

            def sumsq(b):
                pe.wait_ge(k_sum, b + 1)
                if due(b):
                    pe.wait_ge(kx_done, b)
                pe.matmul(ps[:, 7, 0:KEYS], ones[:, :], ksum[:, :], start=True, stop=True).then_inc(ss_mm, 1)

            def values(b, par, t, last=False):
                if due(3 * b + t - 2):
                    pe.wait_ge(v_evac, 3 * b + t - 2)
                wh, wl = (wv_hi, wv_lo) if t == 2 else (wvi_hi, wvi_lo)
                for k in range(C):
                    mm = mm3(pe, ps[:, 4 + t, :], ctx_hi[par][:, k, t * P:(t + 1) * P],
                             ctx_lo[par][:, k, t * P:(t + 1) * P], wh[:, k, :], wl[:, k, :], k == 0, k == C - 1)
                mm.then_inc(vl_mm if last else v_mm, 1)

            def project(b, i, par, first=False):
                pe.wait_ge(ctx_lo_done, b + 1)
                for c in range(C):
                    pe.wait_ge(k_evac, 5 + 4 * b + c)
                    for k in range(C):
                        mm = mm3(pe, ps[:, c, 0:IMGP], wki_hi[:, k, c * P:(c + 1) * P], wki_lo[:, k, c * P:(c + 1) * P],
                                 ctx_hi[par][:, k, 0:IMGP], ctx_lo[par][:, k, 0:IMGP], k == 0, k == C - 1)
                    mm.then_inc(ktxt_mm, 1)
                    if c == 0 and not first:
                        sumsq(b - 1)
                for t in range(3):
                    values(b, par, t)

            pe.wait_ge(w_lo_done, 3)
            pe.wait_ge(x1_done, B)
            project(0, 0, 0, True)
            project(1, 0, 1)
            pairs(pe, 1, B // 2, project)
            pe.wait_ge(ctx_lo_done, B + 1)
            values(B, 0, 0, True)
            sumsq(B - 1)

            def transpose_x(b, src, bank, done, free, out_sem):
                pe.wait_ge(done, b + 1)
                if due(b - 1):
                    pe.wait_ge(free, b - 1)
                for c in range(C):
                    mm = pe.transpose(ps[:, bank, c * S:(c + 1) * S], src[b % 2][:, c * P:(c + 1) * P], ident[0:S, 0:S])
                mm.then_inc(out_sem, 1)

            pe.wait_ge(const_ident, 2)
            pe.wait_ge(k_evac, 8 + 4 * B)
            for b in range(B):
                transpose_x(b, xn1, b % 2, xn1_done, xt1_lo_done, x1t_mm)

            def qsumsq(h):
                pe.wait_ge(q_sum, h + 1)
                pe.matmul(ps[:, 6 + h, 0:HALF], ones[:, :], qsum[:, :], start=True, stop=True).then_inc(qss_mm, 1)

            pe.wait_ge(wq_lo_done, 1)
            pe.wait_ge(v_evac, 3 * B)
            pe.wait_ge(vl_done, 1)
            pe.wait_ge(kx_done, B)
            for u in range(2 * C):
                h, c = divmod(u, C)
                pe.wait_ge(xt1_lo_done, B // 2 * (h + 1))
                if due(u - 3):
                    pe.wait_ge(q_evac, u - 3)
                for k in range(C):
                    mm = mm3(pe, ps[:, 2 + c, 0:HALF], wq_hi[:, k, c * P:(c + 1) * P], wq_lo[:, k, c * P:(c + 1) * P],
                             xt1_hi[:, k, h * HALF:(h + 1) * HALF], xt1_lo[:, k, h * HALF:(h + 1) * HALF],
                             k == 0, k == C - 1)
                mm.then_inc(q_mm, 1)
                if u == C:
                    qsumsq(0)
            qsumsq(1)

            def scores(n, g, a):
                pe.wait_ge(sk_hi, 2 * n + 2)
                pe.wait_ge(sk_klo, n + 1)
                pe.wait_ge(sk_qlo, n + 1)
                if due(8 * (n - 1) + 4 * a + 4):
                    pe.wait_ge(exp_done, 8 * (n - 1) + 4 * a + 4)
                s = g % 2
                for i, (x_, k_) in enumerate(((qs_hi, ks_hi), (qs_hi, ks_lo), (qs_lo, ks_hi))):
                    for r in (2 * a, 2 * a + 1):
                        rows = slice(HD * r, HD * r + HD)
                        mm = pe.matmul(ps[0:S, r, 0:KEYS], x_[s][rows, :], k_[s][rows, :], start=(i == 0), stop=(i == 2))
                mm.then_inc(s_mm, 1)

            def turn(n, g, t):
                m = 3 * n + t
                pe.wait_ge(norm_done, 4 * n + 4)
                if due(m - 1):
                    pe.wait_ge(pt_lo_done, m - 1)
                k = TILE[t]
                for r in range(R):
                    mm = pe.transpose(ps[0:k, 4 + (g + t) % 2, r * S:(r + 1) * S], prob[g][:, r, t * P:t * P + k],
                                      ident[0:S, 0:S])
                mm.then_inc(t_mm, 1)

            def pv(n, g, t):
                m = 3 * n + t
                pe.wait_ge(vs_lo_done, n + 1)
                pe.wait_ge(pt_lo_done, m + 1)
                if due(4 * (n - 1)):
                    pe.wait_ge(diag_done, 4 * (n - 1))
                k, v, p, o = TILE[t], g % 2, (g + t) % 2, ps[:, 6 + g % 2, 0:R * S]
                mm = mm3(pe, o, vs_hi[v][0:k, t, :], vs_lo[v][0:k, t, :], pt_hi[p][0:k, :], pt_lo[p][0:k, :],
                         t == 0, t == 2)
                mm.then_inc(pv_mm, 1)

            def attend(b, ahead=2):
                for g in range(G):
                    n, more = 4 * b + g, g + 2 < G or ahead
                    n2, g2 = n + 2, (g + 2) % G
                    turn(n, g, 0)
                    turn(n, g, 1)
                    if more:
                        scores(n2, g2, 0)
                    pv(n, g, 0)
                    turn(n, g, 2)
                    pv(n, g, 1)
                    if more:
                        scores(n2, g2, 1)
                    pv(n, g, 2)

            pe.wait_ge(q_evac, 8)
            pe.wait_ge(xt1_lo_done, B)
            for n in range(2):
                for a in range(2):
                    scores(n, n, a)
            pe.wait_ge(qx_done, 2)
            attend(0)
            with pe.Fori(1, B - 1) as b:
                attend(b)
            attend(B - 1, 0)

            pe.wait_ge(wo_lo_done, 1)
            for b in range(B):
                pe.wait_ge(ot_lo_done, b + 1)
                if due(b - 1):
                    pe.wait_ge(x2_done, b - 1)
                if b < 2:
                    pe.wait_ge(exp_done, 8 * B * G)
                for k in range(C):
                    mm = mm3(pe, ps[0:S, b % 2, :], ot_hi[b % 2][:, k, :], ot_lo[b % 2][:, k, :],
                             wo_hi[:, k, :], wo_lo[:, k, :], k == 0, k == C - 1)
                mm.then_inc(o_mm, 1)
                if b >= 1:
                    transpose_x(b - 1, xn2, 2 + (b - 1) % 2, xn2_done, xt_lo_done, x2t_mm)
            transpose_x(B - 1, xn2, 2 + (B - 1) % 2, xn2_done, xt_lo_done, x2t_mm)

            def gate_up(e, par, part, c):
                n = 8 * e + 4 * part + c
                t0, nt = PART[part]
                if due(n - 1):
                    pe.wait_ge(hf_done, n - 1)
                for w, bank, done in ((eg, c % 2, gate_mm), (eu, 2 + c % 2, up_mm)):
                    for k in range(C):
                        mm = mm3(pe, ps[:, bank, 0:nt], w[par][0][:, k, c * P:(c + 1) * P], w[par][1][:, k, c * P:(c + 1) * P],
                                 xt_hi[:, k, t0:t0 + nt], xt_lo[:, k, t0:t0 + nt], k == 0, k == C - 1)
                    mm.then_inc(done, 1)

            def down(e, par, part):
                pe.wait_ge(h_lo_done, 8 * e + 4 * part + 4)
                for j in range(4 * part, (4, NT)[part]):
                    d = NT * e + j
                    if due(d - 1):
                        pe.wait_ge(acc_done, d - 1)
                    for k in range(FC):
                        mm = mm3(pe, ps[:, 4 + (par + j) % 2, :], h_hi[:, k, j * P:(j + 1) * P], h_lo[:, k, j * P:(j + 1) * P],
                                 ed[par][0][:, k, :], ed[par][1][:, k, :], k == 0, k == FC - 1)
                    mm.then_inc(down_mm, 1)

            def expert(e, i, par, last=False):
                for c in range(1, FC):
                    gate_up(e, par, 0, c)
                gate_up(e, par, 1, 0)
                pe.wait_ge(e_lo_done, 3 * e + 3)
                down(e, par, 0)
                for c in range(1, FC):
                    gate_up(e, par, 1, c)
                if not last:
                    pe.wait_ge(e_lo_done, 3 * e + 5)
                    gate_up(e + 1, 1 - par, 0, 0)
                down(e, par, 1)

            pe.wait_ge(xt_lo_done, B)
            pe.wait_ge(e_lo_done, 2)
            gate_up(0, 0, 0, 0)
            pe.wait_ge(wr_lo_done, 1)
            pe.wait_ge(diag_done, 4 * B * G)
            for h in range(2):
                for k in range(C):
                    mm = mm3(pe, ps[0:WRP, 6 + h, 0:HALF], wr_hi[:, k, :], wr_lo[:, k, :],
                             xt_hi[:, k, h * HALF:(h + 1) * HALF], xt_lo[:, k, h * HALF:(h + 1) * HALF], k == 0, k == C - 1)
                mm.then_inc(z_mm, 1)
            gate_up(0, 0, 0, 1)
            pe.wait_ge(zt_done, 2)
            for j in range(NT):
                mm = pe.transpose(ps[:, 6, j * E:(j + 1) * E], zT[:, j * P:(j + 1) * P], ident[0:E, 0:E])
            mm.then_inc(zz_mm, 1)
            for c in range(2, FC):
                gate_up(0, 0, 0, c)
            gate_up(0, 0, 1, 0)
            pe.wait_ge(e_lo_done, 3)
            down(0, 0, 0)
            for c in range(1, FC):
                gate_up(0, 0, 1, c)
            pe.wait_ge(e_lo_done, 5)
            gate_up(1, 1, 0, 0)
            down(0, 0, 1)
            expert(1, 0, 1)
            pairs(pe, 1, E // 2 - 1, expert)
            expert(E - 2, 0, 0)
            expert(E - 1, 0, 1, True)

        @block.scalar
        def _(act):
            own = Count()
            act.preload_act_table_set("natural_log_exp_and_others")

            def hi(o, i):
                return act.activation(o, i, ACT.Copy)

            def root(r, t):
                act.activation(r, t, ACT.Ln).then_inc(act_own, 1)
                act.wait_ge(act_own, own.next())
                return act.activation(r, r, ACT.Exp, scale=-0.5)

            act.wait_ge(d_wk, 16)
            hi(wk_hi[:], wk_raw[:]).then_inc(wk_hi_done, 1)
            act.wait_ge(d_txt[0], 16)
            hi(txt_hi[:], txt_raw[0][:]).then_inc(txt_hi_done, 1)

            def ktxt_out(u):
                t, c = divmod(u, C)
                act.wait_ge(ktxt_mm, u + 1)
                act.activation(KT[:, c, t * TB:(t + 1) * TB, IMGP:KEYS],
                               ps[:, c, 0:TXTN].rearrange("p (b n) -> p b n", b=TB), ACT.Identity,
                               bias=col[:, KB + c:KB + c + 1]).then_inc(k_evac, 1)

            act.wait_ge(d_small, 16)
            for u in range(3):
                ktxt_out(u)
            act.wait_ge(ktxt_mm, 4)
            act.wait_ge(d_txt[1], 16)
            act.wait_ge(txt_lo_done, 1)
            hi(txt_hi[:], txt_raw[1][:]).then_inc(txt_hi_done, 1)
            ktxt_out(3)
            act.wait_ge(ln0_x, 1)
            root(lnr0[:], lnx[:]).then_inc(ln0_r, 1)
            act.wait_ge(d_w[0], 16)
            hi(wki_hi[:], w_slot[0][:]).then_inc(w_hi_done, 1)
            ktxt_out(4)
            act.wait_ge(d_w[1], 16)
            hi(wv_hi[:], w_slot[1][:]).then_inc(w_hi_done, 1)
            for u in range(5, 8):
                ktxt_out(u)
            act.wait_ge(a5_mm, B)
            act.wait_ge(d_w[0], 32)
            hi(wvi_hi[:], w_slot[0][:]).then_inc(w_hi_done, 1)

            def split_ctx(b, par, count, n=CKEYS):
                if due(count):
                    act.wait_ge(d_ctx[par], count)
                if due(3 * (b - 1)):
                    act.wait_ge(v_mm, 3 * (b - 1))
                hi(ctx_hi[par][:, :, 0:n], ctx_raw[par][:, :, 0:n]).then_inc(ctx_hi_done, 1)

            act.wait_ge(w_lo_done, 3)
            split_ctx(0, 0, 16)
            act.wait_ge(ln1_x, 1)
            root(lnr0[:], lnx[:]).then_inc(ln1_r, 1)

            def read_project(b, i, par, first=False, last=False):
                if last:
                    split_ctx(B, 0, 16 * (B // 2 + 1), P)
                else:
                    split_ctx(b + 1, 1 - par, 16 * (i + 1 + par))
                for c in range(C):
                    act.wait_ge(ktxt_mm, 2 * C + C * b + c + 1)
                    act.activation(KT[:, c, ds(b, 1), 0:IMGP].rearrange("p a n -> p (a n)"), ps[:, c, 0:IMGP],
                                   ACT.Identity, bias=col[:, KIB + c:KIB + c + 1]).then_inc(k_evac, 1)
                if not first:
                    if due(b):
                        act.wait_ge(kx_done, b)
                    act.activation(kr0[:], kx[:], ACT.Ln).then_inc(act_own, 1)
                    act.wait_ge(act_own, own.next())
                    act.activation(kr0[:], kr0[:], ACT.Exp, scale=-0.5).then_inc(kr_done, 1)
                for t in range(3):
                    act.wait_ge(v_mm, 3 * b + t + 1)
                    act.activation(VV[:, ds(b, 1), t, :].rearrange("p a n -> p (a n)"), ps[:, 4 + t, :],
                                   ACT.Copy).then_inc(v_evac, 1)

            read_project(0, 0, 0, True)
            read_project(1, 0, 1)
            with act.Fori(1, B // 2 - 1) as i:
                own.enter(i, 1, 2)
                for par in range(2):
                    read_project(2 * i + par, i, par)
            own.leave(B // 2 - 2)
            read_project(B - 2, B // 2 - 1, 0)
            read_project(B - 1, B // 2 - 1, 1, last=True)
            act.wait_ge(vl_mm, 1)
            act.activation(vlast[:], ps[0:B, 4, :], ACT.Copy).then_inc(vl_done, 1)
            act.wait_ge(kx_done, B)
            root(kr0[:], kx[:]).then_inc(kr_done, 1)

            act.wait_ge(d_wq, 16)
            hi(wq_hi[:], wq_raw[:]).then_inc(wq_hi_done, 1)
            for b in range(B):
                act.wait_ge(x1t_mm, b + 1)
                hi(xt1_hi[:, :, b * S:(b + 1) * S], ps[:, b % 2, 0:C * S].rearrange("p (c n) -> p c n", c=C)).then_inc(xt1_hi_done, 1)
            for u in range(2 * C):
                h, c = divmod(u, C)
                act.wait_ge(q_mm, u + 1)
                act.activation(QF[:, c, h * HALF:(h + 1) * HALF], ps[:, 2 + c, 0:HALF], ACT.Identity,
                               bias=col[:, QB + c:QB + c + 1]).then_inc(q_evac, 1)
                if u == C + 1:
                    act.wait_ge(qx_done, 1)
                    root(qr0[:], qx[:]).then_inc(qr_done, 1)
            act.wait_ge(qx_done, 2)
            root(qr0[:], qx[:]).then_inc(qr_done, 1)

            def stage_kq(b, g):
                n = 4 * b + g
                if due(2 * n - 2):
                    act.wait_ge(s_mm, 2 * n - 2)
                act.activation(ks_hi[g % 2][:, :], KT[:, g, ds(b, 1), :].rearrange("p a n -> p (a n)"),
                               ACT.Copy).then_inc(sk_hi, 1)
                act.activation(qs_hi[g % 2][:, :], QF[:, g, ds(b * S, S)], ACT.Copy).then_inc(sk_hi, 1)

            def stage_v(b, g):
                n = 4 * b + g
                if due(3 * n - 3):
                    act.wait_ge(pv_mm, 3 * n - 3)
                act.activation(vs_hi[g % 2][:, :, :],
                               VV[:, ds(b, 1), :, g * P:(g + 1) * P].rearrange("p a t n -> p (a t) n"),
                               ACT.Copy).then_inc(vs_hi_done, 1)

            def exps(n, g, a):
                act.wait_ge(max_done, 4 * n + 2 * a + 2)
                if due(3 * n - 9):
                    act.wait_ge(t_mm, 3 * n - 9)
                for r in (2 * a, 2 * a + 1):
                    for kind, (k0, k1) in enumerate(((0, IMG), (IMGP, KEYS))):
                        act.activation(prob[g][:, r, k0:k1], ps[0:S, r, k0:k1], ACT.Exp, bias=nmax[:, g, r, kind:kind + 1],
                                       accum_out=psums[:, g, r, kind:kind + 1]).then_inc(exp_done, 1)

            def pt_hi_part(n, g, t):
                m, k = 3 * n + t, TILE[t]
                act.wait_ge(t_mm, m + 1)
                if due(m - 1):
                    act.wait_ge(pv_mm, m - 1)
                hi(pt_hi[(g + t) % 2][0:k, :], ps[0:k, 4 + (g + t) % 2, 0:R * S]).then_inc(pt_hi_done, 1)

            def attend(b, left=3):
                for g in range(G):
                    n = 4 * b + g
                    pt_hi_part(n, g, 0)
                    pt_hi_part(n, g, 1)
                    if g + 3 < G or left:
                        stage_kq(b + (g + 3) // G, (g + 3) % G)
                    if g + 1 < G or left:
                        stage_v(b + (g + 1) // G, (g + 1) % G)
                    pt_hi_part(n, g, 2)
                    if g + 2 < G or left:
                        for a in range(2):
                            exps(n + 2, (g + 2) % G, a)

            act.wait_ge(k_fin, 8 * B)
            act.wait_ge(q_fin, 8)
            stage_kq(0, 0)
            stage_kq(0, 1)
            act.wait_ge(d_vl, 16 * B)
            stage_v(0, 0)
            act.wait_ge(qx_done, 2)
            for n in range(2):
                for a in range(2):
                    exps(n, n, a)
            stage_kq(0, 2)
            act.wait_ge(d_wo, 16)
            hi(wo_hi[:], wo_raw[:]).then_inc(wo_hi_done, 1)
            attend(0)
            with act.Fori(1, B - 1) as b:
                attend(b)
            attend(B - 1, 0)

            def split_e(e, par, k, count):
                if due(count):
                    act.wait_ge(d_e[k], count)
                w = (eg, eu, ed)[k]
                act.activation(w[par][0][:], e_raw[k][:], ACT.Copy).then_inc(e_hi_done, 1)

            act.wait_ge(pv_mm, 3 * B * G)
            for b in range(B + 2):
                if b < B:
                    act.wait_ge(diag_done, 4 * B * G)
                    if due(b - 1):
                        act.wait_ge(o_mm, b - 1)
                    hi(ot_hi[b % 2][:, :, :], QF[:, :, b * S:(b + 1) * S]).then_inc(ot_hi_done, 1)
                if 1 <= b <= B:
                    act.wait_ge(ln2_x, b)
                    root(lnr0[:, b - 1:b], lnx[:, b - 1:b]).then_inc(ln2_r, 1)
                if b >= 2:
                    if due(b - 1):
                        act.wait_ge(x2t_mm, b - 1)
                    hi(xt_hi[:, :, (b - 2) * S:(b - 1) * S], ps[:, 2 + b % 2, 0:C * S].rearrange("p (c n) -> p c n", c=C)).then_inc(xt_hi_done, 1)
                if b in (2, 4, 6):
                    split_e(0, 0, b // 2 - 1, 16)

            act.wait_ge(d_wr, 16)
            act.wait_ge(wr_hi_done, 1)
            act.wait_ge(xt_lo_done, B)
            act.wait_ge(d_acc, 16 * n_acc)
            hi(wr_hi[:, :, 0:E], wr_raw[:, :, :]).then_inc(wr_hi_done, 1)
            for h in range(2):
                act.wait_ge(z_mm, h + 1)
                act.activation(zT[:, h * HALF:(h + 1) * HALF], ps[0:E, 6 + h, 0:HALF], ACT.Copy).then_inc(zt_done, 1)
            act.wait_ge(r_dve, 1)
            act.activation(inh[:], z[:], ACT.Exp, scale=-1.0).then_inc(r_act, 1)
            act.wait_ge(r_dve, 2)
            act.activation(zone[:], dist[:], ACT.Exp, scale=-1.0 / 0.1).then_inc(r_act, 1)
            act.activation(fb[:], dist[:], ACT.Exp, scale=-1.0 / 0.3).then_inc(r_act, 1)

            def unit(n, nt):
                act.wait_ge(gate_mm, n + 1)
                if due(n - 1):
                    act.wait_ge(hf_done, n - 1)
                return nt

            def gate_up(e, part, c, first=False):
                n = 8 * e + 4 * part + c
                t0, nt = PART[part]
                unit(n, nt)
                act.activation(silu[c % 2][:, 0:nt], ps[:, c % 2, 0:nt], ACT.Silu).then_inc(silu_done, 1)
                act.wait_ge(hf_done, n + 1)
                if due(NT * e - 3 if part == 0 else NT * e):
                    act.wait_ge(down_mm, NT * e - 3 if part == 0 else NT * e)
                hi(h_hi[:, c, t0:t0 + nt], hf[c % 2][:, 0:nt]).then_inc(h_hi_done, 1)

            def expert(e, i, par, last=False):
                for c in range(1, FC):
                    gate_up(e, 0, c)
                    if not last:
                        if due(NT * e):
                            act.wait_ge(down_mm, NT * e)
                        split_e(e + 1, 1 - par, c - 1, 16 * (e + 2))
                for c in range(FC):
                    gate_up(e, 1, c)
                if not last:
                    gate_up(e + 1, 0, 0)

            act.wait_ge(d_acc, 16 * n_acc)
            act.wait_ge(xt_lo_done, B)
            gate_up(0, 0, 0)
            expert(0, 0, 0)
            expert(1, 0, 1)
            pairs(act, 1, E // 2 - 1, expert)
            expert(E - 2, 0, 0)
            expert(E - 1, 0, 1, True)

        @block.vector
        def _(dve):
            own = Count()

            def lo(o, i, hi_):
                return dve.tensor_tensor(o, i, f(hi_), ALU.subtract)

            def refine(r, r0_, a, x_):
                dve.tensor_tensor(a, r0_, r0_, ALU.mult).then_inc(dve_own, 1)
                dve.wait_ge(dve_own, own.next())
                dve.scalar_tensor_tensor(a, a, -0.5, x_, ALU.mult, ALU.mult).then_inc(dve_own, 1)
                dve.wait_ge(dve_own, own.next())
                return dve.scalar_tensor_tensor(r, a, 1.5, r0_, ALU.add, ALU.mult)

            def ln_sums(bs):
                for b in bs:
                    ins = dve.bn_stats(stats[:, b, :], X[:, b, :])
                ins.then_inc(dve_own, 1)
                dve.wait_ge(dve_own, own.next())
                for b in bs:
                    ins = dve.bn_aggr(mv[:, b, :], stats[:, b, :])
                ins.then_inc(dve_own, 1)
                dve.wait_ge(dve_own, own.next())

            dve.memset(ones[:], 1.0).then_inc(const_ones, 1)
            dve.wait_ge(wk_hi_done, 1)
            lo(wk_lo[:], wk_raw[:], wk_hi[:]).then_inc(wk_lo_done, 1)
            dve.wait_ge(txt_hi_done, 1)
            lo(txt_lo[:], txt_raw[0][:], txt_hi[:]).then_inc(txt_lo_done, 1)

            dve.wait_ge(d_x, 16)
            ln_sums(range(B))
            dve.tensor_scalar(lnx[:], mv[:, :, 1], LN_EPS, None, ALU.add).then_inc(ln0_x, 1)
            dve.wait_ge(ln0_r, 1)
            refine(rstd[:], lnr0[:], lna[:], lnx[:]).then_inc(dve_own, 1)
            dve.wait_ge(dve_own, own.next())
            dve.tensor_tensor(rm[:], rstd[:], mv[:, :, 0], ALU.mult).then_inc(ln0_done, 1)
            dve.wait_ge(ktxt_mm, 4)
            dve.wait_ge(txt_hi_done, 2)
            lo(txt_lo[:], txt_raw[1][:], txt_hi[:]).then_inc(txt_lo_done, 1)
            dve.wait_ge(d_small, 16)
            dve.tensor_scalar(qscale[:], col[:, NQ:NQ + C], float(HD) ** -0.5, None, ALU.mult).then_inc(dve_own, 1)
            dve.wait_ge(dve_own, own.next())
            dve.tensor_tensor(vbsum[:], col[:, VB:VB + C], col[:, VIB:VIB + C], ALU.add).then_inc(dve_own, 1)
            dve.wait_ge(dve_own, own.next())
            dve.wait_ge(const_ident, 2)
            dve.tensor_copy(rep[:], ident[:].rearrange("p (g d) -> p g d", g=G).unsqueeze(2).to_broadcast([P, G, R, HD]))\
               .then_inc(a2_done, 1)
            dve.wait_ge(a1_mm, 1)
            dve.tensor_scalar(mcorr[:], ps[:, 4, 64:64 + B], 1.0 / S, None, ALU.mult).then_inc(dve_own, 1)
            dve.wait_ge(dve_own, own.next())
            dve.scalar_tensor_tensor(meanT[:], ps[:, 4, 0:C * B].rearrange("p (c b) -> p c b", c=C), 1.0 / S,
                                     mcorr[:].unsqueeze(1).to_broadcast([P, C, B]), ALU.mult, ALU.subtract)\
               .then_inc(a1_done, 1)
            dve.wait_ge(w_hi_done, 1)
            lo(wki_lo[:], w_slot[0][:], wki_hi[:]).then_inc(w_lo_done, 1)
            dve.wait_ge(a2_mm, 1)
            dve.tensor_copy(vT[:], ps[:, 5, 0:B]).then_inc(a2_done, 1)
            dve.wait_ge(a3_mm, 1)
            dve.tensor_copy(vrep[:].rearrange("p g b -> p (g b)"), ps[:, 6, 0:G * B]).then_inc(a3_done, 1)
            dve.wait_ge(w_hi_done, 2)
            lo(wv_lo[:], w_slot[1][:], wv_hi[:]).then_inc(w_lo_done, 1)
            dve.wait_ge(a4_mm, 1)
            dve.tensor_tensor(o8[:], ps[0:B, 7, :], o8[:], ALU.add).then_inc(a4_done, 1)
            for b in range(B):
                dve.wait_ge(a5_mm, b + 1)
                dve.tensor_tensor(X[:, b, :], ps[0:S, 4 + b % 4, :], X[:, b, :], ALU.add).then_inc(x1_done, 1)
            dve.wait_ge(w_hi_done, 3)
            lo(wvi_lo[:], w_slot[0][:], wvi_hi[:]).then_inc(w_lo_done, 1)
            dve.wait_ge(ctx_hi_done, 1)
            lo(ctx_lo[0][:], ctx_raw[0][:], ctx_hi[0][:]).then_inc(ctx_lo_done, 1)
            dve.wait_ge(x1_done, B)
            ln_sums(range(B))
            dve.tensor_scalar(lnx[:], mv[:, :, 1], LN_EPS, None, ALU.add).then_inc(ln1_x, 1)
            dve.wait_ge(ln1_r, 1)
            refine(rstd[:], lnr0[:], lna[:], lnx[:]).then_inc(dve_own, 1)
            dve.wait_ge(dve_own, own.next())

            def key_norm(b):
                dve.wait_ge(ss_mm, b + 1)
                if due(b):
                    dve.wait_ge(kr_done, b)
                dve.tensor_scalar(kx[:], ps[:, 7, 0:KEYS], 1.0 / D, RMS_EPS, ALU.mult, ALU.add).then_inc(kx_done, 1)
                dve.wait_ge(kr_done, b + 1)
                refine(ka[:], kr0[:], ka[:], kx[:]).then_inc(dve_own, 1)
                dve.wait_ge(dve_own, own.next())
                for c in range(C):
                    for k0, k1, w in ((0, IMGP, NKI), (IMGP, KEYS, NK)):
                        kt = KT[:, c, ds(b, 1), k0:k1].rearrange("p a n -> p (a n)")
                        dve.scalar_tensor_tensor(kt, kt, col[:, w + c:w + c + 1], ka[:, k0:k1], ALU.mult, ALU.mult)\
                           .then_inc(k_fin, 1)

            def project(b, i, par, first=False, last=False):
                n = P if last else CKEYS
                dve.wait_ge(ctx_hi_done, b + 2)
                lo(ctx_lo[1 - par][:, :, 0:n], ctx_raw[1 - par][:, :, 0:n], ctx_hi[1 - par][:, :, 0:n]).then_inc(ctx_lo_done, 1)
                if not first:
                    if due(8 * (b - 1)):
                        dve.wait_ge(k_fin, 8 * (b - 1))
                    key_norm(b - 1)

            project(0, 0, 0, True)
            project(1, 0, 1)
            with dve.Fori(1, B // 2 - 1) as i:
                own.enter(i, 1, 6)
                for par in range(2):
                    project(2 * i + par, i, par)
            own.leave(B // 2 - 2)
            project(B - 2, B // 2 - 1, 0)
            project(B - 1, B // 2 - 1, 1, last=True)
            if due(8 * (B - 1)):
                dve.wait_ge(k_fin, 8 * (B - 1))
            key_norm(B - 1)

            dve.wait_ge(vl_mm, 1)
            dve.wait_ge(wq_hi_done, 1)
            lo(wq_lo[:], wq_raw[:], wq_hi[:]).then_inc(wq_lo_done, 1)
            for b in range(B + 1):
                if b < B:
                    if due(b - 1):
                        dve.wait_ge(x1t_mm, b - 1)
                    dve.tensor_scalar(xn1[b % 2][:], X[:, b, :], mv[:, b, 0:1], rstd[:, b:b + 1], ALU.subtract, ALU.mult)\
                       .then_inc(xn1_done, 1)
                if b >= 1:
                    c = b - 1
                    dve.wait_ge(xt1_hi_done, c + 1)
                    lo(xt1_lo[:, :, c * S:(c + 1) * S], ps[:, c % 2, 0:C * S].rearrange("p (c n) -> p c n", c=C), xt1_hi[:, :, c * S:(c + 1) * S]).then_inc(xt1_lo_done, 1)
            for h in range(2):
                dve.wait_ge(qss_mm, h + 1)
                if due(4 * h):
                    dve.wait_ge(q_fin, 4 * h)
                dve.tensor_scalar(qx[:], ps[:, 6 + h, 0:HALF], 1.0 / D, RMS_EPS, ALU.mult, ALU.add).then_inc(qx_done, 1)
                dve.wait_ge(qr_done, h + 1)
                refine(qa[:], qr0[:], qa[:], qx[:]).then_inc(dve_own, 1)
                dve.wait_ge(dve_own, own.next())
                for c in range(C):
                    qf = QF[:, c, h * HALF:(h + 1) * HALF]
                    dve.scalar_tensor_tensor(qf, qf, qscale[:, c:c + 1], qa[:], ALU.mult, ALU.mult).then_inc(q_fin, 1)

            def q_lo(b, g):
                n = 4 * b + g
                dve.wait_ge(sk_hi, 2 * n + 2)
                lo(qs_lo[g % 2][:, :], QF[:, g, ds(b * S, S)], qs_hi[g % 2][:, :]).then_inc(sk_qlo, 1)

            def v_lo(b, g):
                n = 4 * b + g
                dve.wait_ge(vs_hi_done, n + 1)
                lo(vs_lo[g % 2][:, :, :], VV[:, ds(b, 1), :, g * P:(g + 1) * P].rearrange("p a t n -> p (a t) n"), vs_hi[g % 2][:, :, :]).then_inc(vs_lo_done, 1)

            def maxima(n, g, a):
                dve.wait_ge(s_mm, 2 * n + a + 1)
                for kind, (k0, k1) in enumerate(((0, IMG), (IMGP, KEYS))):
                    dve.tensor_reduce(nmax[:, g, 2 * a:2 * a + 2, kind], ps[0:S, 2 * a:2 * a + 2, k0:k1], AX.X, ALU.max,
                                      negate=True).then_inc(max_done, 1)

            def reciprocals(n, g, a):
                dve.wait_ge(exp_done, 8 * n + 4 * a + 4)
                dve.reciprocal(prec[:, g, 2 * a:2 * a + 2, :], psums[:, g, 2 * a:2 * a + 2, :]).then_inc(rec_done, 1)

            def pt_lo_part(n, g, t):
                m, k, s = 3 * n + t, TILE[t], (g + t) % 2
                dve.wait_ge(pt_hi_done, m + 1)
                lo(pt_lo[s][0:k, :], ps[0:k, 4 + s, 0:R * S], pt_hi[s][0:k, :]).then_inc(pt_lo_done, 1)

            def diagonal(b, g):
                n = 4 * b + g
                dve.wait_ge(pv_mm, 3 * n + 3)
                for r in range(R):
                    rows = slice(HD * r, HD * r + HD)
                    dve.tensor_scalar(QF[rows, g, ds(b * S, S)], ps[rows, 6 + g % 2, r * S:(r + 1) * S], vbsum[rows, g:g + 1],
                                      None, ALU.add).then_inc(diag_done, 1)

            def attend(b, left=3):
                for g in range(G):
                    n = 4 * b + g
                    pt_lo_part(n, g, 0)
                    pt_lo_part(n, g, 1)
                    if g + 1 < G or left:
                        reciprocals(n + 1, (g + 1) % G, 1)
                    if g + 2 < G or left:
                        maxima(n + 2, (g + 2) % G, 0)
                    pt_lo_part(n, g, 2)
                    if g + 1 < G or left:
                        v_lo(b + (g + 1) // G, (g + 1) % G)
                    if g + 3 < G or left:
                        q_lo(b + (g + 3) // G, (g + 3) % G)
                    if g + 2 < G or left:
                        maxima(n + 2, (g + 2) % G, 1)
                    diagonal(b, g)
                    if g + 2 < G or left:
                        reciprocals(n + 2, (g + 2) % G, 0)

            q_lo(0, 0)
            q_lo(0, 1)
            v_lo(0, 0)
            dve.wait_ge(q_fin, 8)
            for a in range(2):
                maxima(0, 0, a)
            for a in range(2):
                maxima(1, 1, a)
            reciprocals(0, 0, 0)
            reciprocals(0, 0, 1)
            reciprocals(1, 1, 0)
            q_lo(0, 2)
            dve.wait_ge(wo_hi_done, 1)
            lo(wo_lo[:], wo_raw[:], wo_hi[:]).then_inc(wo_lo_done, 1)
            attend(0)
            with dve.Fori(1, B - 1) as b:
                attend(b)
            attend(B - 1, 0)

            def split_e(e, par, k):
                w = (eg, eu, ed)[k]
                dve.wait_ge(e_hi_done, 3 * e + k + 1)
                lo(w[par][1][:], e_raw[k][:], w[par][0][:]).then_inc(e_lo_done, 1)

            dve.wait_ge(exp_done, 8 * B * G)
            for b in range(B + 2):
                if b < B:
                    dve.wait_ge(ot_hi_done, b + 1)
                    lo(ot_lo[b % 2][:, :, :], QF[:, :, b * S:(b + 1) * S], ot_hi[b % 2][:, :, :]).then_inc(ot_lo_done, 1)
                    dve.wait_ge(o_mm, b + 1)
                    dve.tensor_tensor(X[:, b, :], ps[0:S, b % 2, :], X[:, b, :], ALU.add).then_inc(x2_done, 1)
                    dve.wait_ge(x2_done, b + 1)
                    ln_sums([b])
                    dve.tensor_scalar(lnx[:, b:b + 1], mv[:, b, 1:2], LN_EPS, None, ALU.add).then_inc(ln2_x, 1)
                if 1 <= b <= B:
                    c = b - 1
                    dve.wait_ge(ln2_r, c + 1)
                    refine(rstd[:, c:c + 1], lnr0[:, c:c + 1], lna[:, c:c + 1], lnx[:, c:c + 1]).then_inc(dve_own, 1)
                    dve.wait_ge(dve_own, own.next())
                    if due(c - 1):
                        dve.wait_ge(x2t_mm, c - 1)
                    dve.tensor_scalar(xn2[c % 2][:], X[:, c, :], mv[:, c, 0:1], rstd[:, c:c + 1], ALU.subtract, ALU.mult)\
                       .then_inc(xn2_done, 1)
                if b >= 2:
                    c = b - 2
                    dve.wait_ge(xt_hi_done, c + 1)
                    lo(xt_lo[:, :, c * S:(c + 1) * S], ps[:, 2 + c % 2, 0:C * S].rearrange("p (c n) -> p c n", c=C), xt_hi[:, :, c * S:(c + 1) * S]).then_inc(xt_lo_done, 1)
                if b in (2, 4, 6):
                    split_e(0, 0, b // 2 - 1)

            dve.wait_ge(d_acc, 16 * n_acc)
            dve.wait_ge(xn2_done, B)
            dve.memset(f(wr_hi[:]), 0.0).then_inc(dve_own, 1)
            dve.wait_ge(dve_own, own.next())
            dve.memset(f(wr_lo[:]), 0.0).then_inc(wr_hi_done, 1)
            dve.wait_ge(wr_hi_done, 2)
            dve.tensor_tensor(wr_lo[:, :, 0:E], wr_raw[:, :, :], f(wr_hi[:, :, 0:E]), ALU.subtract).then_inc(wr_lo_done, 1)
            itemp = s2[:, 0:1]
            dve.reciprocal(itemp, col[:, TEMP:TEMP + 1]).then_inc(dve_own, 1)
            dve.wait_ge(dve_own, own.next())
            dve.wait_ge(zz_mm, 1)
            dve.tensor_scalar(z[:].rearrange("p t e -> p (t e)"), ps[:, 6, 0:NT * E], itemp, None, ALU.mult).then_inc(r_dve, 1)
            dve.wait_ge(r_act, 1)
            dve.tensor_scalar(inh[:], inh[:], 1.0, None, ALU.add).then_inc(dve_own, 1)
            dve.wait_ge(dve_own, own.next())
            dve.reciprocal(inh[:], inh[:]).then_inc(dve_own, 1)
            dve.wait_ge(dve_own, own.next())
            dve.tensor_scalar(dist[:], inh[:], -ZONE_MID, None, ALU.add).then_inc(dve_own, 1)
            dve.wait_ge(dve_own, own.next())
            dve.tensor_scalar(rnk[:], dist[:], -1.0, None, ALU.mult).then_inc(dve_own, 1)
            dve.wait_ge(dve_own, own.next())
            dve.tensor_tensor(dist[:], dist[:], rnk[:], ALU.max).then_inc(r_dve, 1)
            dve.wait_ge(r_dve, 2)
            dve.tensor_scalar(rnk[:], inh[:], ZONE_LO, None, ALU.is_ge).then_inc(dve_own, 1)
            dve.wait_ge(dve_own, own.next())
            dve.scalar_tensor_tensor(rnk[:], inh[:], ZONE_HI, rnk[:], ALU.is_le, ALU.mult).then_inc(dve_own, 1)
            dve.wait_ge(dve_own, own.next())
            dve.wait_ge(r_act, 3)
            dve.tensor_tensor(wtok[:], zone[:], rnk[:], ALU.mult).then_inc(dve_own, 1)
            dve.wait_ge(dve_own, own.next())
            dve.tensor_reduce(s1[:], wtok[:], AX.X, ALU.add).then_inc(dve_own, 1)
            dve.wait_ge(dve_own, own.next())
            dve.tensor_scalar(s1[:], s1[:], 1e-8, None, ALU.is_lt).then_inc(dve_own, 1)
            dve.wait_ge(dve_own, own.next())
            fb_e = fb[:].unsqueeze(3).to_broadcast([P, NT, E, E])
            fb_j = fb[:].unsqueeze(2).to_broadcast([P, NT, E, E])
            dve.tensor_tensor(rank2[:], fb_j, fb_e, ALU.is_gt).then_inc(dve_own, 1)
            dve.wait_ge(dve_own, own.next())
            dve.tensor_reduce(rnk[:], rank2[:], AX.X, ALU.add).then_inc(dve_own, 1)
            dve.wait_ge(dve_own, own.next())
            dve.tensor_tensor(rank2[:], fb_j, fb_e, ALU.is_equal).then_inc(dve_own, 1)
            dve.wait_ge(dve_own, own.next())
            dve.wait_ge(const_ident, 3)
            dve.tensor_tensor(rank2[:], rank2[:], tril[:].unsqueeze(1).to_broadcast([P, NT, E, E]), ALU.mult).then_inc(dve_own, 1)
            dve.wait_ge(dve_own, own.next())
            dve.tensor_reduce(inh[:], rank2[:], AX.X, ALU.add).then_inc(dve_own, 1)
            dve.wait_ge(dve_own, own.next())
            dve.tensor_tensor(rnk[:], rnk[:], inh[:], ALU.add).then_inc(dve_own, 1)
            dve.wait_ge(dve_own, own.next())
            dve.scalar_tensor_tensor(fb[:], rnk[:], 1.5, fb[:], ALU.is_lt, ALU.mult).then_inc(dve_own, 1)
            dve.wait_ge(dve_own, own.next())

            def over_sum(t):
                dve.tensor_reduce(s2[:], t[:], AX.X, ALU.add).then_inc(dve_own, 1)
                dve.wait_ge(dve_own, own.next())
                dve.tensor_scalar(s2[:], s2[:], 1e-8, None, ALU.max).then_inc(dve_own, 1)
                dve.wait_ge(dve_own, own.next())
                dve.reciprocal(s2[:], s2[:]).then_inc(dve_own, 1)
                dve.wait_ge(dve_own, own.next())
                dve.tensor_tensor(t[:], t[:], s2[:].unsqueeze(2).to_broadcast([P, NT, E]), ALU.mult).then_inc(dve_own, 1)
                dve.wait_ge(dve_own, own.next())

            over_sum(fb)
            dve.tensor_tensor(fb[:], fb[:], s1[:].unsqueeze(2).to_broadcast([P, NT, E]), ALU.mult).then_inc(dve_own, 1)
            dve.wait_ge(dve_own, own.next())
            dve.tensor_scalar(s1[:], s1[:], -1.0, 1.0, ALU.mult, ALU.add).then_inc(dve_own, 1)
            dve.wait_ge(dve_own, own.next())
            dve.tensor_tensor(wtok[:], wtok[:], s1[:].unsqueeze(2).to_broadcast([P, NT, E]), ALU.mult).then_inc(dve_own, 1)
            dve.wait_ge(dve_own, own.next())
            dve.tensor_tensor(wtok[:], wtok[:], fb[:], ALU.add).then_inc(dve_own, 1)
            dve.wait_ge(dve_own, own.next())
            over_sum(wtok)

            def gate_up(e, part, c):
                n = 8 * e + 4 * part + c
                t0, nt = PART[part]
                dve.wait_ge(silu_done, n + 1)
                dve.wait_ge(up_mm, n + 1)
                if due(n - 1):
                    dve.wait_ge(h_hi_done, n - 1)
                if due(n - 1):
                    dve.wait_ge(h_lo_done, n - 1)
                dve.tensor_tensor(hf[c % 2][:, 0:nt], silu[c % 2][:, 0:nt], ps[:, 2 + c % 2, 0:nt], ALU.mult)\
                   .then_inc(hf_done, 1)
                dve.wait_ge(h_hi_done, n + 1)
                lo(h_lo[:, c, t0:t0 + nt], hf[c % 2][:, 0:nt], h_hi[:, c, t0:t0 + nt]).then_inc(h_lo_done, 1)

            def add(e, par, part):
                for j in range(4 * part, (4, NT)[part]):
                    d = NT * e + j
                    dve.wait_ge(down_mm, d + 1)
                    if due(d - NT + 1):
                        dve.wait_ge(acc_done, d - NT + 1)
                    dve.scalar_tensor_tensor(acc[:, j, :], ps[:, 4 + (par + j) % 2, :],
                                             wtok[:, j, ds(e, 1)], acc[:, j, :], ALU.mult, ALU.add)\
                       .then_inc(acc_done, 1)

            def expert(e, i, par, last=False):
                for c in range(1, FC):
                    gate_up(e, 0, c)
                    if not last:
                        split_e(e + 1, 1 - par, c - 1)
                gate_up(e, 1, 0)
                add(e, par, 0)
                for c in range(1, FC):
                    gate_up(e, 1, c)
                if not last:
                    gate_up(e + 1, 0, 0)
                add(e, par, 1)

            gate_up(0, 0, 0)
            expert(0, 0, 0)
            expert(1, 0, 1)
            pairs(dve, 1, E // 2 - 1, expert)
            expert(E - 2, 0, 0)
            expert(E - 1, 0, 1, True)

        @block.gpsimd
        def _(pool):
            own = Count()
            pool.memset(ident[:], 0.0).then_inc(pool_own, 1)
            pool.wait_ge(pool_own, own.next())
            pool.affine_select(out=ident[:], in_=ident[:], compare_op=ALU.not_equal, fill=1.0, base=0,
                               pattern=[[-1, P]], channel_multiplier=1).then_inc(const_ident, 2)
            pool.memset(sel[:], 0.0).then_inc(pool_own, 1)
            pool.wait_ge(pool_own, own.next())
            pool.affine_select(out=sel[:], in_=sel[:], compare_op=ALU.not_equal, fill=1.0, base=0,
                               pattern=[[-1, B], [0, S]], channel_multiplier=1).then_inc(const_sel, 1)
            pool.memset(tril[:], 1.0).then_inc(pool_own, 1)
            pool.wait_ge(pool_own, own.next())
            pool.affine_select(out=tril[:], in_=tril[:], compare_op=ALU.is_gt, fill=0.0, base=0,
                               pattern=[[1, E], [-1, E]], channel_multiplier=0).then_inc(const_ident, 1)

            def square_sum(b, first=False):
                for c in range(C):
                    kt = KT[:, c, ds(b, 1), :].rearrange("p a n -> p (a n)")
                    pool.wait_ge(k_evac, 2 * C + C * b + c + 1)
                    if c == 0:
                        if due(b):
                            pool.wait_ge(ss_mm, b)
                        pool.tensor_tensor(ksum[:], kt, kt, ALU.mult).then_inc(pool_own, 1)
                        pool.wait_ge(pool_own, own.next())
                    else:
                        pool.tensor_tensor(ksq[:], kt, kt, ALU.mult).then_inc(pool_own, 1)
                        pool.wait_ge(pool_own, own.next())
                        ins = pool.tensor_tensor(ksum[:], ksum[:], ksq[:], ALU.add)
                        if c < C - 1:
                            ins.then_inc(pool_own, 1)
                            pool.wait_ge(pool_own, own.next())
                        else:
                            ins.then_inc(k_sum, 1)

            square_sum(0)
            with pool.Fori(1, B) as b:
                own.enter(b, 1, 2 * C - 2)
                square_sum(b)
            own.leave(B - 1)

            pool.wait_ge(d_ob, 16)
            for b in range(B):
                pool.wait_ge(xn1_done, b + 1)
                ins = pool.tensor_tensor(X[:, b, :], X[:, b, :], ob_sb[:], ALU.add)
            ins.then_inc(pool_own, 1)
            pool.wait_ge(pool_own, own.next())
            for h in range(2):
                for c in range(C):
                    qf = QF[:, c, h * HALF:(h + 1) * HALF]
                    pool.wait_ge(q_evac, C * h + c + 1)
                    if c == 0:
                        if due(h):
                            pool.wait_ge(qss_mm, h)
                        pool.tensor_tensor(qsum[:], qf, qf, ALU.mult).then_inc(pool_own, 1)
                        pool.wait_ge(pool_own, own.next())
                    else:
                        pool.tensor_tensor(qsq[:], qf, qf, ALU.mult).then_inc(pool_own, 1)
                        pool.wait_ge(pool_own, own.next())
                        ins = pool.tensor_tensor(qsum[:], qsum[:], qsq[:], ALU.add)
                        if c < C - 1:
                            ins.then_inc(pool_own, 1)
                            pool.wait_ge(pool_own, own.next())
                        else:
                            ins.then_inc(q_sum, 1)

            pool.wait_ge(q_fin, 8)
            for i in range(4):
                ins = pool.memset(prob[i][:, :, IMG:IMGP], 0.0)
            ins.then_inc(pool_own, 1)
            pool.wait_ge(pool_own, own.next())

            def k_lo(b, g):
                n = 4 * b + g
                pool.wait_ge(sk_hi, 2 * n + 1)
                pool.tensor_tensor(ks_lo[g % 2][:, :], KT[:, g, ds(b, 1), :].rearrange("p a n -> p (a n)"),
                                   f(ks_hi[g % 2][:, :]), ALU.subtract).then_inc(sk_klo, 1)

            def normalise(n, g, a):
                pool.wait_ge(rec_done, 2 * n + a + 1)
                for kind, (k0, k1) in enumerate(((0, IMG), (IMGP, KEYS))):
                    p = prob[g][:, 2 * a:2 * a + 2, k0:k1]
                    pool.tensor_tensor(p, p, prec[:, g, 2 * a:2 * a + 2, kind:kind + 1].to_broadcast([S, 2, k1 - k0]), ALU.mult)\
                        .then_inc(norm_done, 1)

            def attend(b, left=3):
                for g in range(G):
                    n = 4 * b + g
                    if g + 1 < G or left:
                        normalise(n + 1, (g + 1) % G, 1)
                    if g + 3 < G or left:
                        k_lo(b + (g + 3) // G, (g + 3) % G)
                    if g + 2 < G or left:
                        normalise(n + 2, (g + 2) % G, 0)

            k_lo(0, 0)
            k_lo(0, 1)
            normalise(0, 0, 0)
            normalise(0, 0, 1)
            normalise(1, 1, 0)
            k_lo(0, 2)
            attend(0)
            with pool.Fori(1, B - 1) as b:
                attend(b)
            attend(B - 1, 0)


NAMES = ("x", "ctxT", "ctx_txt", "ctx_last", "wkv", "wo_attn", "bo8", "wkT", "wkiT", "wvT", "wviT", "wqT", "woT", "ob",
         "cols", "wg", "wu", "wd", "wr")


def lay_out(i):
    c = np.asarray(i["ctx_2048"])
    t = c.transpose(0, 2, 1).reshape(B, C, P, CTX).transpose(0, 2, 1, 3)
    ctxT = np.zeros((B, P, C, CKEYS), c.dtype)
    ctxT[..., :IMG] = t[..., :IMG]
    ctxT[..., IMGP:KEYS] = t[..., IMG:]
    ctx_txt = t[..., IMG:].reshape(B // TB, TB, P, C, TXT).transpose(0, 2, 3, 1, 4).reshape(B // TB, P, C, TXTN)
    ctx_last = np.zeros((P, C, P), c.dtype)
    ctx_last[..., :B] = t[..., IMG - 1].transpose(1, 2, 0)

    def wT(w):
        return np.asarray(w).T.reshape(C, P, D).transpose(1, 0, 2)

    def vec(v):
        return np.asarray(v).reshape(C, P).T

    x = "L0_xattn_"
    temp = np.broadcast_to(np.asarray(i["L0_ffn_temperature"]).reshape(1, 1), (P, 1))
    cols = np.concatenate([vec(i[x + n]) for n in ("q_b", "k_b", "k_img_b", "v_b", "v_img_b", "norm_q_w", "norm_k_w",
                                                   "norm_k_img_w")] + [temp], axis=1)
    arrays = (i["x"], ctxT, ctx_txt, ctx_last, i["L0_attn_Wkv"], i["L0_attn_Wo"],
              np.broadcast_to(np.asarray(i["L0_attn_bo"]), (B, D)),
              wT(i[x + "k_w"]), wT(i[x + "k_img_w"]), wT(i[x + "v_w"]), wT(i[x + "v_img_w"]), wT(i[x + "q_w"]),
              wT(i[x + "o_w"]), np.broadcast_to(np.asarray(i[x + "o_b"]), (S, D)), cols,
              i["L0_ffn_Wg"], i["L0_ffn_Wu"], i["L0_ffn_Wd"], i["L0_ffn_Wr"])
    return {n: np.ascontiguousarray(a) for n, a in zip(NAMES, arrays)}


def kernel(**inputs):
    import concourse.bacc as bacc
    from concourse.bass_utils import run_bass_kernel_spmd

    nc = bacc.Bacc("TRN2", target_bir_lowering=False, num_devices=1)
    arrays = {f"in_{n}": a for n, a in lay_out(inputs).items()}
    args = [nc.dram_tensor(n, a.shape, mybir.dt.from_np(a.dtype), kind="ExternalInput").ap() for n, a in arrays.items()]
    out = nc.dram_tensor("out", (NTOK, D), F32, kind="ExternalOutput").ap()
    decoder(nc, *args, out)
    r = run_bass_kernel_spmd(nc, [arrays], core_ids=[0])
    return r.results[0]["out"].reshape(B, S, D)
```

```python
from contextlib import ExitStack

import numpy as np

import concourse.bass as bass
from concourse import mybir

F32 = mybir.dt.float32
F32R = mybir.dt.float32r
ALU = mybir.AluOpType
ACT = mybir.ActivationFunctionType
AX = mybir.AxisListType

P = 128
B, S, D = 8, 112, 512
C = D // P
NH, HD = 16, 32
G = 4
R = NH // G
IMG, CTX = 257, 375
TXT = CTX - IMG
IMGP = IMG + 1
KEYS = IMGP + TXT
TILE = [P, P, KEYS - 2 * P]
CKEYS = 3 * P
TB = 4
TXTN = TB * TXT
HALF = B // 2 * S
E, F = 8, 512
FC = F // P
NT = B * S // P
NTOK = B * S
PART = [(0, 4 * P), (4 * P, 3 * P)]
WINDOW_SIDE, GLOBAL = 64, 64
LN_EPS, RMS_EPS = 1e-5, 1e-6
WRP = 72
ZONE_MID = float(1.0 / np.e)
ZONE_LO = float(np.float32(0.5 - np.log(4.0 / 3.0)))
ZONE_HI = 0.5
QB, KB, KIB, VB, VIB, NQ, NK, NKI, TEMP = (C * i for i in range(9))
NCOLS = TEMP + 1

assert S - 1 - GLOBAL <= WINDOW_SIDE


def due(value):
    return not isinstance(value, int) or value > 0


class Count:

    def __init__(self):
        self.base, self.n = 0, 0

    def next(self):
        self.n += 1
        return self.base + self.n

    def enter(self, i, first, per):
        self.start, self.per = self.base + self.n, per
        self.base, self.n = self.start + (i - first) * per, 0

    def leave(self, rounds):
        assert self.n == self.per, (self.n, self.per)
        self.base, self.n = self.start + rounds * self.per, 0


def decoder(nc, x, ctxT, ctx_txt, ctx_last, wkv, wo_attn, bo8, wkT, wkiT, wvT, wviT, wqT, woT, ob, cols,
            wg, wu, wd, wr, out):
    with ExitStack() as ctx:
        base = 16640
        end = 229368

        def at(name, offset, shape, dt=F32):
            size = int(np.prod(shape[1:])) * 4
            assert base + offset + size <= end and offset % 32 == 0, (name, offset, size)
            return nc.alloc_sbuf_tensor_at(name, list(shape), dt, offset=base + offset)

        def pair(name, offset, shape):
            size = int(np.prod(shape[1:])) * 4
            return at(name + "_hi", offset, shape, F32R), at(name + "_lo", offset + size, shape, F32R)

        def sem(name):
            return ctx.enter_context(nc.semaphore(name))

        ident = at("ident", 0, [P, P])
        ones = at("ones", 512, [P, P])
        col = at("col", 1024, [P, NCOLS])
        wr_raw = at("wr_raw", 1184, [P, C, E])
        qscale = at("qscale", 1312, [P, C])
        vbsum = at("vbsum", 1328 + 16, [P, C])
        stats = at("stats", 1536, [S, B, 6])
        mv = at("mv", 1728, [S, B, 2])
        lnx, lnr0, lna, rstd = (at(n, 1792 + 32 * i, [S, B]) for i, n in enumerate(("lnx", "lnr0", "lna", "rstd")))
        rm = at("rm", 1920, [S, B])
        meanT = at("meanT", 1952, [P, C, B])
        vT = at("vT", 2080, [P, B])
        vrep = at("vrep", 2112, [P, G, B])
        mcorr = at("mcorr", 2240, [P, B])
        vlast = at("vlast", 2496, [B, D])
        tril = at("tril", 5120, [P, E, E])
        KT0, VV0, QF0 = 5376, 5376 + 48128, 5376 + 48128 + 49152
        KT = at("KT", KT0, [P, C, B, KEYS])
        VV = at("VV", VV0, [P, B, 3, D])
        wk_hi, wk_lo = pair("wk", VV0, [P, C, D])
        txt_raw = [at(f"txt_raw{t}", VV0 + 16384 + 7552 * t, [P, C, TXTN]) for t in range(2)]
        txt_hi, txt_lo = pair("txt", VV0 + 31488, [P, C, TXTN])
        A0 = QF0
        wki_hi, wki_lo = pair("wki", A0, [P, C, D])
        wv_hi, wv_lo = pair("wv", A0 + 16384, [P, C, D])
        wvi_hi, wvi_lo = pair("wvi", A0 + 32768, [P, C, D])
        woA = at("woA", A0 + 32768, [P, G, D])
        wvA = at("wvA", A0 + 40960, [P, C, P])
        rep = at("rep", A0 + 43008, [P, G, R, HD])
        o8 = at("o8", A0 + 45056, [B, D])
        CT0 = A0 + 49152
        ctx_hi, ctx_lo = zip(*(pair(f"ctx{i}", CT0 + 12288 * i, [P, C, CKEYS]) for i in range(2)))
        w_slot = [at(f"w_slot{i}", CT0 + 8192 * i, [P, C, D]) for i in range(2)]
        ctx_raw = [at(f"ctx_raw{i}", CT0 + 24576 + 6144 * i, [P, C, CKEYS]) for i in range(2)]
        wk_raw = at("wk_raw", CT0 + 24576, [P, C, D])
        KS0 = CT0 + 36864
        ksq, ksum, kx, kr0, ka = (at(n, KS0 + 1504 * i, [P, KEYS]) for i, n in enumerate(("ksq", "ksum", "kx", "kr0", "ka")))
        sel = at("sel", CT0 + 16384, [B, B, S])
        QF = at("QF", QF0, [P, C, NTOK])
        X1 = QF0 + 14336
        xt1_hi, xt1_lo = pair("xt1", X1, [P, C, NTOK])
        wq_hi, wq_lo = pair("wq", X1 + 28672, [P, C, D])
        qsq, qsum, qx, qr0, qa = (at(n, X1 + 45056 + 1792 * i, [P, HALF]) for i, n in enumerate(("qsq", "qsum", "qx", "qr0", "qa")))
        xn1 = [at(f"xn1_{i}", X1 + 54016 + 2048 * i, [S, D]) for i in range(2)]
        wq_raw = at("wq_raw", X1 + 58112, [P, C, D])
        ob_sb = at("ob_sb", X1 + 66304, [S, D])
        pt_hi, pt_lo = zip(*(pair(f"pt{i}", X1 + 3584 * i, [P, R * S]) for i in range(3)))
        qs_hi = [at(f"qs{i}_hi", X1 + 10752 + 1792 * i, [P, R, S], F32R) for i in range(2)]
        qs_lo = [at(f"qs{i}_lo", 2496 + 448 * i, [P, S], F32R) for i in range(2)]
        nmax, psums, prec = (at(n, 4544 + 128 * i, [S, G, R, 2]) for i, n in enumerate(("nmax", "psums", "prec")))
        nmr = at("nmr", 4928, [S, B])
        wo_raw = at("wo_raw", QF0 + 28672, [P, C, D])
        prob = [at(f"prob{i}", QF0 + 36864 + 6016 * i, [S, R, KEYS]) for i in range(4)]
        wo_hi, wo_lo = pair("wo", QF0 + 60928, [P, C, D])
        ks_hi, ks_lo = zip(*(pair(f"ks{i}", QF0 + 77312 + 3008 * i, [P, KEYS]) for i in range(2)))
        vs_hi, vs_lo = zip(*(pair(f"vs{i}", QF0 + 83328 + 3072 * i, [P, 3, P]) for i in range(2)))
        xn2 = [at(f"xn2_{i}", QF0 + 89472 + 2048 * i, [S, D]) for i in range(2)]
        X0 = (end - base - 16384) // 32 * 32
        X = at("X", X0, [S, B, D])
        ot_hi, ot_lo = zip(*(pair(f"ot{i}", VV0 + 16384 + 3584 * i, [P, C, S]) for i in range(4)))
        r0 = QF0 + 77312
        zT = at("zT", X1, [E, NTOK])
        wr_hi, wr_lo = pair("wr", r0, [P, C, WRP])
        rank2 = at("rank2", r0 + 2304, [P, NT, E, E])
        z, inh, dist, zone, fb, rnk = (at(n, r0 + 4096 + 224 * i, [P, NT, E])
                                       for i, n in enumerate(("z", "inh", "dist", "zone", "fb", "rnk")))
        s1, s2 = (at(n, r0 + 5440 + 32 * i, [P, NT]) for i, n in enumerate(("s1", "s2")))
        xt_hi, xt_lo = pair("xt", KT0, [P, C, NTOK])
        acc = at("acc", KT0 + 28672, [P, NT, D])
        silu = [at(f"silu{i}", KT0 + 43008 + 2048 * i, [P, 4 * P]) for i in range(2)]
        wtok = at("wtok", KT0 + 47104, [P, NT, E])
        h_hi, h_lo = pair("h", QF0, [P, FC, NTOK])
        e_raw = [at(f"e_raw{i}", QF0 + 28672 + 8192 * i, [P, C, D]) for i in range(3)]
        eu, ed, eg = ([pair(f"{n}{i}", (VV0, QF0 + 53248)[i] + 16384 * k, [P, C, D]) for i in range(2)]
                      for k, n in enumerate(("eu", "ed", "eg")))
        hf = [at(f"hf{i}", QF0 + 102400 + 2048 * i, [P, 4 * P]) for i in range(2)]
        ps = ctx.enter_context(nc.psum_tensor("ps", [P, 8, 512], F32))

        (d_wk, d_x, d_small, d_attn, d_wq, d_ob, d_wo, d_acc, d_wr, d_out, d_vl) = (
            sem(n) for n in ("d_wk", "d_x", "d_small", "d_attn", "d_wq", "d_ob", "d_wo", "d_acc", "d_wr", "d_out", "d_vl"))
        d_txt = [sem(f"d_txt{t}") for t in range(2)]
        d_w = [sem(f"d_w{i}") for i in range(2)]
        d_ctx = [sem(f"d_ctx{i}") for i in range(2)]
        d_e = [sem(f"d_e{k}") for k in range(3)]
        const_ones = sem("const_ones")
        const_ident = sem("const_ident")
        const_sel = sem("const_sel")
        dve_own = sem("dve_own")
        pool_own = sem("pool_own")
        act_own = sem("act_own")
        wk_hi_done = sem("wk_hi_done")
        wk_lo_done = sem("wk_lo_done")
        txt_hi_done = sem("txt_hi_done")
        txt_lo_done = sem("txt_lo_done")
        ktxt_mm = sem("ktxt_mm")
        k_evac = sem("k_evac")
        ln0_x = sem("ln0_x")
        ln0_r = sem("ln0_r")
        ln0_done = sem("ln0_done")
        a1_mm = sem("a1_mm")
        a1_done = sem("a1_done")
        a2_mm = sem("a2_mm")
        a2_done = sem("a2_done")
        a3_mm = sem("a3_mm")
        a3_done = sem("a3_done")
        a4_mm = sem("a4_mm")
        a4_done = sem("a4_done")
        a5_mm = sem("a5_mm")
        x1_done = sem("x1_done")
        ln1_x = sem("ln1_x")
        ln1_r = sem("ln1_r")
        w_hi_done = sem("w_hi_done")
        w_lo_done = sem("w_lo_done")
        ctx_hi_done = sem("ctx_hi_done")
        ctx_lo_done = sem("ctx_lo_done")
        v_mm = sem("v_mm")
        v_evac = sem("v_evac")
        k_sum = sem("k_sum")
        ss_mm = sem("ss_mm")
        kx_done = sem("kx_done")
        kr_done = sem("kr_done")
        k_fin = sem("k_fin")
        vl_mm = sem("vl_mm")
        vl_done = sem("vl_done")
        wq_hi_done = sem("wq_hi_done")
        wq_lo_done = sem("wq_lo_done")
        xn1_done = sem("xn1_done")
        x1t_mm = sem("x1t_mm")
        xt1_hi_done = sem("xt1_hi_done")
        xt1_lo_done = sem("xt1_lo_done")
        q_mm = sem("q_mm")
        q_evac = sem("q_evac")
        q_sum = sem("q_sum")
        qss_mm = sem("qss_mm")
        qx_done = sem("qx_done")
        qr_done = sem("qr_done")
        q_fin = sem("q_fin")
        qs_zero = sem("qs_zero")
        sk_qhi = sem("sk_qhi")
        sk_hi = sem("sk_hi")
        sk_klo = sem("sk_klo")
        sk_qlo = sem("sk_qlo")
        s_mm = sem("s_mm")
        max_done = sem("max_done")
        exp_done = sem("exp_done")
        rec_done = sem("rec_done")
        norm_done = sem("norm_done")
        t_mm = sem("t_mm")
        pt_hi_done = sem("pt_hi_done")
        pt_lo_done = sem("pt_lo_done")
        vs_hi_done = sem("vs_hi_done")
        vs_lo_done = sem("vs_lo_done")
        pv_mm = sem("pv_mm")
        diag_done = sem("diag_done")
        wo_hi_done = sem("wo_hi_done")
        wo_lo_done = sem("wo_lo_done")
        ot_hi_done = sem("ot_hi_done")
        ot_lo_done = sem("ot_lo_done")
        o_mm = sem("o_mm")
        x2_done = sem("x2_done")
        ln2_x = sem("ln2_x")
        ln2_r = sem("ln2_r")
        ln2_done = sem("ln2_done")
        xn2_done = sem("xn2_done")
        x2t_mm = sem("x2t_mm")
        xt_hi_done = sem("xt_hi_done")
        xt_lo_done = sem("xt_lo_done")
        wr_zero = sem("wr_zero")
        wr_hi_done = sem("wr_hi_done")
        wr_lo_done = sem("wr_lo_done")
        z_mm = sem("z_mm")
        zt_done = sem("zt_done")
        zz_mm = sem("zz_mm")
        z_done = sem("z_done")
        r_act = sem("r_act")
        r_dve = sem("r_dve")
        e_hi_done = sem("e_hi_done")
        e_lo_done = sem("e_lo_done")
        gate_mm = sem("gate_mm")
        up_mm = sem("up_mm")
        silu_done = sem("silu_done")
        hf_done = sem("hf_done")
        h_hi_done = sem("h_hi_done")
        h_lo_done = sem("h_lo_done")
        down_mm = sem("down_mm")
        acc_done = sem("acc_done")

        ds = bass.ds

        def row(t, b):
            return t[:, ds(b, 1), :].rearrange("p a n -> p (a n)")

        def mm3(pe, o, wh, wl, xh, xl, first, last):
            pe.matmul(o, wh, xh, start=first, stop=False)
            pe.matmul(o, wh, xl, start=False, stop=False)
            return pe.matmul(o, wl, xh, start=False, stop=last)

        def f(t):
            return t.bitcast(F32)

        def pairs(eng, i_first, i_last, body):
            with eng.Fori(i_first, i_last) as i:
                for par in range(2):
                    body(2 * i + par, i, par)

        n_acc = 1 + sum(1 for i in range(1, NTOK) if i % S == 0 or i % P == 0)
        block = ctx.enter_context(nc.Block())

        @block.sync
        def _(sp):
            sp.dma_start(wk_raw[:], wkT).then_inc(d_wk, 16)
            sp.dma_start(txt_raw[0][:], ctx_txt[0]).then_inc(d_txt[0], 16)
            sp.dma_start(X[:], x.rearrange("b q d -> q b d")).then_inc(d_x, 16)
            sp.dma_start(col[:], cols).then_inc(d_small, 16)
            sp.dma_start(wr_raw[:], wr.rearrange("(c p) e -> p c e", p=P)).then_inc(d_wr, 16)
            sp.dma_start(txt_raw[1][:], ctx_txt[1]).then_inc(d_txt[1], 16)
            sp.dma_start(wvA[:], wkv.rearrange("(c p) n -> p c n", p=P)[:, :, P:2 * P]).then_inc(d_attn, 16)
            sp.dma_start(woA[:], wo_attn.rearrange("(g p) n -> p g n", p=P)).then_inc(d_attn, 16)
            sp.dma_start(o8[:], bo8).then_inc(d_attn, 16)
            sp.dma_start(w_slot[0][:], wkiT).then_inc(d_w[0], 16)
            sp.dma_start(w_slot[1][:], wvT).then_inc(d_w[1], 16)
            sp.wait_ge(w_lo_done, 1)
            sp.dma_start(w_slot[0][:], wviT).then_inc(d_w[0], 16)
            sp.wait_ge(wk_lo_done, 1)

            def load_ctx(b, i, par):
                if due(b - 1):
                    sp.wait_ge(ctx_lo_done, b - 1)
                sp.dma_start(ctx_raw[par][:], ctxT[ds(b, 1)].rearrange("a p c n -> (a p) c n")).then_inc(d_ctx[par], 16)

            load_ctx(0, 0, 0)
            load_ctx(1, 0, 1)
            pairs(sp, 1, B // 2, load_ctx)
            if due(B - 1):
                sp.wait_ge(ctx_lo_done, B - 1)
            sp.dma_start(ctx_raw[0][:, :, 0:P], ctx_last).then_inc(d_ctx[0], 16)
            sp.wait_ge(vl_mm, 1)
            sp.dma_start(wq_raw[:], wqT).then_inc(d_wq, 16)
            sp.dma_start(ob_sb[:], ob).then_inc(d_ob, 16)
            sp.wait_ge(vl_done, 1)
            sp.wait_ge(v_evac, 3 * B)
            for b in range(B):
                sp.dma_start(VV[0:1, b, 2, :], vlast[b:b + 1, :]).then_inc(d_vl, 16)
            sp.wait_ge(q_fin, 8)
            sp.dma_start(wo_raw[:], woT).then_inc(d_wo, 16)
            sp.wait_ge(wo_lo_done, 1)

            def load_e(e, i, par):
                for k, w in enumerate((wg, wu, wd)):
                    if due(3 * e + k - 2):
                        sp.wait_ge(e_lo_done, 3 * e + k - 2)
                    if isinstance(e, int) and 3 * e + k == 1:
                        sp.wait_ge(t_mm, 3 * B * G)
                    sp.dma_start(e_raw[k][:], w[ds(e, 1)].rearrange("a (c p) n -> p (a c) n", p=P)).then_inc(d_e[k], 16)

            load_e(0, 0, 0)
            flat = 0
            while flat < NTOK:
                b, s = divmod(flat, S)
                t, p = divmod(flat, P)
                n = min(S - s, P - p)
                if s == 0:
                    sp.wait_ge(x2_done, b + 1)
                sp.dma_start(acc[p:p + n, t, :], X[s:s + n, b, :]).then_inc(d_acc, 16)
                flat += n
            load_e(1, 0, 1)
            pairs(sp, 1, E // 2, load_e)
            for j in range(NT):
                if due(NT * (E - 1) + j + 1):
                    sp.wait_ge(acc_done, NT * (E - 1) + j + 1)
                sp.dma_start(out[j * P:(j + 1) * P, :], acc[:, j, :]).then_inc(d_out, 16)
            sp.wait_ge(d_out, 16 * NT)

        @block.tensor
        def _(pe):
            def ktxt(u):
                t, c = divmod(u, C)
                pe.wait_ge(wk_lo_done, 1)
                pe.wait_ge(txt_lo_done, t + 1)
                if due(u - 3):
                    pe.wait_ge(k_evac, u - 3)
                for k in range(C):
                    mm = mm3(pe, ps[:, c, 0:TXTN], wk_hi[:, k, c * P:(c + 1) * P], wk_lo[:, k, c * P:(c + 1) * P],
                             txt_hi[:, k, :], txt_lo[:, k, :], k == 0, k == C - 1)
                mm.then_inc(ktxt_mm, 1)

            for u in range(4):
                ktxt(u)
            pe.wait_ge(ln0_done, 1)
            pe.wait_ge(const_ones, 1)
            for b in range(B):
                for c in range(C):
                    pe.matmul(ps[:, 4, c * B + b:c * B + b + 1], X[:, b, c * P:(c + 1) * P], rstd[:, b:b + 1],
                              start=True, stop=True)
            pe.matmul(ps[:, 4, 64:64 + B], ones[0:S, :], rm[:, :], start=True, stop=True).then_inc(a1_mm, 1)
            ktxt(4)
            pe.wait_ge(a1_done, 1)
            pe.wait_ge(d_attn, 48)
            for c in range(C):
                mm = pe.matmul(ps[:, 5, 0:B], wvA[:, c, :], meanT[:, c, :], start=(c == 0), stop=(c == C - 1))
            mm.then_inc(a2_mm, 1)
            ktxt(5)
            pe.wait_ge(a2_done, 2)
            for g in range(G):
                mm = pe.matmul(ps[:, 6, g * B:(g + 1) * B], rep[:, g, :, :].rearrange("p r d -> p (r d)"), vT[:, :],
                               start=True, stop=True)
            mm.then_inc(a3_mm, 1)
            ktxt(6)
            pe.wait_ge(a3_done, 1)
            for g in range(G):
                mm = pe.matmul(ps[0:B, 7, :], vrep[:, g, :], woA[:, g, :], start=(g == 0), stop=(g == G - 1))
            mm.then_inc(a4_mm, 1)
            ktxt(7)
            pe.wait_ge(a4_done, 1)
            pe.wait_ge(const_sel, 1)
            for b in range(B):
                if due(b - 3):
                    pe.wait_ge(x1_done, b - 3)
                pe.matmul(ps[0:S, 4 + b % 4, :], sel[:, b, :], o8[:, :], start=True, stop=True).then_inc(a5_mm, 1)

            def sumsq(b):
                pe.wait_ge(k_sum, b + 1)
                if due(b):
                    pe.wait_ge(kx_done, b)
                pe.matmul(ps[:, 7, 0:KEYS], ones[:, :], ksum[:, :], start=True, stop=True).then_inc(ss_mm, 1)

            def values(b, par, t, last=False):
                if due(3 * b + t - 2):
                    pe.wait_ge(v_evac, 3 * b + t - 2)
                wh, wl = (wv_hi, wv_lo) if t == 2 else (wvi_hi, wvi_lo)
                for k in range(C):
                    mm = mm3(pe, ps[:, 4 + t, :], ctx_hi[par][:, k, t * P:(t + 1) * P],
                             ctx_lo[par][:, k, t * P:(t + 1) * P], wh[:, k, :], wl[:, k, :], k == 0, k == C - 1)
                mm.then_inc(vl_mm if last else v_mm, 1)

            def project(b, i, par, first=False):
                pe.wait_ge(ctx_lo_done, b + 1)
                for c in range(C):
                    pe.wait_ge(k_evac, 5 + 4 * b + c)
                    for k in range(C):
                        mm = mm3(pe, ps[:, c, 0:IMGP], wki_hi[:, k, c * P:(c + 1) * P], wki_lo[:, k, c * P:(c + 1) * P],
                                 ctx_hi[par][:, k, 0:IMGP], ctx_lo[par][:, k, 0:IMGP], k == 0, k == C - 1)
                    mm.then_inc(ktxt_mm, 1)
                    if c == 0 and not first:
                        sumsq(b - 1)
                for t in range(3):
                    values(b, par, t)

            pe.wait_ge(w_lo_done, 3)
            pe.wait_ge(x1_done, B)
            project(0, 0, 0, True)
            project(1, 0, 1)
            pairs(pe, 1, B // 2, project)
            pe.wait_ge(ctx_lo_done, B + 1)
            values(B, 0, 0, True)
            sumsq(B - 1)

            def transpose_x(b, src, bank, done, free, out_sem):
                pe.wait_ge(done, b + 1)
                if due(b - 1):
                    pe.wait_ge(free, b - 1)
                for c in range(C):
                    mm = pe.transpose(ps[:, bank, c * S:(c + 1) * S], src[b % 2][:, c * P:(c + 1) * P], ident[0:S, 0:S])
                mm.then_inc(out_sem, 1)

            pe.wait_ge(const_ident, 2)
            pe.wait_ge(k_evac, 8 + 4 * B)
            for b in range(B):
                transpose_x(b, xn1, b % 2, xn1_done, xt1_lo_done, x1t_mm)

            def qsumsq(h):
                pe.wait_ge(q_sum, h + 1)
                pe.matmul(ps[:, 6 + h, 0:HALF], ones[:, :], qsum[:, :], start=True, stop=True).then_inc(qss_mm, 1)

            pe.wait_ge(wq_lo_done, 1)
            pe.wait_ge(v_evac, 3 * B)
            pe.wait_ge(vl_done, 1)
            pe.wait_ge(kx_done, B)
            for u in range(2 * C):
                h, c = divmod(u, C)
                pe.wait_ge(xt1_lo_done, B // 2 * (h + 1))
                if due(u - 3):
                    pe.wait_ge(q_evac, u - 3)
                for k in range(C):
                    mm = mm3(pe, ps[:, 2 + c, 0:HALF], wq_hi[:, k, c * P:(c + 1) * P], wq_lo[:, k, c * P:(c + 1) * P],
                             xt1_hi[:, k, h * HALF:(h + 1) * HALF], xt1_lo[:, k, h * HALF:(h + 1) * HALF],
                             k == 0, k == C - 1)
                mm.then_inc(q_mm, 1)
                if u == C:
                    qsumsq(0)
            qsumsq(1)

            def scores(n, g, a):
                pe.wait_ge(sk_hi, 3 * n + 3)
                pe.wait_ge(sk_klo, n + 1)
                pe.wait_ge(sk_qlo, 4 * n + 4)
                if due(8 * (n - 1) + 4 * a + 4):
                    pe.wait_ge(exp_done, 8 * (n - 1) + 4 * a + 4)
                s = g % 2
                for r in (2 * a, 2 * a + 1):
                    rows, o = slice(HD * r, HD * r + HD), ps[0:S, r, 0:KEYS]
                    pe.matmul(o, qs_hi[s][:, r, :], ks_hi[s][:, :], start=True, stop=False)
                    pe.matmul(o, qs_hi[s][:, r, :], ks_lo[s][:, :], start=False, stop=False)
                    mm = pe.matmul(o, qs_lo[s][rows, :], ks_hi[s][rows, :], start=False, stop=True)
                mm.then_inc(s_mm, 1)

            def turn(n, g, t):
                m = 3 * n + t
                pe.wait_ge(norm_done, 4 * n + 4)
                if due(m - 1):
                    pe.wait_ge(pt_lo_done, m - 1)
                k = TILE[t]
                for r in range(R):
                    mm = pe.transpose(ps[0:k, 4 + (g + t) % 2, r * S:(r + 1) * S], prob[g][:, r, t * P:t * P + k],
                                      ident[0:S, 0:S])
                mm.then_inc(t_mm, 1)

            def pv(n, g, t):
                m = 3 * n + t
                pe.wait_ge(vs_lo_done, n + 1)
                pe.wait_ge(pt_lo_done, m + 1)
                if due(4 * (n - 1)):
                    pe.wait_ge(diag_done, 4 * (n - 1))
                k, v, p, o = TILE[t], g % 2, t, ps[:, 6 + g % 2, 0:R * S]
                mm = mm3(pe, o, vs_hi[v][0:k, t, :], vs_lo[v][0:k, t, :], pt_hi[p][0:k, :], pt_lo[p][0:k, :],
                         t == 0, t == 2)
                mm.then_inc(pv_mm, 1)

            def project_out(b):
                pe.wait_ge(ot_lo_done, b + 1)
                if due(b - 3):
                    pe.wait_ge(x2_done, b - 3)
                for k in range(C):
                    mm = mm3(pe, ps[0:S, b % 4, :], ot_hi[b % 4][:, k, :], ot_lo[b % 4][:, k, :],
                             wo_hi[:, k, :], wo_lo[:, k, :], k == 0, k == C - 1)
                mm.then_inc(o_mm, 1)

            def attend(b, first=False, last=False):
                for g in range(G):
                    n = 4 * b + g
                    for t in range(3):
                        turn(n, g, t)
                        if t < 2 and not (last and g + 2 >= G):
                            scores(n + 2, (g + 2) % G, t)
                        if not (first and 3 * g + t < 2):
                            back = (t - 2) // 3
                            pv(n + back, (g + back) % G, (t - 2) % 3)

            pe.wait_ge(q_evac, 8)
            pe.wait_ge(xt1_lo_done, B)
            for n in range(2):
                for a in range(2):
                    scores(n, n, a)
            pe.wait_ge(qx_done, 2)
            attend(0, first=True)
            with pe.Fori(1, B - 1) as b:
                attend(b)
            attend(B - 1, last=True)
            pe.wait_ge(wo_lo_done, 1)
            pe.wait_ge(exp_done, 8 * B * G)
            project_out(0)
            pv(B * G - 1, G - 1, 1)
            project_out(1)
            pv(B * G - 1, G - 1, 2)

            def logits(h):
                pe.wait_ge(wr_lo_done, 1)
                pe.wait_ge(xt_lo_done, B // 2 * (h + 1))
                pe.wait_ge(diag_done, 4 * B * G)
                for k in range(C):
                    mm = mm3(pe, ps[0:WRP, 6 + h, 0:HALF], wr_hi[:, k, :], wr_lo[:, k, :],
                             xt_hi[:, k, h * HALF:(h + 1) * HALF], xt_lo[:, k, h * HALF:(h + 1) * HALF], k == 0, k == C - 1)
                mm.then_inc(z_mm, 1)

            for b in range(2, B + 2):
                if b < B:
                    project_out(b)
                if b == B:
                    logits(0)
                transpose_x(b - 2, xn2, 4 + b % 2, xn2_done, xt_lo_done, x2t_mm)
            logits(1)
            pe.wait_ge(zt_done, 2)
            for j in range(NT):
                mm = pe.transpose(ps[:, 6, j * E:(j + 1) * E], zT[:, j * P:(j + 1) * P], ident[0:E, 0:E])
            mm.then_inc(zz_mm, 1)

            def gate_up(e, par, part, c):
                n = 8 * e + 4 * part + c
                t0, nt = PART[part]
                if due(n - 1):
                    pe.wait_ge(hf_done, n - 1)
                for w, bank, done in ((eg, c % 2, gate_mm), (eu, 2 + c % 2, up_mm)):
                    for k in range(C):
                        mm = mm3(pe, ps[:, bank, 0:nt], w[par][0][:, k, c * P:(c + 1) * P], w[par][1][:, k, c * P:(c + 1) * P],
                                 xt_hi[:, k, t0:t0 + nt], xt_lo[:, k, t0:t0 + nt], k == 0, k == C - 1)
                    mm.then_inc(done, 1)

            def down(e, par, part):
                pe.wait_ge(h_lo_done, 8 * e + 4 * part + 4)
                for j in range(4 * part, (4, NT)[part]):
                    d = NT * e + j
                    if due(d - 1):
                        pe.wait_ge(acc_done, d - 1)
                    for k in range(FC):
                        mm = mm3(pe, ps[:, 4 + (par + j) % 2, :], h_hi[:, k, j * P:(j + 1) * P], h_lo[:, k, j * P:(j + 1) * P],
                                 ed[par][0][:, k, :], ed[par][1][:, k, :], k == 0, k == FC - 1)
                    mm.then_inc(down_mm, 1)

            def expert(e, i, par, last=False):
                for c in range(1, FC):
                    gate_up(e, par, 0, c)
                gate_up(e, par, 1, 0)
                pe.wait_ge(e_lo_done, 3 * e + 3)
                down(e, par, 0)
                for c in range(1, FC):
                    gate_up(e, par, 1, c)
                if not last:
                    pe.wait_ge(e_lo_done, 3 * e + 5)
                    gate_up(e + 1, 1 - par, 0, 0)
                down(e, par, 1)

            pe.wait_ge(xt_lo_done, B)
            pe.wait_ge(x2_done, B)
            pe.wait_ge(e_lo_done, 2)
            for c in range(FC):
                gate_up(0, 0, 0, c)
            gate_up(0, 0, 1, 0)
            pe.wait_ge(e_lo_done, 3)
            down(0, 0, 0)
            for c in range(1, FC):
                gate_up(0, 0, 1, c)
            pe.wait_ge(e_lo_done, 5)
            gate_up(1, 1, 0, 0)
            down(0, 0, 1)
            expert(1, 0, 1)
            pairs(pe, 1, E // 2 - 1, expert)
            expert(E - 2, 0, 0)
            expert(E - 1, 0, 1, True)

        @block.scalar
        def _(act):
            own = Count()
            act.preload_act_table_set("natural_log_exp_and_others")

            def hi(o, i):
                return act.activation(o, i, ACT.Copy)

            def root(r, t):
                act.activation(r, t, ACT.Ln).then_inc(act_own, 1)
                act.wait_ge(act_own, own.next())
                return act.activation(r, r, ACT.Exp, scale=-0.5)

            act.wait_ge(d_wk, 16)
            hi(wk_hi[:], wk_raw[:]).then_inc(wk_hi_done, 1)
            act.wait_ge(d_txt[0], 16)
            hi(txt_hi[:], txt_raw[0][:]).then_inc(txt_hi_done, 1)

            def ktxt_out(u):
                t, c = divmod(u, C)
                act.wait_ge(ktxt_mm, u + 1)
                act.activation(KT[:, c, t * TB:(t + 1) * TB, IMGP:KEYS],
                               ps[:, c, 0:TXTN].rearrange("p (b n) -> p b n", b=TB), ACT.Identity,
                               bias=col[:, KB + c:KB + c + 1]).then_inc(k_evac, 1)

            act.wait_ge(d_small, 16)
            for u in range(3):
                ktxt_out(u)
            act.wait_ge(ktxt_mm, 4)
            act.wait_ge(d_txt[1], 16)
            act.wait_ge(txt_lo_done, 1)
            hi(txt_hi[:], txt_raw[1][:]).then_inc(txt_hi_done, 1)
            ktxt_out(3)
            act.wait_ge(ln0_x, 1)
            root(lnr0[:], lnx[:]).then_inc(ln0_r, 1)
            act.wait_ge(d_w[0], 16)
            hi(wki_hi[:], w_slot[0][:]).then_inc(w_hi_done, 1)
            ktxt_out(4)
            act.wait_ge(d_w[1], 16)
            hi(wv_hi[:], w_slot[1][:]).then_inc(w_hi_done, 1)
            for u in range(5, 8):
                ktxt_out(u)
            act.wait_ge(a5_mm, B)
            act.wait_ge(d_w[0], 32)
            hi(wvi_hi[:], w_slot[0][:]).then_inc(w_hi_done, 1)

            def split_ctx(b, par, count, n=CKEYS):
                if due(count):
                    act.wait_ge(d_ctx[par], count)
                if due(3 * (b - 1)):
                    act.wait_ge(v_mm, 3 * (b - 1))
                hi(ctx_hi[par][:, :, 0:n], ctx_raw[par][:, :, 0:n]).then_inc(ctx_hi_done, 1)

            act.wait_ge(w_lo_done, 3)
            split_ctx(0, 0, 16)
            act.wait_ge(ln1_x, 1)
            root(lnr0[:], lnx[:]).then_inc(ln1_r, 1)

            def read_project(b, i, par, first=False, last=False):
                if last:
                    split_ctx(B, 0, 16 * (B // 2 + 1), P)
                else:
                    split_ctx(b + 1, 1 - par, 16 * (i + 1 + par))
                for c in range(C):
                    act.wait_ge(ktxt_mm, 2 * C + C * b + c + 1)
                    act.activation(KT[:, c, ds(b, 1), 0:IMGP].rearrange("p a n -> p (a n)"), ps[:, c, 0:IMGP],
                                   ACT.Identity, bias=col[:, KIB + c:KIB + c + 1]).then_inc(k_evac, 1)
                if not first:
                    if due(b):
                        act.wait_ge(kx_done, b)
                    act.activation(kr0[:], kx[:], ACT.Ln).then_inc(act_own, 1)
                    act.wait_ge(act_own, own.next())
                    act.activation(kr0[:], kr0[:], ACT.Exp, scale=-0.5).then_inc(kr_done, 1)
                for t in range(3):
                    act.wait_ge(v_mm, 3 * b + t + 1)
                    act.activation(VV[:, ds(b, 1), t, :].rearrange("p a n -> p (a n)"), ps[:, 4 + t, :],
                                   ACT.Copy).then_inc(v_evac, 1)

            read_project(0, 0, 0, True)
            read_project(1, 0, 1)
            with act.Fori(1, B // 2 - 1) as i:
                own.enter(i, 1, 2)
                for par in range(2):
                    read_project(2 * i + par, i, par)
            own.leave(B // 2 - 2)
            read_project(B - 2, B // 2 - 1, 0)
            read_project(B - 1, B // 2 - 1, 1, last=True)
            act.wait_ge(vl_mm, 1)
            act.activation(vlast[:], ps[0:B, 4, :], ACT.Copy).then_inc(vl_done, 1)
            act.wait_ge(kx_done, B)
            root(kr0[:], kx[:]).then_inc(kr_done, 1)

            act.wait_ge(d_wq, 16)
            hi(wq_hi[:], wq_raw[:]).then_inc(wq_hi_done, 1)
            for b in range(B):
                act.wait_ge(x1t_mm, b + 1)
                hi(xt1_hi[:, :, b * S:(b + 1) * S], ps[:, b % 2, 0:C * S].rearrange("p (c n) -> p c n", c=C)).then_inc(xt1_hi_done, 1)
            for u in range(2 * C):
                h, c = divmod(u, C)
                act.wait_ge(q_mm, u + 1)
                act.activation(QF[:, c, h * HALF:(h + 1) * HALF], ps[:, 2 + c, 0:HALF], ACT.Identity,
                               bias=col[:, QB + c:QB + c + 1]).then_inc(q_evac, 1)
                if u == C + 1:
                    act.wait_ge(qx_done, 1)
                    root(qr0[:], qx[:]).then_inc(qr_done, 1)
            act.wait_ge(qx_done, 2)
            root(qr0[:], qx[:]).then_inc(qr_done, 1)

            def stage_kq(b, g):
                n = 4 * b + g
                if due(2 * n - 2):
                    act.wait_ge(s_mm, 2 * n - 2)
                act.activation(ks_hi[g % 2][:, :], KT[:, g, ds(b, 1), :].rearrange("p a n -> p (a n)"),
                               ACT.Copy).then_inc(sk_hi, 1)
                for r in range(R // 2):
                    rows = slice(HD * r, HD * r + HD)
                    act.activation(qs_hi[g % 2][rows, r, :], QF[rows, g, ds(b * S, S)], ACT.Copy).then_inc(sk_hi, 1)

            def stage_v(b, g):
                n = 4 * b + g
                if due(3 * n - 3):
                    act.wait_ge(pv_mm, 3 * n - 3)
                act.activation(vs_hi[g % 2][:, :, :],
                               VV[:, ds(b, 1), :, g * P:(g + 1) * P].rearrange("p a t n -> p (a t) n"),
                               ACT.Copy).then_inc(vs_hi_done, 1)

            def exps(n, g, a):
                act.wait_ge(max_done, 4 * n + 2 * a + 2)
                if due(3 * n - 9):
                    act.wait_ge(t_mm, 3 * n - 9)
                for r in (2 * a, 2 * a + 1):
                    for kind, (k0, k1) in enumerate(((0, IMG), (IMGP, KEYS))):
                        act.activation(prob[g][:, r, k0:k1], ps[0:S, r, k0:k1], ACT.Exp, bias=nmax[:, g, r, kind:kind + 1],
                                       accum_out=psums[:, g, r, kind:kind + 1]).then_inc(exp_done, 1)

            def pt_hi_part(n, g, t):
                m, k = 3 * n + t, TILE[t]
                act.wait_ge(t_mm, m + 1)
                if due(m - 2):
                    act.wait_ge(pv_mm, m - 2)
                hi(pt_hi[t][0:k, :], ps[0:k, 4 + (g + t) % 2, 0:R * S]).then_inc(pt_hi_done, 1)

            def split_o(b):
                if due(b - 3):
                    act.wait_ge(o_mm, b - 3)
                hi(ot_hi[b % 4][:, :, :], QF[:, :, b * S:(b + 1) * S]).then_inc(ot_hi_done, 1)

            def attend(b, last=False):
                for g in range(G):
                    n = 4 * b + g
                    pt_hi_part(n, g, 0)
                    stage_v(b, g)
                    if not last or g + 3 < G:
                        stage_kq(b + (g + 3) // G, (g + 3) % G)
                    if last and g == G - 1:
                        split_o(1)
                    pt_hi_part(n, g, 1)
                    if not last or g + 2 < G:
                        exps(n + 2, (g + 2) % G, 0)
                    elif g == G - 1:
                        split_o(2)
                    pt_hi_part(n, g, 2)
                    if not last or g + 2 < G:
                        exps(n + 2, (g + 2) % G, 1)
                    elif g == 2:
                        split_o(0)

            act.wait_ge(k_fin, 8 * B)
            act.wait_ge(q_fin, 8)
            act.wait_ge(qs_zero, 2)
            stage_kq(0, 0)
            stage_kq(0, 1)
            act.wait_ge(d_vl, 16 * B)
            act.wait_ge(qx_done, 2)
            for n in range(2):
                for a in range(2):
                    exps(n, n, a)
            stage_kq(0, 2)
            act.wait_ge(d_wo, 16)
            hi(wo_hi[:], wo_raw[:]).then_inc(wo_hi_done, 1)
            attend(0)
            with act.Fori(1, B - 1) as b:
                attend(b)
            attend(B - 1, last=True)

            def split_e(e, par, k, count):
                if due(count):
                    act.wait_ge(d_e[k], count)
                w = (eg, eu, ed)[k]
                act.activation(w[par][0][:], e_raw[k][:], ACT.Copy).then_inc(e_hi_done, 1)

            for b in range(1, B + 3):
                if b >= 3:
                    c = b - 3
                    act.wait_ge(x2t_mm, c + 1)
                    hi(xt_hi[:, :, c * S:(c + 1) * S], ps[:, 4 + c % 2, 0:C * S].rearrange("p (c n) -> p c n", c=C))\
                        .then_inc(xt_hi_done, 1)
                if b + 2 < B:
                    split_o(b + 2)
                if b <= B:
                    c = b - 1
                    act.wait_ge(ln2_x, b)
                    root(lnr0[:, c:b], lnx[:, c:b]).then_inc(ln2_r, 1)
                    act.wait_ge(ln2_done, b)
                    if due(c - 1):
                        act.wait_ge(x2t_mm, c - 1)
                    act.activation(xn2[c % 2][:], X[:, c, :], ACT.Identity, bias=nmr[:, c:b],
                                   scale=rstd[:, c:b]).then_inc(xn2_done, 1)
                if b in (2, 4, 8):
                    split_e(0, 0, (2, 4, 8).index(b), 16)
                if b == 6:
                    act.wait_ge(wr_zero, 1)
                    act.wait_ge(d_wr, 16)
                    hi(wr_hi[:, :, 0:E], wr_raw[:, :, :]).then_inc(wr_hi_done, 1)
                if b == B:
                    act.wait_ge(z_mm, 1)
                    act.activation(zT[:, 0:HALF], ps[0:E, 6, 0:HALF], ACT.Copy).then_inc(zt_done, 1)

            act.wait_ge(z_mm, 2)
            act.activation(zT[:, HALF:NTOK], ps[0:E, 7, 0:HALF], ACT.Copy).then_inc(zt_done, 1)
            act.wait_ge(r_dve, 1)
            act.activation(inh[:], z[:], ACT.Exp, scale=-1.0).then_inc(r_act, 1)
            act.wait_ge(r_dve, 2)
            act.activation(zone[:], dist[:], ACT.Exp, scale=-1.0 / 0.1).then_inc(r_act, 1)
            act.activation(fb[:], dist[:], ACT.Exp, scale=-1.0 / 0.3).then_inc(r_act, 1)

            def unit(n, nt):
                act.wait_ge(gate_mm, n + 1)
                if due(n - 1):
                    act.wait_ge(hf_done, n - 1)
                return nt

            def gate_up(e, part, c, first=False):
                n = 8 * e + 4 * part + c
                t0, nt = PART[part]
                unit(n, nt)
                act.activation(silu[c % 2][:, 0:nt], ps[:, c % 2, 0:nt], ACT.Silu).then_inc(silu_done, 1)
                act.wait_ge(hf_done, n + 1)
                if due(NT * e - 3 if part == 0 else NT * e):
                    act.wait_ge(down_mm, NT * e - 3 if part == 0 else NT * e)
                hi(h_hi[:, c, t0:t0 + nt], hf[c % 2][:, 0:nt]).then_inc(h_hi_done, 1)

            def expert(e, i, par, last=False):
                for c in range(1, FC):
                    gate_up(e, 0, c)
                    if not last:
                        if due(NT * e):
                            act.wait_ge(down_mm, NT * e)
                        split_e(e + 1, 1 - par, c - 1, 16 * (e + 2))
                for c in range(FC):
                    gate_up(e, 1, c)
                if not last:
                    gate_up(e + 1, 0, 0)

            act.wait_ge(d_acc, 16 * n_acc)
            act.wait_ge(xt_lo_done, B)
            gate_up(0, 0, 0)
            expert(0, 0, 0)
            expert(1, 0, 1)
            pairs(act, 1, E // 2 - 1, expert)
            expert(E - 2, 0, 0)
            expert(E - 1, 0, 1, True)

        @block.vector
        def _(dve):
            own = Count()

            def lo(o, i, hi_):
                return dve.tensor_tensor(o, i, f(hi_), ALU.subtract)

            def refine(r, r0_, a, x_):
                dve.tensor_tensor(a, r0_, r0_, ALU.mult).then_inc(dve_own, 1)
                dve.wait_ge(dve_own, own.next())
                dve.scalar_tensor_tensor(a, a, -0.5, x_, ALU.mult, ALU.mult).then_inc(dve_own, 1)
                dve.wait_ge(dve_own, own.next())
                return dve.scalar_tensor_tensor(r, a, 1.5, r0_, ALU.add, ALU.mult)

            def ln_sums(bs):
                for b in bs:
                    ins = dve.bn_stats(stats[:, b, :], X[:, b, :])
                ins.then_inc(dve_own, 1)
                dve.wait_ge(dve_own, own.next())
                for b in bs:
                    ins = dve.bn_aggr(mv[:, b, :], stats[:, b, :])
                ins.then_inc(dve_own, 1)
                dve.wait_ge(dve_own, own.next())

            dve.memset(ones[:], 1.0).then_inc(const_ones, 1)
            dve.wait_ge(wk_hi_done, 1)
            lo(wk_lo[:], wk_raw[:], wk_hi[:]).then_inc(wk_lo_done, 1)
            dve.wait_ge(txt_hi_done, 1)
            lo(txt_lo[:], txt_raw[0][:], txt_hi[:]).then_inc(txt_lo_done, 1)

            dve.wait_ge(d_x, 16)
            ln_sums(range(B))
            dve.tensor_scalar(lnx[:], mv[:, :, 1], LN_EPS, None, ALU.add).then_inc(ln0_x, 1)
            dve.wait_ge(ln0_r, 1)
            refine(rstd[:], lnr0[:], lna[:], lnx[:]).then_inc(dve_own, 1)
            dve.wait_ge(dve_own, own.next())
            dve.tensor_tensor(rm[:], rstd[:], mv[:, :, 0], ALU.mult).then_inc(ln0_done, 1)
            dve.wait_ge(ktxt_mm, 4)
            dve.wait_ge(txt_hi_done, 2)
            lo(txt_lo[:], txt_raw[1][:], txt_hi[:]).then_inc(txt_lo_done, 1)
            dve.wait_ge(d_small, 16)
            dve.tensor_scalar(qscale[:], col[:, NQ:NQ + C], float(HD) ** -0.5, None, ALU.mult).then_inc(dve_own, 1)
            dve.wait_ge(dve_own, own.next())
            dve.tensor_tensor(vbsum[:], col[:, VB:VB + C], col[:, VIB:VIB + C], ALU.add).then_inc(dve_own, 1)
            dve.wait_ge(dve_own, own.next())
            dve.wait_ge(const_ident, 2)
            dve.tensor_copy(rep[:], ident[:].rearrange("p (g d) -> p g d", g=G).unsqueeze(2).to_broadcast([P, G, R, HD]))\
               .then_inc(a2_done, 1)
            dve.wait_ge(a1_mm, 1)
            dve.tensor_scalar(mcorr[:], ps[:, 4, 64:64 + B], 1.0 / S, None, ALU.mult).then_inc(dve_own, 1)
            dve.wait_ge(dve_own, own.next())
            dve.scalar_tensor_tensor(meanT[:], ps[:, 4, 0:C * B].rearrange("p (c b) -> p c b", c=C), 1.0 / S,
                                     mcorr[:].unsqueeze(1).to_broadcast([P, C, B]), ALU.mult, ALU.subtract)\
               .then_inc(a1_done, 1)
            dve.wait_ge(w_hi_done, 1)
            lo(wki_lo[:], w_slot[0][:], wki_hi[:]).then_inc(w_lo_done, 1)
            dve.wait_ge(a2_mm, 1)
            dve.tensor_copy(vT[:], ps[:, 5, 0:B]).then_inc(a2_done, 1)
            dve.wait_ge(a3_mm, 1)
            dve.tensor_copy(vrep[:].rearrange("p g b -> p (g b)"), ps[:, 6, 0:G * B]).then_inc(a3_done, 1)
            dve.wait_ge(w_hi_done, 2)
            lo(wv_lo[:], w_slot[1][:], wv_hi[:]).then_inc(w_lo_done, 1)
            dve.wait_ge(a4_mm, 1)
            dve.tensor_tensor(o8[:], ps[0:B, 7, :], o8[:], ALU.add).then_inc(a4_done, 1)
            for b in range(B):
                dve.wait_ge(a5_mm, b + 1)
                dve.tensor_tensor(X[:, b, :], ps[0:S, 4 + b % 4, :], X[:, b, :], ALU.add).then_inc(x1_done, 1)
            dve.wait_ge(w_hi_done, 3)
            lo(wvi_lo[:], w_slot[0][:], wvi_hi[:]).then_inc(w_lo_done, 1)
            dve.wait_ge(ctx_hi_done, 1)
            lo(ctx_lo[0][:], ctx_raw[0][:], ctx_hi[0][:]).then_inc(ctx_lo_done, 1)
            dve.wait_ge(x1_done, B)
            ln_sums(range(B))
            dve.tensor_scalar(lnx[:], mv[:, :, 1], LN_EPS, None, ALU.add).then_inc(ln1_x, 1)
            dve.wait_ge(ln1_r, 1)
            refine(rstd[:], lnr0[:], lna[:], lnx[:]).then_inc(dve_own, 1)
            dve.wait_ge(dve_own, own.next())

            def key_norm(b):
                dve.wait_ge(ss_mm, b + 1)
                if due(b):
                    dve.wait_ge(kr_done, b)
                dve.tensor_scalar(kx[:], ps[:, 7, 0:KEYS], 1.0 / D, RMS_EPS, ALU.mult, ALU.add).then_inc(kx_done, 1)
                dve.wait_ge(kr_done, b + 1)
                refine(ka[:], kr0[:], ka[:], kx[:]).then_inc(dve_own, 1)
                dve.wait_ge(dve_own, own.next())
                for c in range(C):
                    for k0, k1, w in ((0, IMGP, NKI), (IMGP, KEYS, NK)):
                        kt = KT[:, c, ds(b, 1), k0:k1].rearrange("p a n -> p (a n)")
                        dve.scalar_tensor_tensor(kt, kt, col[:, w + c:w + c + 1], ka[:, k0:k1], ALU.mult, ALU.mult)\
                           .then_inc(k_fin, 1)

            def project(b, i, par, first=False, last=False):
                n = P if last else CKEYS
                dve.wait_ge(ctx_hi_done, b + 2)
                lo(ctx_lo[1 - par][:, :, 0:n], ctx_raw[1 - par][:, :, 0:n], ctx_hi[1 - par][:, :, 0:n]).then_inc(ctx_lo_done, 1)
                if not first:
                    if due(8 * (b - 1)):
                        dve.wait_ge(k_fin, 8 * (b - 1))
                    key_norm(b - 1)

            project(0, 0, 0, True)
            project(1, 0, 1)
            with dve.Fori(1, B // 2 - 1) as i:
                own.enter(i, 1, 6)
                for par in range(2):
                    project(2 * i + par, i, par)
            own.leave(B // 2 - 2)
            project(B - 2, B // 2 - 1, 0)
            project(B - 1, B // 2 - 1, 1, last=True)
            if due(8 * (B - 1)):
                dve.wait_ge(k_fin, 8 * (B - 1))
            key_norm(B - 1)

            dve.wait_ge(vl_mm, 1)
            dve.wait_ge(wq_hi_done, 1)
            lo(wq_lo[:], wq_raw[:], wq_hi[:]).then_inc(wq_lo_done, 1)
            for b in range(B + 1):
                if b < B:
                    if due(b - 1):
                        dve.wait_ge(x1t_mm, b - 1)
                    dve.tensor_scalar(xn1[b % 2][:], X[:, b, :], mv[:, b, 0:1], rstd[:, b:b + 1], ALU.subtract, ALU.mult)\
                       .then_inc(xn1_done, 1)
                if b >= 1:
                    c = b - 1
                    dve.wait_ge(xt1_hi_done, c + 1)
                    lo(xt1_lo[:, :, c * S:(c + 1) * S], ps[:, c % 2, 0:C * S].rearrange("p (c n) -> p c n", c=C), xt1_hi[:, :, c * S:(c + 1) * S]).then_inc(xt1_lo_done, 1)
            for h in range(2):
                dve.wait_ge(qss_mm, h + 1)
                if due(4 * h):
                    dve.wait_ge(q_fin, 4 * h)
                dve.tensor_scalar(qx[:], ps[:, 6 + h, 0:HALF], 1.0 / D, RMS_EPS, ALU.mult, ALU.add).then_inc(qx_done, 1)
                dve.wait_ge(qr_done, h + 1)
                refine(qa[:], qr0[:], qa[:], qx[:]).then_inc(dve_own, 1)
                dve.wait_ge(dve_own, own.next())
                for c in range(C):
                    qf = QF[:, c, h * HALF:(h + 1) * HALF]
                    dve.scalar_tensor_tensor(qf, qf, qscale[:, c:c + 1], qa[:], ALU.mult, ALU.mult).then_inc(q_fin, 1)

            def split_q(b, g):
                n = 4 * b + g
                if due(2 * n - 2):
                    dve.wait_ge(s_mm, 2 * n - 2)
                for r in range(R // 2, R):
                    rows = slice(HD * r, HD * r + HD)
                    dve.tensor_copy(qs_hi[g % 2][rows, r, :], QF[rows, g, ds(b * S, S)]).then_inc(sk_qhi, 1)
                for r in range(R):
                    rows = slice(HD * r, HD * r + HD)
                    if r == 0:
                        dve.wait_ge(sk_hi, 3 * n + 3)
                    if r == R // 2:
                        dve.wait_ge(sk_qhi, 2 * n + 2)
                    lo(qs_lo[g % 2][rows, :], QF[rows, g, ds(b * S, S)], qs_hi[g % 2][rows, r, :]).then_inc(sk_qlo, 1)

            def maxima(n, g, a):
                dve.wait_ge(s_mm, 2 * n + a + 1)
                for kind, (k0, k1) in enumerate(((0, IMG), (IMGP, KEYS))):
                    dve.tensor_reduce(nmax[:, g, 2 * a:2 * a + 2, kind], ps[0:S, 2 * a:2 * a + 2, k0:k1], AX.X, ALU.max,
                                      negate=True).then_inc(max_done, 1)

            def reciprocals(n, g, a):
                dve.wait_ge(exp_done, 8 * n + 4 * a + 4)
                dve.reciprocal(prec[:, g, 2 * a:2 * a + 2, :], psums[:, g, 2 * a:2 * a + 2, :]).then_inc(rec_done, 1)

            def pt_lo_part(n, g, t):
                m, k, s = 3 * n + t, TILE[t], (g + t) % 2
                dve.wait_ge(pt_hi_done, m + 1)
                lo(pt_lo[t][0:k, :], ps[0:k, 4 + s, 0:R * S], pt_hi[t][0:k, :]).then_inc(pt_lo_done, 1)

            def diagonal(b, g):
                n = 4 * b + g
                dve.wait_ge(pv_mm, 3 * n + 3)
                for r in range(R):
                    rows = slice(HD * r, HD * r + HD)
                    dve.tensor_scalar(QF[rows, g, ds(b * S, S)], ps[rows, 6 + g % 2, r * S:(r + 1) * S], vbsum[rows, g:g + 1],
                                      None, ALU.add).then_inc(diag_done, 1)

            def attend(b, first=False, last=False):
                for g in range(G):
                    n = 4 * b + g
                    pt_lo_part(n, g, 0)
                    if not last or g + 1 < G:
                        reciprocals(n + 1, (g + 1) % G, 1)
                    if not last or g + 2 < G:
                        maxima(n + 2, (g + 2) % G, 0)
                    pt_lo_part(n, g, 1)
                    if not last or g + 2 < G:
                        maxima(n + 2, (g + 2) % G, 1)
                    if not last or g + 3 < G:
                        split_q(b + (g + 3) // G, (g + 3) % G)
                    pt_lo_part(n, g, 2)
                    if not last or g + 2 < G:
                        reciprocals(n + 2, (g + 2) % G, 0)
                    if not (first and g == 0):
                        diagonal(b - (g == 0), (g - 1) % G)

            dve.wait_ge(d_vl, 16 * B)
            dve.wait_ge(qs_zero, 2)
            split_q(0, 0)
            split_q(0, 1)
            dve.wait_ge(q_fin, 8)
            for a in range(2):
                maxima(0, 0, a)
            for a in range(2):
                maxima(1, 1, a)
            reciprocals(0, 0, 0)
            reciprocals(0, 0, 1)
            reciprocals(1, 1, 0)
            split_q(0, 2)
            dve.wait_ge(wo_hi_done, 1)
            lo(wo_lo[:], wo_raw[:], wo_hi[:]).then_inc(wo_lo_done, 1)
            attend(0, first=True)
            with dve.Fori(1, B - 1) as b:
                attend(b)
            attend(B - 1, last=True)
            dve.wait_ge(s_mm, 2 * B * G)
            dve.memset(f(wr_hi[:]), 0.0).then_inc(dve_own, 1)
            dve.wait_ge(dve_own, own.next())
            dve.memset(f(wr_lo[:]), 0.0).then_inc(wr_zero, 1)
            diagonal(B - 1, 3)

            for b in range(1, B + 3):
                c = b - 1
                if b <= B:
                    dve.wait_ge(o_mm, b)
                    dve.tensor_tensor(X[:, c, :], ps[0:S, c % 4, :], X[:, c, :], ALU.add).then_inc(x2_done, 1)
                    dve.wait_ge(x2_done, b)
                    ln_sums([c])
                    dve.tensor_scalar(lnx[:, c:b], mv[:, c, 1:2], LN_EPS, None, ALU.add).then_inc(ln2_x, 1)
                if b >= 3:
                    t = b - 3
                    dve.wait_ge(xt_hi_done, t + 1)
                    lo(xt_lo[:, :, t * S:(t + 1) * S], ps[:, 4 + t % 2, 0:C * S].rearrange("p (c n) -> p c n", c=C),
                       xt_hi[:, :, t * S:(t + 1) * S]).then_inc(xt_lo_done, 1)
                if b == B - 1:
                    dve.wait_ge(wr_hi_done, 1)
                    dve.wait_ge(wr_zero, 1)
                    lo(wr_lo[:, :, 0:E], wr_raw[:, :, :], wr_hi[:, :, 0:E]).then_inc(wr_lo_done, 1)
                if b <= B:
                    dve.wait_ge(ln2_r, b)
                    refine(rstd[:, c:b], lnr0[:, c:b], lna[:, c:b], lnx[:, c:b]).then_inc(dve_own, 1)
                    dve.wait_ge(dve_own, own.next())
                    dve.scalar_tensor_tensor(nmr[:, c:b], mv[:, c, 0:1], -1.0, rstd[:, c:b], ALU.mult, ALU.mult)\
                       .then_inc(ln2_done, 1)

            itemp = s2[:, 0:1]
            dve.reciprocal(itemp, col[:, TEMP:TEMP + 1]).then_inc(dve_own, 1)
            dve.wait_ge(dve_own, own.next())
            dve.wait_ge(zz_mm, 1)
            dve.tensor_scalar(z[:].rearrange("p t e -> p (t e)"), ps[:, 6, 0:NT * E], itemp, None, ALU.mult).then_inc(r_dve, 1)
            dve.wait_ge(r_act, 1)
            dve.tensor_scalar(inh[:], inh[:], 1.0, None, ALU.add).then_inc(dve_own, 1)
            dve.wait_ge(dve_own, own.next())
            dve.reciprocal(inh[:], inh[:]).then_inc(dve_own, 1)
            dve.wait_ge(dve_own, own.next())
            dve.tensor_scalar(dist[:], inh[:], -ZONE_MID, None, ALU.add).then_inc(dve_own, 1)
            dve.wait_ge(dve_own, own.next())
            dve.tensor_scalar(rnk[:], dist[:], -1.0, None, ALU.mult).then_inc(dve_own, 1)
            dve.wait_ge(dve_own, own.next())
            dve.tensor_tensor(dist[:], dist[:], rnk[:], ALU.max).then_inc(r_dve, 1)
            dve.wait_ge(r_dve, 2)
            dve.tensor_scalar(rnk[:], inh[:], ZONE_LO, None, ALU.is_ge).then_inc(dve_own, 1)
            dve.wait_ge(dve_own, own.next())
            dve.scalar_tensor_tensor(rnk[:], inh[:], ZONE_HI, rnk[:], ALU.is_le, ALU.mult).then_inc(dve_own, 1)
            dve.wait_ge(dve_own, own.next())
            dve.wait_ge(r_act, 3)
            dve.tensor_tensor(wtok[:], zone[:], rnk[:], ALU.mult).then_inc(dve_own, 1)
            dve.wait_ge(dve_own, own.next())
            dve.tensor_reduce(s1[:], wtok[:], AX.X, ALU.add).then_inc(dve_own, 1)
            dve.wait_ge(dve_own, own.next())
            dve.tensor_scalar(s1[:], s1[:], 1e-8, None, ALU.is_lt).then_inc(dve_own, 1)
            dve.wait_ge(dve_own, own.next())
            fb_e = fb[:].unsqueeze(3).to_broadcast([P, NT, E, E])
            fb_j = fb[:].unsqueeze(2).to_broadcast([P, NT, E, E])
            dve.tensor_tensor(rank2[:], fb_j, fb_e, ALU.is_gt).then_inc(dve_own, 1)
            dve.wait_ge(dve_own, own.next())
            dve.tensor_reduce(rnk[:], rank2[:], AX.X, ALU.add).then_inc(dve_own, 1)
            dve.wait_ge(dve_own, own.next())
            dve.tensor_tensor(rank2[:], fb_j, fb_e, ALU.is_equal).then_inc(dve_own, 1)
            dve.wait_ge(dve_own, own.next())
            dve.wait_ge(const_ident, 3)
            dve.tensor_tensor(rank2[:], rank2[:], tril[:].unsqueeze(1).to_broadcast([P, NT, E, E]), ALU.mult).then_inc(dve_own, 1)
            dve.wait_ge(dve_own, own.next())
            dve.tensor_reduce(inh[:], rank2[:], AX.X, ALU.add).then_inc(dve_own, 1)
            dve.wait_ge(dve_own, own.next())
            dve.tensor_tensor(rnk[:], rnk[:], inh[:], ALU.add).then_inc(dve_own, 1)
            dve.wait_ge(dve_own, own.next())
            dve.scalar_tensor_tensor(fb[:], rnk[:], 1.5, fb[:], ALU.is_lt, ALU.mult).then_inc(dve_own, 1)
            dve.wait_ge(dve_own, own.next())

            def over_sum(t):
                dve.tensor_reduce(s2[:], t[:], AX.X, ALU.add).then_inc(dve_own, 1)
                dve.wait_ge(dve_own, own.next())
                dve.tensor_scalar(s2[:], s2[:], 1e-8, None, ALU.max).then_inc(dve_own, 1)
                dve.wait_ge(dve_own, own.next())
                dve.reciprocal(s2[:], s2[:]).then_inc(dve_own, 1)
                dve.wait_ge(dve_own, own.next())
                dve.tensor_tensor(t[:], t[:], s2[:].unsqueeze(2).to_broadcast([P, NT, E]), ALU.mult).then_inc(dve_own, 1)
                dve.wait_ge(dve_own, own.next())

            over_sum(fb)
            dve.tensor_tensor(fb[:], fb[:], s1[:].unsqueeze(2).to_broadcast([P, NT, E]), ALU.mult).then_inc(dve_own, 1)
            dve.wait_ge(dve_own, own.next())
            dve.tensor_scalar(s1[:], s1[:], -1.0, 1.0, ALU.mult, ALU.add).then_inc(dve_own, 1)
            dve.wait_ge(dve_own, own.next())
            dve.tensor_tensor(wtok[:], wtok[:], s1[:].unsqueeze(2).to_broadcast([P, NT, E]), ALU.mult).then_inc(dve_own, 1)
            dve.wait_ge(dve_own, own.next())
            dve.tensor_tensor(wtok[:], wtok[:], fb[:], ALU.add).then_inc(dve_own, 1)
            dve.wait_ge(dve_own, own.next())
            over_sum(wtok)

            def gate_up(e, part, c):
                n = 8 * e + 4 * part + c
                t0, nt = PART[part]
                dve.wait_ge(silu_done, n + 1)
                dve.wait_ge(up_mm, n + 1)
                if due(n - 1):
                    dve.wait_ge(h_hi_done, n - 1)
                if due(n - 1):
                    dve.wait_ge(h_lo_done, n - 1)
                dve.tensor_tensor(hf[c % 2][:, 0:nt], silu[c % 2][:, 0:nt], ps[:, 2 + c % 2, 0:nt], ALU.mult)\
                   .then_inc(hf_done, 1)
                dve.wait_ge(h_hi_done, n + 1)
                lo(h_lo[:, c, t0:t0 + nt], hf[c % 2][:, 0:nt], h_hi[:, c, t0:t0 + nt]).then_inc(h_lo_done, 1)

            def add(e, par, part):
                for j in range(4 * part, (4, NT)[part]):
                    d = NT * e + j
                    dve.wait_ge(down_mm, d + 1)
                    if due(d - NT + 1):
                        dve.wait_ge(acc_done, d - NT + 1)
                    dve.scalar_tensor_tensor(acc[:, j, :], ps[:, 4 + (par + j) % 2, :],
                                             wtok[:, j, ds(e, 1)], acc[:, j, :], ALU.mult, ALU.add)\
                       .then_inc(acc_done, 1)

            def expert(e, i, par, last=False):
                for c in range(1, FC):
                    gate_up(e, 0, c)
                gate_up(e, 1, 0)
                add(e, par, 0)
                for c in range(1, FC):
                    gate_up(e, 1, c)
                if not last:
                    gate_up(e + 1, 0, 0)
                add(e, par, 1)

            gate_up(0, 0, 0)
            expert(0, 0, 0)
            expert(1, 0, 1)
            pairs(dve, 1, E // 2 - 1, expert)
            expert(E - 2, 0, 0)
            expert(E - 1, 0, 1, True)

        @block.gpsimd
        def _(pool):
            own = Count()
            pool.memset(ident[:], 0.0).then_inc(pool_own, 1)
            pool.wait_ge(pool_own, own.next())
            pool.affine_select(out=ident[:], in_=ident[:], compare_op=ALU.not_equal, fill=1.0, base=0,
                               pattern=[[-1, P]], channel_multiplier=1).then_inc(const_ident, 2)
            pool.memset(sel[:], 0.0).then_inc(pool_own, 1)
            pool.wait_ge(pool_own, own.next())
            pool.affine_select(out=sel[:], in_=sel[:], compare_op=ALU.not_equal, fill=1.0, base=0,
                               pattern=[[-1, B], [0, S]], channel_multiplier=1).then_inc(const_sel, 1)
            pool.memset(tril[:], 1.0).then_inc(pool_own, 1)
            pool.wait_ge(pool_own, own.next())
            pool.affine_select(out=tril[:], in_=tril[:], compare_op=ALU.is_gt, fill=0.0, base=0,
                               pattern=[[1, E], [-1, E]], channel_multiplier=0).then_inc(const_ident, 1)

            def square_sum(b, first=False):
                for c in range(C):
                    kt = KT[:, c, ds(b, 1), :].rearrange("p a n -> p (a n)")
                    pool.wait_ge(k_evac, 2 * C + C * b + c + 1)
                    if c == 0:
                        if due(b):
                            pool.wait_ge(ss_mm, b)
                        pool.tensor_tensor(ksum[:], kt, kt, ALU.mult).then_inc(pool_own, 1)
                        pool.wait_ge(pool_own, own.next())
                    else:
                        pool.tensor_tensor(ksq[:], kt, kt, ALU.mult).then_inc(pool_own, 1)
                        pool.wait_ge(pool_own, own.next())
                        ins = pool.tensor_tensor(ksum[:], ksum[:], ksq[:], ALU.add)
                        if c < C - 1:
                            ins.then_inc(pool_own, 1)
                            pool.wait_ge(pool_own, own.next())
                        else:
                            ins.then_inc(k_sum, 1)

            square_sum(0)
            with pool.Fori(1, B) as b:
                own.enter(b, 1, 2 * C - 2)
                square_sum(b)
            own.leave(B - 1)

            pool.wait_ge(d_ob, 16)
            for b in range(B):
                pool.wait_ge(xn1_done, b + 1)
                ins = pool.tensor_tensor(X[:, b, :], X[:, b, :], ob_sb[:], ALU.add)
            ins.then_inc(pool_own, 1)
            pool.wait_ge(pool_own, own.next())
            for h in range(2):
                for c in range(C):
                    qf = QF[:, c, h * HALF:(h + 1) * HALF]
                    pool.wait_ge(q_evac, C * h + c + 1)
                    if c == 0:
                        if due(h):
                            pool.wait_ge(qss_mm, h)
                        pool.tensor_tensor(qsum[:], qf, qf, ALU.mult).then_inc(pool_own, 1)
                        pool.wait_ge(pool_own, own.next())
                    else:
                        pool.tensor_tensor(qsq[:], qf, qf, ALU.mult).then_inc(pool_own, 1)
                        pool.wait_ge(pool_own, own.next())
                        ins = pool.tensor_tensor(qsum[:], qsum[:], qsq[:], ALU.add)
                        if c < C - 1:
                            ins.then_inc(pool_own, 1)
                            pool.wait_ge(pool_own, own.next())
                        else:
                            ins.then_inc(q_sum, 1)

            pool.wait_ge(q_fin, 8)
            pool.wait_ge(q_mm, 2 * C)
            for i in range(2):
                pool.memset(f(qs_hi[i][:]), 0.0).then_inc(qs_zero, 1)
            for i in range(4):
                ins = pool.memset(prob[i][:, :, IMG:IMGP], 0.0)
            ins.then_inc(pool_own, 1)
            pool.wait_ge(pool_own, own.next())

            def k_lo(b, g):
                n = 4 * b + g
                pool.wait_ge(sk_hi, 3 * n + 1)
                pool.tensor_tensor(ks_lo[g % 2][:, :], KT[:, g, ds(b, 1), :].rearrange("p a n -> p (a n)"),
                                   f(ks_hi[g % 2][:, :]), ALU.subtract).then_inc(sk_klo, 1)

            def v_lo(b, g):
                n = 4 * b + g
                pool.wait_ge(vs_hi_done, n + 1)
                pool.tensor_tensor(vs_lo[g % 2][:, :, :], VV[:, ds(b, 1), :, g * P:(g + 1) * P].rearrange("p a t n -> p (a t) n"),
                                   f(vs_hi[g % 2][:, :, :]), ALU.subtract).then_inc(vs_lo_done, 1)

            def normalise(n, g, a):
                pool.wait_ge(rec_done, 2 * n + a + 1)
                for kind, (k0, k1) in enumerate(((0, IMG), (IMGP, KEYS))):
                    p = prob[g][:, 2 * a:2 * a + 2, k0:k1]
                    pool.tensor_tensor(p, p, prec[:, g, 2 * a:2 * a + 2, kind:kind + 1].to_broadcast([S, 2, k1 - k0]), ALU.mult)\
                        .then_inc(norm_done, 1)

            def attend(b, last=False):
                for g in range(G):
                    n = 4 * b + g
                    v_lo(b, g)
                    if not last or g + 1 < G:
                        normalise(n + 1, (g + 1) % G, 1)
                    if not last or g + 3 < G:
                        k_lo(b + (g + 3) // G, (g + 3) % G)
                    if not last or g + 2 < G:
                        normalise(n + 2, (g + 2) % G, 0)

            k_lo(0, 0)
            k_lo(0, 1)
            normalise(0, 0, 0)
            normalise(0, 0, 1)
            normalise(1, 1, 0)
            k_lo(0, 2)
            attend(0)
            with pool.Fori(1, B - 1) as b:
                attend(b)
            attend(B - 1, last=True)

            def o_lo(b):
                pool.wait_ge(ot_hi_done, b + 1)
                pool.tensor_tensor(ot_lo[b % 4][:, :, :], QF[:, :, b * S:(b + 1) * S], f(ot_hi[b % 4][:, :, :]), ALU.subtract)\
                    .then_inc(ot_lo_done, 1)

            def e_lo(e, par):
                for k in range(3):
                    e_lo_part(e, par, k)

            def e_lo_part(e, par, k):
                w = (eg, eu, ed)[k]
                pool.wait_ge(e_hi_done, 3 * e + k + 1)
                pool.tensor_tensor(w[par][1][:], e_raw[k][:], f(w[par][0][:]), ALU.subtract).then_inc(e_lo_done, 1)

            for b in range(B):
                o_lo(b)
                if b == 5:
                    e_lo_part(0, 0, 0)
            e_lo_part(0, 0, 1)
            e_lo_part(0, 0, 2)
            e_lo(1, 1)
            pairs(pool, 1, E // 2, lambda e, i, par: e_lo(e, par))


NAMES = ("x", "ctxT", "ctx_txt", "ctx_last", "wkv", "wo_attn", "bo8", "wkT", "wkiT", "wvT", "wviT", "wqT", "woT", "ob",
         "cols", "wg", "wu", "wd", "wr")


def lay_out(i):
    c = np.asarray(i["ctx_2048"])
    t = c.transpose(0, 2, 1).reshape(B, C, P, CTX).transpose(0, 2, 1, 3)
    ctxT = np.zeros((B, P, C, CKEYS), c.dtype)
    ctxT[..., :IMG] = t[..., :IMG]
    ctxT[..., IMGP:KEYS] = t[..., IMG:]
    ctx_txt = t[..., IMG:].reshape(B // TB, TB, P, C, TXT).transpose(0, 2, 3, 1, 4).reshape(B // TB, P, C, TXTN)
    ctx_last = np.zeros((P, C, P), c.dtype)
    ctx_last[..., :B] = t[..., IMG - 1].transpose(1, 2, 0)

    def wT(w):
        return np.asarray(w).T.reshape(C, P, D).transpose(1, 0, 2)

    def vec(v):
        return np.asarray(v).reshape(C, P).T

    x = "L0_xattn_"
    temp = np.broadcast_to(np.asarray(i["L0_ffn_temperature"]).reshape(1, 1), (P, 1))
    cols = np.concatenate([vec(i[x + n]) for n in ("q_b", "k_b", "k_img_b", "v_b", "v_img_b", "norm_q_w", "norm_k_w",
                                                   "norm_k_img_w")] + [temp], axis=1)
    arrays = (i["x"], ctxT, ctx_txt, ctx_last, i["L0_attn_Wkv"], i["L0_attn_Wo"],
              np.broadcast_to(np.asarray(i["L0_attn_bo"]), (B, D)),
              wT(i[x + "k_w"]), wT(i[x + "k_img_w"]), wT(i[x + "v_w"]), wT(i[x + "v_img_w"]), wT(i[x + "q_w"]),
              wT(i[x + "o_w"]), np.broadcast_to(np.asarray(i[x + "o_b"]), (S, D)), cols,
              i["L0_ffn_Wg"], i["L0_ffn_Wu"], i["L0_ffn_Wd"], i["L0_ffn_Wr"])
    return {n: np.ascontiguousarray(a) for n, a in zip(NAMES, arrays)}


def kernel(**inputs):
    import concourse.bacc as bacc
    from concourse.bass_utils import run_bass_kernel_spmd

    nc = bacc.Bacc("TRN2", target_bir_lowering=False, num_devices=1)
    arrays = {f"in_{n}": a for n, a in lay_out(inputs).items()}
    args = [nc.dram_tensor(n, a.shape, mybir.dt.from_np(a.dtype), kind="ExternalInput").ap() for n, a in arrays.items()]
    out = nc.dram_tensor("out", (NTOK, D), F32, kind="ExternalOutput").ap()
    decoder(nc, *args, out)
    r = run_bass_kernel_spmd(nc, [arrays], core_ids=[0])
    return r.results[0]["out"].reshape(B, S, D)
```

```python
from contextlib import ExitStack

import numpy as np

import concourse.bass as bass
from concourse import mybir

F32 = mybir.dt.float32
F32R = mybir.dt.float32r
ALU = mybir.AluOpType
ACT = mybir.ActivationFunctionType
AX = mybir.AxisListType

P = 128
B, S, D = 8, 112, 512
C = D // P
NH, HD = 16, 32
G = 4
R = NH // G
IMG, CTX = 257, 375
TXT = CTX - IMG
IMGP = IMG + 1
KEYS = IMGP + TXT
TILE = [P, P, KEYS - 2 * P]
CKEYS = 3 * P
TB = 4
TXTN = TB * TXT
HALF = B // 2 * S
E, F = 8, 512
FC = F // P
NT = B * S // P
NTOK = B * S
PART = [(0, 4 * P), (4 * P, 3 * P)]
WINDOW_SIDE, GLOBAL = 64, 64
LN_EPS, RMS_EPS = 1e-5, 1e-6
WRP = 72
ZONE_MID = float(1.0 / np.e)
ZONE_LO = float(np.float32(0.5 - np.log(4.0 / 3.0)))
ZONE_HI = 0.5
QB, KB, KIB, VB, VIB, NQ, NK, NKI, TEMP = (C * i for i in range(9))
NCOLS = TEMP + 1

assert S - 1 - GLOBAL <= WINDOW_SIDE


def due(value):
    return not isinstance(value, int) or value > 0


class Count:

    def __init__(self):
        self.base, self.n = 0, 0

    def next(self):
        self.n += 1
        return self.base + self.n

    def enter(self, i, first, per):
        self.start, self.per = self.base + self.n, per
        self.base, self.n = self.start + (i - first) * per, 0

    def leave(self, rounds):
        assert self.n == self.per, (self.n, self.per)
        self.base, self.n = self.start + rounds * self.per, 0


def decoder(nc, x, ctxT, ctx_txt, ctx_last, wkv, wo_attn, bo8, wkT, wkiT, wvT, wviT, wqT, woT, ob, cols,
            wg, wu, wd, wr, out):
    with ExitStack() as ctx:
        base = 16640
        end = 229368

        def at(name, offset, shape, dt=F32):
            size = int(np.prod(shape[1:])) * 4
            assert base + offset + size <= end and offset % 32 == 0, (name, offset, size)
            return nc.alloc_sbuf_tensor_at(name, list(shape), dt, offset=base + offset)

        def pair(name, offset, shape):
            size = int(np.prod(shape[1:])) * 4
            return at(name + "_hi", offset, shape, F32R), at(name + "_lo", offset + size, shape, F32R)

        def sem(name):
            return ctx.enter_context(nc.semaphore(name))

        ident = at("ident", 0, [P, P])
        ones = at("ones", 512, [P, P])
        col = at("col", 1024, [P, NCOLS])
        wr_raw = at("wr_raw", 1184, [P, C, E])
        qscale = at("qscale", 1312, [P, C])
        vbsum = at("vbsum", 1328 + 16, [P, C])
        stats = at("stats", 1536, [S, B, 6])
        mv = at("mv", 1728, [S, B, 2])
        lnx, lnr0, lna, rstd = (at(n, 1792 + 32 * i, [S, B]) for i, n in enumerate(("lnx", "lnr0", "lna", "rstd")))
        rm = at("rm", 1920, [S, B])
        meanT = at("meanT", 1952, [P, C, B])
        vT = at("vT", 2080, [P, B])
        vrep = at("vrep", 2112, [P, G, B])
        mcorr = at("mcorr", 2240, [B, 1])
        mean8 = at("mean8", 2496, [B, D])
        eye8 = at("eye8", 4544, [S, B, B])
        rmask = at("rmask", 4800, [S, B, B])
        vlast = at("vlast", 2496, [B, D])
        tril = at("tril", 5120, [P, E, E])
        KT0, VV0, QF0 = 5376, 5376 + 48128, 5376 + 48128 + 49152
        KT = at("KT", KT0, [P, C, B, KEYS])
        VV = at("VV", VV0, [P, B, 3, D])
        wk_hi, wk_lo = pair("wk", VV0, [P, C, D])
        txt_raw = [at(f"txt_raw{t}", VV0 + 16384 + 7552 * t, [P, C, TXTN]) for t in range(2)]
        txt_hi, txt_lo = pair("txt", VV0 + 31488, [P, C, TXTN])
        A0 = QF0
        wki_hi, wki_lo = pair("wki", A0, [P, C, D])
        wv_hi, wv_lo = pair("wv", A0 + 16384, [P, C, D])
        wvi_hi, wvi_lo = pair("wvi", A0 + 32768, [P, C, D])
        CT0 = A0 + 49152
        woA = at("woA", CT0 + 16384, [P, G, D])
        wvA = at("wvA", CT0 + 32768, [P, C, P])
        rep = at("rep", CT0 + 34816, [P, G, R, HD])
        o8 = at("o8", CT0 + 36864, [B, D])
        sel = at("sel", CT0 + 38912, [B, B, S], F32R)
        o8_hi = at("o8_hi", 2496, [B, D], F32R)
        o8_lo = at("o8_lo", VV0 + 46592, [B, D], F32R)
        ctx_hi, ctx_lo = zip(*(pair(f"ctx{i}", CT0 + 12288 * i, [P, C, CKEYS]) for i in range(2)))
        w_slot = [at(f"w_slot{i}", CT0 + 8192 * i, [P, C, D]) for i in range(2)]
        ctx_raw = [at(f"ctx_raw{i}", CT0 + 24576 + 6144 * i, [P, C, CKEYS]) for i in range(2)]
        last_raw = at("last_raw", CT0 + 32768, [P, C, P])
        wk_raw = at("wk_raw", CT0 + 24576, [P, C, D])
        KS0 = CT0 + 36864
        ksq, ksum, kx, kr0, ka = (at(n, KS0 + 1504 * i, [P, KEYS]) for i, n in enumerate(("ksq", "ksum", "kx", "kr0", "ka")))
        QF = at("QF", QF0, [P, C, NTOK])
        X1 = QF0 + 14336
        xt1_hi, xt1_lo = pair("xt1", X1, [P, C, NTOK])
        wq_hi, wq_lo = pair("wq", X1 + 28672, [P, C, D])
        qsq, qsum, qx, qr0, qa = (at(n, X1 + 45056 + 1792 * i, [P, HALF]) for i, n in enumerate(("qsq", "qsum", "qx", "qr0", "qa")))
        xn1 = [at(f"xn1_{i}", X1 + 54016 + 2048 * i, [S, D]) for i in range(2)]
        qsum2, qsq2 = (at(n, X1 + 54016 + 1792 * i, [P, HALF]) for i, n in enumerate(("qsum2", "qsq2")))
        wq_raw = at("wq_raw", CT0 + 24576, [P, C, D])
        ob_sb = at("ob_sb", X1 + 69632, [S, D])
        pt_hi, pt_lo = zip(*(pair(f"pt{i}", X1 + 3584 * i, [P, R * S]) for i in range(3)))
        qs_hi = [at(f"qs{i}_hi", X1 + 62976 + 1792 * i, [P, R, S], F32R) for i in range(2)]
        qs_lo = [at(f"qs{i}_lo", 2496 + 448 * i, [P, S], F32R) for i in range(2)]
        qh = [at(f"qh{i}", 3392 + 448 * i, [P, S], F32R) for i in range(2)]
        nmax, psums, prec = (at(n, 4544 + 128 * i, [S, G, R, 2]) for i, n in enumerate(("nmax", "psums", "prec")))
        nmr = at("nmr", 4928, [S, B])
        wo_raw = at("wo_raw", QF0 + 28672, [P, C, D])
        prob = [at(f"prob{i}", QF0 + 36864 + 6016 * i, [S, R, KEYS]) for i in range(4)]
        wo_hi, wo_lo = pair("wo", QF0 + 60928, [P, C, D])
        ks_hi, ks_lo = zip(*(pair(f"ks{i}", X1 + 66560 + 3008 * i, [P, KEYS]) for i in range(2)))
        vs_hi, vs_lo = zip(*(pair(f"vs{i}", X1 + 72576 + 3072 * i, [P, 3, P]) for i in range(2)))
        xn2 = [at(f"xn2_{i}", KT0 + 43008 + 2048 * i, [S, D]) for i in range(2)]
        X0 = (end - base - 16384) // 32 * 32
        X = at("X", X0, [S, B, D])
        ot_hi, ot_lo = zip(*(pair(f"ot{i}", VV0 + 16384 + 3584 * i, [P, C, S]) for i in range(4)))
        r0 = QF0 + 77312
        zT = at("zT", X1, [E, NTOK])
        wr_hi, wr_lo = pair("wr", r0, [P, C, WRP])
        rank2 = at("rank2", r0 + 2304, [P, NT, E, E])
        z, inh, dist, zone, fb, rnk = (at(n, r0 + 4096 + 224 * i, [P, NT, E])
                                       for i, n in enumerate(("z", "inh", "dist", "zone", "fb", "rnk")))
        s1, s2 = (at(n, r0 + 5440 + 32 * i, [P, NT]) for i, n in enumerate(("s1", "s2")))
        xt_hi, xt_lo = pair("xt", KT0, [P, C, NTOK])
        acc = at("acc", KT0 + 28672, [P, NT, D])
        silu = [at(f"silu{i}", KT0 + 43008 + 2048 * i, [P, 4 * P]) for i in range(2)]
        wtok = at("wtok", KT0 + 47104, [P, NT, E])
        h_hi, h_lo = pair("h", QF0, [P, FC, NTOK])
        e_raw = [at(f"e_raw{i}", QF0 + 28672 + 8192 * i, [P, C, D]) for i in range(3)]
        eu, ed, eg = ([pair(f"{n}{i}", (VV0, QF0 + 53248)[i] + 16384 * k, [P, C, D]) for i in range(2)]
                      for k, n in enumerate(("eu", "ed", "eg")))
        hf = [at(f"hf{i}", QF0 + 102400 + 2048 * i, [P, 4 * P]) for i in range(2)]
        ps = ctx.enter_context(nc.psum_tensor("ps", [P, 8, 512], F32))

        (d_wk, d_x, d_small, d_attn, d_wq, d_ob, d_wo, d_acc, d_wr, d_out, d_vlast) = (
            sem(n) for n in ("d_wk", "d_x", "d_small", "d_attn", "d_wq", "d_ob", "d_wo", "d_acc", "d_wr", "d_out", "d_vlast"))
        d_txt = [sem(f"d_txt{t}") for t in range(2)]
        d_w = [sem(f"d_w{i}") for i in range(2)]
        d_ctx = [sem(f"d_ctx{i}") for i in range(2)]
        d_e = [sem(f"d_e{k}") for k in range(3)]
        const_ones = sem("const_ones")
        const_ident = sem("const_ident")
        const_sel = sem("const_sel")
        const_eye = sem("const_eye")
        turned_mean_mm = sem("turned_mean_mm")
        o8_hi_done = sem("o8_hi_done")
        o8_lo_done = sem("o8_lo_done")
        turned_mean_done = sem("turned_mean_done")
        wv_lo_done = sem("wv_lo_done")
        dve_own = sem("dve_own")
        pool_own = sem("pool_own")
        act_own = sem("act_own")
        wk_hi_done = sem("wk_hi_done")
        wk_lo_done = sem("wk_lo_done")
        txt_hi_done = sem("txt_hi_done")
        txt_lo_done = sem("txt_lo_done")
        k_mm = sem("k_mm")
        k_evac = sem("k_evac")
        ln0_var = sem("ln0_var")
        ln0_root = sem("ln0_root")
        ln0_done = sem("ln0_done")
        sums_mm = sem("sums_mm")
        mean_done = sem("mean_done")
        mean_v_mm = sem("mean_v_mm")
        mean_v_done = sem("mean_v_done")
        heads_mm = sem("heads_mm")
        heads_done = sem("heads_done")
        attn_mm = sem("attn_mm")
        attn_done = sem("attn_done")
        broadcast_mm = sem("broadcast_mm")
        x1_done = sem("x1_done")
        ln1_var = sem("ln1_var")
        ln1_root = sem("ln1_root")
        w_hi_done = sem("w_hi_done")
        w_lo_done = sem("w_lo_done")
        ctx_hi_done = sem("ctx_hi_done")
        ctx_lo_done = sem("ctx_lo_done")
        v_mm = sem("v_mm")
        v_evac = sem("v_evac")
        k_sum = sem("k_sum")
        k_square_mm = sem("k_square_mm")
        k_mean_done = sem("k_mean_done")
        k_root_done = sem("k_root_done")
        k_fin = sem("k_fin")
        vlast_mm = sem("vlast_mm")
        vlast_done = sem("vlast_done")
        wq_hi_done = sem("wq_hi_done")
        wq_lo_done = sem("wq_lo_done")
        xn1_done = sem("xn1_done")
        x1t_mm = sem("x1t_mm")
        xt1_hi_done = sem("xt1_hi_done")
        xt1_lo_done = sem("xt1_lo_done")
        q_mm = sem("q_mm")
        q_evac = sem("q_evac")
        q_sum = sem("q_sum")
        q_sum2 = sem("q_sum2")
        q_square_mm = sem("q_square_mm")
        q_mean_done = sem("q_mean_done")
        q_root_done = sem("q_root_done")
        q_fin = sem("q_fin")
        ob_done = sem("ob_done")
        qs_zero = sem("qs_zero")
        q_hi_done = sem("q_hi_done")
        k_hi_done = sem("k_hi_done")
        k_lo_done = sem("k_lo_done")
        q_lo_done = sem("q_lo_done")
        score_mm = sem("score_mm")
        max_done = sem("max_done")
        exp_done = sem("exp_done")
        rec_done = sem("rec_done")
        norm_done = sem("norm_done")
        turn_mm = sem("turn_mm")
        pt_hi_done = sem("pt_hi_done")
        pt_lo_done = sem("pt_lo_done")
        vs_hi_done = sem("vs_hi_done")
        vs_lo_done = sem("vs_lo_done")
        pv_mm = sem("pv_mm")
        diag_done = sem("diag_done")
        wo_hi_done = sem("wo_hi_done")
        wo_lo_done = sem("wo_lo_done")
        ot_hi_done = sem("ot_hi_done")
        ot_lo_done = sem("ot_lo_done")
        o_mm = sem("o_mm")
        x2_done = sem("x2_done")
        ln2_var = sem("ln2_var")
        ln2_root = sem("ln2_root")
        ln2_done = sem("ln2_done")
        xn2_done = sem("xn2_done")
        x2t_mm = sem("x2t_mm")
        xt_hi_done = sem("xt_hi_done")
        xt_lo_done = sem("xt_lo_done")
        wr_zero = sem("wr_zero")
        wr_hi_done = sem("wr_hi_done")
        wr_lo_done = sem("wr_lo_done")
        logit_mm = sem("logit_mm")
        logit_out = sem("logit_out")
        turned_logit_mm = sem("turned_logit_mm")
        router_act = sem("router_act")
        router_dve = sem("router_dve")
        e_hi_done = sem("e_hi_done")
        e_lo_done = sem("e_lo_done")
        gate_mm = sem("gate_mm")
        up_mm = sem("up_mm")
        silu_done = sem("silu_done")
        hf_done = sem("hf_done")
        h_hi_done = sem("h_hi_done")
        h_lo_done = sem("h_lo_done")
        down_mm = sem("down_mm")
        acc_done = sem("acc_done")

        ds = bass.ds

        def mm3(pe, o, wh, wl, xh, xl, first, last):
            pe.matmul(o, wh, xh, start=first, stop=False)
            pe.matmul(o, wh, xl, start=False, stop=False)
            return pe.matmul(o, wl, xh, start=False, stop=last)

        def f(t):
            return t.bitcast(F32)

        def pairs(eng, i_first, i_last, body):
            with eng.Fori(i_first, i_last) as i:
                for par in range(2):
                    body(2 * i + par, i, par)

        def unit_banks(e, part, c):
            if isinstance(e, int) and e == 0 and part == 0 and c >= 2:
                return (4, 5) if c == 2 else (6, 7)
            return c % 2, 2 + c % 2

        n_acc = 1 + sum(1 for i in range(1, NTOK) if i % S == 0 or i % P == 0)
        block = ctx.enter_context(nc.Block())

        @block.sync
        def _(sp):
            sp.dma_start(wk_raw[:], wkT).then_inc(d_wk, 16)
            sp.dma_start(txt_raw[0][:], ctx_txt[0]).then_inc(d_txt[0], 16)
            sp.dma_start(X[:], x.rearrange("b q d -> q b d")).then_inc(d_x, 16)
            sp.dma_start(col[:], cols).then_inc(d_small, 16)
            sp.dma_start(wr_raw[:], wr.rearrange("(c p) e -> p c e", p=P)).then_inc(d_wr, 16)
            sp.dma_start(txt_raw[1][:], ctx_txt[1]).then_inc(d_txt[1], 16)
            sp.dma_start(wvA[:], wkv.rearrange("(c p) n -> p c n", p=P)[:, :, P:2 * P]).then_inc(d_attn, 16)
            sp.dma_start(woA[:], wo_attn.rearrange("(g p) n -> p g n", p=P)).then_inc(d_attn, 16)
            sp.dma_start(o8[:], bo8).then_inc(d_attn, 16)
            sp.dma_start(w_slot[0][:], wkiT).then_inc(d_w[0], 16)
            sp.dma_start(w_slot[1][:], wvT).then_inc(d_w[1], 16)
            sp.wait_ge(w_lo_done, 1)
            sp.dma_start(w_slot[0][:], wviT).then_inc(d_w[0], 16)
            sp.wait_ge(wk_lo_done, 1)

            def load_ctx(b, i, par):
                if isinstance(b, int) and b == 1:
                    sp.wait_ge(heads_mm, 1)
                if due(b - 1):
                    sp.wait_ge(ctx_lo_done, b - 1)
                sp.dma_start(ctx_raw[par][:], ctxT[ds(b, 1)].rearrange("a p c n -> (a p) c n")).then_inc(d_ctx[par], 16)

            load_ctx(0, 0, 0)
            load_ctx(1, 0, 1)
            pairs(sp, 1, B // 2, load_ctx)
            sp.wait_ge(ctx_lo_done, B)
            sp.dma_start(last_raw[:], ctx_last).then_inc(d_ctx[0], 16)
            sp.dma_start(wq_raw[:], wqT).then_inc(d_wq, 16)
            sp.wait_ge(vlast_mm, 1)
            sp.dma_start(ob_sb[:], ob).then_inc(d_ob, 16)
            sp.wait_ge(vlast_done, 1)
            sp.wait_ge(v_evac, 3 * B)
            for b in range(B):
                sp.dma_start(VV[0:1, b, 2, :], vlast[b:b + 1, :]).then_inc(d_vlast, 16)
            sp.wait_ge(q_mm, 2 * C)
            sp.dma_start(wo_raw[:], woT).then_inc(d_wo, 16)
            sp.wait_ge(wo_lo_done, 1)

            def load_e(e, i, par):
                for k, w in enumerate((wg, wu, wd)):
                    if due(3 * e + k - 2):
                        sp.wait_ge(e_lo_done, 3 * e + k - 2)
                    if isinstance(e, int) and 3 * e + k == 1:
                        sp.wait_ge(turn_mm, 3 * B * G)
                    sp.dma_start(e_raw[k][:], w[ds(e, 1)].rearrange("a (c p) n -> p (a c) n", p=P)).then_inc(d_e[k], 16)

            load_e(0, 0, 0)
            flat = 0
            while flat < NTOK:
                b, s = divmod(flat, S)
                t, p = divmod(flat, P)
                n = min(S - s, P - p)
                if s == 0:
                    sp.wait_ge(x2_done, b + 1)
                sp.dma_start(acc[p:p + n, t, :], X[s:s + n, b, :]).then_inc(d_acc, 16)
                flat += n
            load_e(1, 0, 1)
            pairs(sp, 1, E // 2, load_e)
            for j in range(NT):
                if due(NT * (E - 1) + j + 1):
                    sp.wait_ge(acc_done, NT * (E - 1) + j + 1)
                sp.dma_start(out[j * P:(j + 1) * P, :], acc[:, j, :]).then_inc(d_out, 16)
            sp.wait_ge(d_out, 16 * NT)

        @block.tensor
        def _(pe):
            def ktxt(u):
                t, c = divmod(u, C)
                pe.wait_ge(wk_lo_done, 1)
                pe.wait_ge(txt_lo_done, t + 1)
                if due(u - 3):
                    pe.wait_ge(k_evac, u - 3)
                for k in range(C):
                    mm = mm3(pe, ps[:, c, 0:TXTN], wk_hi[:, k, c * P:(c + 1) * P], wk_lo[:, k, c * P:(c + 1) * P],
                             txt_hi[:, k, :], txt_lo[:, k, :], k == 0, k == C - 1)
                mm.then_inc(k_mm, 1)

            for u in range(4):
                ktxt(u)
            pe.wait_ge(ln0_done, 1)
            pe.wait_ge(const_ones, 1)
            for b in range(B):
                pe.matmul(ps[0:B, 4, :], rmask[:, b, :], X[:, b, :], start=(b == 0), stop=(b == B - 1))
            pe.matmul(ps[0:B, 5, 0:1], rm[:, :], ones[0:S, 0:1], start=True, stop=True).then_inc(sums_mm, 1)
            ktxt(4)
            pe.wait_ge(mean_done, 1)
            pe.wait_ge(const_ident, 2)
            for c in range(C):
                mm = pe.transpose(ps[:, 6, c * B:(c + 1) * B], mean8[:, c * P:(c + 1) * P], ident[0:B, 0:B])
            mm.then_inc(turned_mean_mm, 1)
            ktxt(5)
            pe.wait_ge(turned_mean_done, 1)
            pe.wait_ge(d_attn, 48)
            for c in range(C):
                mm = pe.matmul(ps[:, 5, 0:B], wvA[:, c, :], meanT[:, c, :], start=(c == 0), stop=(c == C - 1))
            mm.then_inc(mean_v_mm, 1)
            ktxt(6)
            pe.wait_ge(mean_v_done, 2)
            for g in range(G):
                mm = pe.matmul(ps[:, 6, g * B:(g + 1) * B], rep[:, g, :, :].rearrange("p r d -> p (r d)"), vT[:, :],
                               start=True, stop=True)
            mm.then_inc(heads_mm, 1)
            ktxt(7)
            pe.wait_ge(heads_done, 1)
            for g in range(G):
                mm = pe.matmul(ps[0:B, 7, :], vrep[:, g, :], woA[:, g, :], start=(g == 0), stop=(g == G - 1))
            mm.then_inc(attn_mm, 1)

            def broadcast(b):
                if due(b - 3):
                    pe.wait_ge(x1_done, b - 3)
                pe.matmul(ps[0:S, 4 + b % 4, :], sel[:, b, :], o8_hi[:, :], start=True, stop=False)
                pe.matmul(ps[0:S, 4 + b % 4, :], sel[:, b, :], o8_lo[:, :], start=False, stop=True).then_inc(broadcast_mm, 1)

            def sumsq(b):
                pe.wait_ge(k_sum, b + 1)
                if due(b):
                    pe.wait_ge(k_mean_done, b)
                pe.matmul(ps[:, 7, 0:KEYS], ones[:, :], ksum[:, :], start=True, stop=True).then_inc(k_square_mm, 1)

            def values(b, par, t, last=False):
                if due(3 * b + t - 2):
                    pe.wait_ge(v_evac, 3 * b + t - 2)
                wh, wl = (wv_hi, wv_lo) if t == 2 else (wvi_hi, wvi_lo)
                for k in range(C):
                    mm = mm3(pe, ps[:, 4 + t, :], ctx_hi[par][:, k, t * P:(t + 1) * P],
                             ctx_lo[par][:, k, t * P:(t + 1) * P], wh[:, k, :], wl[:, k, :], k == 0, k == C - 1)
                mm.then_inc(vlast_mm if last else v_mm, 1)

            def project(b, i, par, first=False):
                pe.wait_ge(ctx_lo_done, b + 1)
                for c in range(C):
                    pe.wait_ge(k_evac, 5 + 4 * b + c)
                    for k in range(C):
                        mm = mm3(pe, ps[:, c, 0:IMGP], wki_hi[:, k, c * P:(c + 1) * P], wki_lo[:, k, c * P:(c + 1) * P],
                                 ctx_hi[par][:, k, 0:IMGP], ctx_lo[par][:, k, 0:IMGP], k == 0, k == C - 1)
                    mm.then_inc(k_mm, 1)
                    if c == 0 and not first:
                        sumsq(b - 1)
                    if first:
                        if c == 0:
                            pe.wait_ge(o8_lo_done, 1)
                            pe.wait_ge(const_sel, 1)
                        broadcast(2 * c)
                        broadcast(2 * c + 1)
                if first:
                    pe.wait_ge(x1_done, B)
                for t in range(3):
                    values(b, par, t)

            pe.wait_ge(w_lo_done, 1)
            pe.wait_ge(wv_lo_done, 2)
            project(0, 0, 0, True)
            project(1, 0, 1)
            pairs(pe, 1, B // 2, project)
            pe.wait_ge(ctx_lo_done, B + 1)
            values(B, 0, 0, True)
            sumsq(B - 1)

            def transpose_x(b, src, bank, done, free, out_sem):
                pe.wait_ge(done, b + 1)
                if due(b - 1):
                    pe.wait_ge(free, b - 1)
                for c in range(C):
                    mm = pe.transpose(ps[:, bank, c * S:(c + 1) * S], src[b % 2][:, c * P:(c + 1) * P], ident[0:S, 0:S])
                mm.then_inc(out_sem, 1)

            pe.wait_ge(const_ident, 2)
            pe.wait_ge(k_evac, 8 + 4 * B)
            def qsumsq(h):
                pe.wait_ge(q_sum, h + 1)
                pe.wait_ge(q_evac, 4 * h + 1)
                mm = pe.matmul(ps[:, 2 + 2 * h, 0:HALF], ones[:, :], qsum[:, :], start=True, stop=(h == 0))
                if h == 1:
                    pe.wait_ge(q_sum2, 1)
                    mm = pe.matmul(ps[:, 4, 0:HALF], ones[:, :], qsum2[:, :], start=False, stop=True)
                mm.then_inc(q_square_mm, 1)

            for b in range(B // 2):
                transpose_x(b, xn1, b % 2, xn1_done, xt1_lo_done, x1t_mm)
            pe.wait_ge(wq_lo_done, 1)
            for u in range(2 * C):
                h, c = divmod(u, C)
                bank = 2 + 2 * h + c
                pe.wait_ge(xt1_lo_done, B // 2 * (h + 1))
                if u == 2:
                    pe.wait_ge(v_evac, 3 * B)
                    pe.wait_ge(vlast_done, 1)
                if bank == 7:
                    pe.wait_ge(k_mean_done, B)
                if h == 1 and c < 2:
                    pe.wait_ge(q_evac, 3 + c)
                for k in range(C):
                    mm = mm3(pe, ps[:, bank, 0:HALF], wq_hi[:, k, c * P:(c + 1) * P], wq_lo[:, k, c * P:(c + 1) * P],
                             xt1_hi[:, k, h * HALF:(h + 1) * HALF], xt1_lo[:, k, h * HALF:(h + 1) * HALF],
                             k == 0, k == C - 1)
                mm.then_inc(q_mm, 1)
                if h == 0:
                    transpose_x(B // 2 + c, xn1, c % 2, xn1_done, xt1_lo_done, x1t_mm)
                if u == C:
                    qsumsq(0)

            def scores(n, g, a):
                pe.wait_ge(k_hi_done, n + 1)
                pe.wait_ge(q_hi_done, 5 * n + 5)
                pe.wait_ge(k_lo_done, n + 1)
                pe.wait_ge(q_lo_done, n + 1)
                if due(8 * (n - 1) + 4 * a + 4):
                    pe.wait_ge(exp_done, 8 * (n - 1) + 4 * a + 4)
                s = g % 2
                for r in (2 * a, 2 * a + 1):
                    rows, o = slice(HD * r, HD * r + HD), ps[0:S, r, 0:KEYS]
                    pe.matmul(o, qs_hi[s][:, r, :], ks_hi[s][:, :], start=True, stop=False)
                    pe.matmul(o, qs_hi[s][:, r, :], ks_lo[s][:, :], start=False, stop=False)
                    mm = pe.matmul(o, qs_lo[s][rows, :], ks_hi[s][rows, :], start=False, stop=True)
                mm.then_inc(score_mm, 1)

            def turn(n, g, t):
                m = 3 * n + t
                pe.wait_ge(norm_done, 4 * n + 4)
                if due(m - 1):
                    pe.wait_ge(pt_lo_done, m - 1)
                k = TILE[t]
                for r in range(R):
                    mm = pe.transpose(ps[0:k, 4 + (g + t) % 2, r * S:(r + 1) * S], prob[g][:, r, t * P:t * P + k],
                                      ident[0:S, 0:S])
                mm.then_inc(turn_mm, 1)

            def pv(n, g, t):
                m = 3 * n + t
                pe.wait_ge(vs_lo_done, n + 1)
                pe.wait_ge(pt_lo_done, m + 1)
                if due(4 * (n - 1)):
                    pe.wait_ge(diag_done, 4 * (n - 1))
                k, v, p, o = TILE[t], g % 2, t, ps[:, 6 + g % 2, 0:R * S]
                mm = mm3(pe, o, vs_hi[v][0:k, t, :], vs_lo[v][0:k, t, :], pt_hi[p][0:k, :], pt_lo[p][0:k, :],
                         t == 0, t == 2)
                mm.then_inc(pv_mm, 1)

            def project_out(b):
                pe.wait_ge(ot_lo_done, b + 1)
                if due(b - 3):
                    pe.wait_ge(x2_done, b - 3)
                for k in range(C):
                    mm = mm3(pe, ps[0:S, b % 4, :], ot_hi[b % 4][:, k, :], ot_lo[b % 4][:, k, :],
                             wo_hi[:, k, :], wo_lo[:, k, :], k == 0, k == C - 1)
                mm.then_inc(o_mm, 1)

            def attend(b, first=False, last=False):
                for g in range(G):
                    n = 4 * b + g
                    for t in range(3):
                        turn(n, g, t)
                        if t < 2 and not (last and g + 2 >= G):
                            scores(n + 2, (g + 2) % G, t)
                        if not (first and 3 * g + t < 2):
                            back = (t - 2) // 3
                            pv(n + back, (g + back) % G, (t - 2) % 3)
                        if last and g == G - 1 and t > 0:
                            if t == 1:
                                pe.wait_ge(wo_lo_done, 1)
                                pe.wait_ge(exp_done, 8 * B * G)
                            project_out(t - 1)

            pe.wait_ge(q_mean_done, 1)
            for n in range(2):
                for a in range(2):
                    scores(n, n, a)
                if n == 0:
                    qsumsq(1)
            pe.wait_ge(q_mean_done, 2)
            pe.wait_ge(q_evac, 2 * C)
            attend(0, first=True)
            with pe.Fori(1, B - 1) as b:
                attend(b)
            attend(B - 1, last=True)
            pv(B * G - 1, G - 1, 1)
            project_out(2)
            pv(B * G - 1, G - 1, 2)
            project_out(3)

            def logits(h):
                pe.wait_ge(wr_lo_done, 1)
                pe.wait_ge(xt_lo_done, B // 2 * (h + 1))
                pe.wait_ge(diag_done, 4 * B * G)
                for k in range(C):
                    mm = mm3(pe, ps[0:WRP, 6 + h, 0:HALF], wr_hi[:, k, :], wr_lo[:, k, :],
                             xt_hi[:, k, h * HALF:(h + 1) * HALF], xt_lo[:, k, h * HALF:(h + 1) * HALF], k == 0, k == C - 1)
                mm.then_inc(logit_mm, 1)

            def gate_up(e, par, part, c):
                n = 8 * e + 4 * part + c
                t0, nt = PART[part]
                banks = unit_banks(e, part, c)
                if banks[0] == 6:
                    pe.wait_ge(router_dve, 1)
                if banks[0] < 4 and due(n - 1):
                    pe.wait_ge(hf_done, n - 1)
                for w, bank, done in ((eg, banks[0], gate_mm), (eu, banks[1], up_mm)):
                    for k in range(C):
                        mm = mm3(pe, ps[:, bank, 0:nt], w[par][0][:, k, c * P:(c + 1) * P], w[par][1][:, k, c * P:(c + 1) * P],
                                 xt_hi[:, k, t0:t0 + nt], xt_lo[:, k, t0:t0 + nt], k == 0, k == C - 1)
                    mm.then_inc(done, 1)

            for b in range(0, B, 2):
                if b + 4 < B:
                    project_out(b + 4)
                    project_out(b + 5)
                if b == B - 2:
                    logits(0)
                for i in (b, b + 1):
                    transpose_x(i, xn2, 4 + i % 2, xn2_done, xt_lo_done, x2t_mm)
            pe.wait_ge(x2_done, B)
            pe.wait_ge(e_lo_done, 2)
            pe.wait_ge(xt_lo_done, 5)
            gate_up(0, 0, 0, 0)
            logits(1)
            pe.wait_ge(logit_out, 2)
            for j in range(NT):
                mm = pe.transpose(ps[:, 6, j * E:(j + 1) * E], zT[:, j * P:(j + 1) * P], ident[0:E, 0:E])
            mm.then_inc(turned_logit_mm, 1)

            def down(e, par, part):
                pe.wait_ge(h_lo_done, 8 * e + 4 * part + 4)
                for j in range(4 * part, (4, NT)[part]):
                    d = NT * e + j
                    if due(d - 1):
                        pe.wait_ge(acc_done, d - 1)
                    for k in range(FC):
                        mm = mm3(pe, ps[:, 4 + (par + j) % 2, :], h_hi[:, k, j * P:(j + 1) * P], h_lo[:, k, j * P:(j + 1) * P],
                                 ed[par][0][:, k, :], ed[par][1][:, k, :], k == 0, k == FC - 1)
                    mm.then_inc(down_mm, 1)

            def expert(e, i, par, last=False):
                for c in range(1, FC):
                    gate_up(e, par, 0, c)
                gate_up(e, par, 1, 0)
                if last:
                    for c in range(1, FC):
                        gate_up(e, par, 1, c)
                pe.wait_ge(e_lo_done, 3 * e + 3)
                down(e, par, 0)
                if not last:
                    for c in range(1, FC):
                        gate_up(e, par, 1, c)
                    pe.wait_ge(e_lo_done, 3 * e + 5)
                    gate_up(e + 1, 1 - par, 0, 0)
                down(e, par, 1)

            for c in range(1, FC):
                gate_up(0, 0, 0, c)
            gate_up(0, 0, 1, 0)
            pe.wait_ge(e_lo_done, 3)
            down(0, 0, 0)
            for c in range(1, FC):
                gate_up(0, 0, 1, c)
            pe.wait_ge(e_lo_done, 5)
            gate_up(1, 1, 0, 0)
            down(0, 0, 1)
            expert(1, 0, 1)
            pairs(pe, 1, E // 2 - 1, expert)
            expert(E - 2, 0, 0)
            expert(E - 1, 0, 1, True)

        @block.scalar
        def _(act):
            own = Count()
            act.preload_act_table_set("natural_log_exp_and_others")

            def hi(o, i):
                return act.activation(o, i, ACT.Copy)

            def root(r, t):
                act.activation(r, t, ACT.Ln).then_inc(act_own, 1)
                act.wait_ge(act_own, own.next())
                return act.activation(r, r, ACT.Exp, scale=-0.5)

            act.wait_ge(d_wk, 16)
            hi(wk_hi[:], wk_raw[:]).then_inc(wk_hi_done, 1)
            act.wait_ge(d_txt[0], 16)
            hi(txt_hi[:], txt_raw[0][:]).then_inc(txt_hi_done, 1)

            def ktxt_out(u):
                t, c = divmod(u, C)
                act.wait_ge(k_mm, u + 1)
                act.activation(KT[:, c, t * TB:(t + 1) * TB, IMGP:KEYS],
                               ps[:, c, 0:TXTN].rearrange("p (b n) -> p b n", b=TB), ACT.Identity,
                               bias=col[:, KB + c:KB + c + 1]).then_inc(k_evac, 1)

            act.wait_ge(d_small, 16)
            act.wait_ge(ln0_var, 1)
            root(lnr0[:], lnx[:]).then_inc(ln0_root, 1)
            for u in range(3):
                ktxt_out(u)
            act.wait_ge(k_mm, 4)
            act.wait_ge(d_txt[1], 16)
            act.wait_ge(txt_lo_done, 1)
            hi(txt_hi[:], txt_raw[1][:]).then_inc(txt_hi_done, 1)
            ktxt_out(3)
            act.wait_ge(d_w[0], 16)
            hi(wki_hi[:], w_slot[0][:]).then_inc(w_hi_done, 1)
            act.wait_ge(d_w[1], 16)
            hi(wv_hi[:], w_slot[1][:]).then_inc(w_hi_done, 1)
            ktxt_out(4)
            ktxt_out(5)
            act.wait_ge(d_w[0], 32)
            hi(wvi_hi[:], w_slot[0][:]).then_inc(w_hi_done, 1)
            ktxt_out(6)

            def split_ctx(b, par, count, n=CKEYS):
                if due(count):
                    act.wait_ge(d_ctx[par], count)
                if due(3 * (b - 1)):
                    act.wait_ge(v_mm, 3 * (b - 1))
                elif b == 1:
                    act.wait_ge(attn_mm, 1)
                hi(ctx_hi[par][:, :, 0:n], (ctx_raw[par] if n == CKEYS else last_raw)[:]).then_inc(ctx_hi_done, 1)

            act.wait_ge(w_lo_done, 1)
            act.wait_ge(wv_lo_done, 2)
            split_ctx(0, 0, 16)
            act.wait_ge(attn_done, 1)
            hi(o8_hi[:], o8[:]).then_inc(o8_hi_done, 1)
            ktxt_out(7)

            def read_project(b, i, par, first=False, last=False):
                if last:
                    split_ctx(B, 0, 16 * (B // 2 + 1), P)
                else:
                    split_ctx(b + 1, 1 - par, 16 * (i + 1 + par))
                for c in range(C):
                    act.wait_ge(k_mm, 2 * C + C * b + c + 1)
                    act.activation(KT[:, c, ds(b, 1), 0:IMGP].rearrange("p a n -> p (a n)"), ps[:, c, 0:IMGP],
                                   ACT.Identity, bias=col[:, KIB + c:KIB + c + 1]).then_inc(k_evac, 1)
                if not first:
                    if due(b):
                        act.wait_ge(k_mean_done, b)
                    act.activation(kr0[:], kx[:], ACT.Ln).then_inc(act_own, 1)
                    act.wait_ge(act_own, own.next())
                    act.activation(kr0[:], kr0[:], ACT.Exp, scale=-0.5).then_inc(k_root_done, 1)
                for t in range(3):
                    act.wait_ge(v_mm, 3 * b + t + 1)
                    act.activation(VV[:, ds(b, 1), t, :].rearrange("p a n -> p (a n)"), ps[:, 4 + t, :],
                                   ACT.Copy).then_inc(v_evac, 1)

            read_project(0, 0, 0, True)
            act.wait_ge(ln1_var, 1)
            root(lnr0[:], lnx[:]).then_inc(ln1_root, 1)
            read_project(1, 0, 1)
            with act.Fori(1, B // 2 - 1) as i:
                own.enter(i, 1, 2)
                for par in range(2):
                    read_project(2 * i + par, i, par)
            own.leave(B // 2 - 2)
            read_project(B - 2, B // 2 - 1, 0)
            read_project(B - 1, B // 2 - 1, 1, last=True)
            act.wait_ge(vlast_mm, 1)
            act.activation(vlast[:], ps[0:B, 4, :], ACT.Copy).then_inc(vlast_done, 1)

            def stage_k(b, g):
                n = 4 * b + g
                if due(2 * n - 2):
                    act.wait_ge(score_mm, 2 * n - 2)
                act.activation(ks_hi[g % 2][:, :], KT[:, g, ds(b, 1), :].rearrange("p a n -> p (a n)"),
                               ACT.Copy).then_inc(k_hi_done, 1)

            act.wait_ge(d_wq, 16)
            hi(wq_hi[:], wq_raw[:]).then_inc(wq_hi_done, 1)

            def xt1_hi_part(b):
                act.wait_ge(x1t_mm, b + 1)
                hi(xt1_hi[:, :, b * S:(b + 1) * S], ps[:, b % 2, 0:C * S].rearrange("p (c n) -> p c n", c=C))\
                    .then_inc(xt1_hi_done, 1)

            for b in range(B // 2):
                xt1_hi_part(b)
            act.wait_ge(k_mean_done, B)
            root(kr0[:], kx[:]).then_inc(k_root_done, 1)
            for u in range(2 * C):
                h, c = divmod(u, C)
                act.wait_ge(q_mm, u + 1)
                act.activation(QF[:, c, h * HALF:(h + 1) * HALF], ps[:, 2 + 2 * h + c, 0:HALF], ACT.Identity,
                               bias=col[:, QB + c:QB + c + 1]).then_inc(q_evac, 1)
                if h == 0:
                    xt1_hi_part(B // 2 + c)
                if u == C:
                    act.wait_ge(q_mean_done, 1)
                    root(qr0[:], qx[:]).then_inc(q_root_done, 1)
                if u == C + 1:
                    act.wait_ge(k_fin, 8 * B)
                    act.wait_ge(ob_done, B)
                if C < u < C + 3:
                    stage_k(0, u - C - 1)

            def stage_v(b, g):
                n = 4 * b + g
                if due(3 * n - 3):
                    act.wait_ge(pv_mm, 3 * n - 3)
                act.activation(vs_hi[g % 2][:, :, :],
                               VV[:, ds(b, 1), :, g * P:(g + 1) * P].rearrange("p a t n -> p (a t) n"),
                               ACT.Copy).then_inc(vs_hi_done, 1)

            def exps(n, g, a):
                act.wait_ge(max_done, 4 * n + 2 * a + 2)
                if due(3 * n - 9):
                    act.wait_ge(turn_mm, 3 * n - 9)
                for r in (2 * a, 2 * a + 1):
                    for kind, (k0, k1) in enumerate(((0, IMG), (IMGP, KEYS))):
                        act.activation(prob[g][:, r, k0:k1], ps[0:S, r, k0:k1], ACT.Exp, bias=nmax[:, g, r, kind:kind + 1],
                                       accum_out=psums[:, g, r, kind:kind + 1]).then_inc(exp_done, 1)

            def pt_hi_part(n, g, t):
                m, k = 3 * n + t, TILE[t]
                act.wait_ge(turn_mm, m + 1)
                if due(m - 2):
                    act.wait_ge(pv_mm, m - 2)
                hi(pt_hi[t][0:k, :], ps[0:k, 4 + (g + t) % 2, 0:R * S]).then_inc(pt_hi_done, 1)

            def split_o(b):
                if due(b - 3):
                    act.wait_ge(o_mm, b - 3)
                act.wait_ge(diag_done, 16 * (b + 1))
                hi(ot_hi[b % 4][:, :, :], QF[:, :, b * S:(b + 1) * S]).then_inc(ot_hi_done, 1)

            def x2_norm(c):
                act.wait_ge(ln2_var, c // 2 + 1)
                root(lnr0[:, c:c + 2], lnx[:, c:c + 2]).then_inc(ln2_root, 1)
                act.wait_ge(ln2_done, c // 2 + 1)
                for i in (c, c + 1):
                    if due(i - 1):
                        act.wait_ge(x2t_mm, i - 1)
                    act.activation(xn2[i % 2][:], X[:, i, :], ACT.Identity, bias=nmr[:, i:i + 1],
                                   scale=rstd[:, i:i + 1]).then_inc(xn2_done, 1)

            def attend(b, first=False, last=False):
                for g in range(G):
                    n = 4 * b + g
                    pt_hi_part(n, g, 0)
                    stage_v(b, g)
                    if not last or g + 3 < G:
                        stage_k(b + (g + 3) // G, (g + 3) % G)
                    pt_hi_part(n, g, 1)
                    if first and g == 0:
                        act.wait_ge(d_wo, 16)
                        act.wait_ge(q_fin, 2 * C)
                        hi(wo_hi[:], wo_raw[:]).then_inc(wo_hi_done, 1)
                    if not last or g + 2 < G:
                        exps(n + 2, (g + 2) % G, 0)
                    pt_hi_part(n, g, 2)
                    if not last or g + 2 < G:
                        exps(n + 2, (g + 2) % G, 1)
                    if last and g >= 2:
                        split_o(2 * g - 4)
                        split_o(2 * g - 3)

            act.wait_ge(d_vlast, 16 * B)
            act.wait_ge(q_sum2, 1)
            act.wait_ge(q_sum, 2)
            for n in range(2):
                for a in range(2):
                    exps(n, n, a)
                if n == 0:
                    act.wait_ge(q_mean_done, 2)
                    root(qr0[:], qx[:]).then_inc(q_root_done, 1)
                    stage_k(0, 2)
            act.wait_ge(q_fin, 8)
            attend(0, first=True)
            with act.Fori(1, B - 1) as b:
                attend(b)
            attend(B - 1, last=True)

            def split_e(e, par, k, count):
                if due(count):
                    act.wait_ge(d_e[k], count)
                w = (eg, eu, ed)[k]
                act.activation(w[par][0][:], e_raw[k][:], ACT.Copy).then_inc(e_hi_done, 1)

            for b in range(0, B + 4, 2):
                if b >= 4:
                    for c in (b - 4, b - 3):
                        act.wait_ge(x2t_mm, c + 1)
                        hi(xt_hi[:, :, c * S:(c + 1) * S], ps[:, 4 + c % 2, 0:C * S].rearrange("p (c n) -> p c n", c=C))\
                            .then_inc(xt_hi_done, 1)
                if b + 4 < B:
                    split_o(b + 4)
                    split_o(b + 5)
                if b < B:
                    x2_norm(b)
                if b in (0, 2, 6):
                    split_e(0, 0, (0, 2, 6).index(b), 16)
                if b == 4:
                    act.wait_ge(wr_zero, 1)
                    act.wait_ge(d_wr, 16)
                    hi(wr_hi[:, :, 0:E], wr_raw[:, :, :]).then_inc(wr_hi_done, 1)
                if b == B:
                    act.wait_ge(logit_mm, 1)
                    act.activation(zT[:, 0:HALF], ps[0:E, 6, 0:HALF], ACT.Copy).then_inc(logit_out, 1)

            act.wait_ge(logit_mm, 2)
            act.activation(zT[:, HALF:NTOK], ps[0:E, 7, 0:HALF], ACT.Copy).then_inc(logit_out, 1)
            act.wait_ge(router_dve, 1)
            act.activation(inh[:], z[:], ACT.Exp, scale=-1.0).then_inc(router_act, 1)
            act.wait_ge(router_dve, 2)
            act.activation(zone[:], dist[:], ACT.Exp, scale=-1.0 / 0.1).then_inc(router_act, 1)
            act.activation(fb[:], dist[:], ACT.Exp, scale=-1.0 / 0.3).then_inc(router_act, 1)

            def gate_up(e, part, c):
                n = 8 * e + 4 * part + c
                t0, nt = PART[part]
                act.wait_ge(gate_mm, n + 1)
                if due(n - 1):
                    act.wait_ge(hf_done, n - 1)
                act.activation(silu[c % 2][:, 0:nt], ps[:, unit_banks(e, part, c)[0], 0:nt], ACT.Silu).then_inc(silu_done, 1)
                act.wait_ge(hf_done, n + 1)
                if due(NT * e - 3 if part == 0 else NT * e):
                    act.wait_ge(down_mm, NT * e - 3 if part == 0 else NT * e)
                hi(h_hi[:, c, t0:t0 + nt], hf[c % 2][:, 0:nt]).then_inc(h_hi_done, 1)

            def expert(e, i, par, last=False):
                for c in range(1, FC):
                    gate_up(e, 0, c)
                    if not last:
                        if due(NT * e):
                            act.wait_ge(down_mm, NT * e)
                        split_e(e + 1, 1 - par, c - 1, 16 * (e + 2))
                for c in range(FC):
                    gate_up(e, 1, c)
                if not last:
                    gate_up(e + 1, 0, 0)

            act.wait_ge(d_acc, 16 * n_acc)
            act.wait_ge(xt_lo_done, B)
            gate_up(0, 0, 0)
            expert(0, 0, 0)
            expert(1, 0, 1)
            pairs(act, 1, E // 2 - 1, expert)
            expert(E - 2, 0, 0)
            expert(E - 1, 0, 1, True)

        @block.vector
        def _(dve):
            own = Count()

            def lo(o, i, hi_):
                return dve.tensor_tensor(o, i, f(hi_), ALU.subtract)

            def refine(r, r0_, a, x_):
                dve.tensor_tensor(a, r0_, r0_, ALU.mult).then_inc(dve_own, 1)
                dve.wait_ge(dve_own, own.next())
                dve.scalar_tensor_tensor(a, a, -0.5, x_, ALU.mult, ALU.mult).then_inc(dve_own, 1)
                dve.wait_ge(dve_own, own.next())
                return dve.scalar_tensor_tensor(r, a, 1.5, r0_, ALU.add, ALU.mult)

            def ln_sums(bs):
                for b in bs:
                    ins = dve.bn_stats(stats[:, b, :], X[:, b, :])
                ins.then_inc(dve_own, 1)
                dve.wait_ge(dve_own, own.next())
                for b in bs:
                    ins = dve.bn_aggr(mv[:, b, :], stats[:, b, :])
                ins.then_inc(dve_own, 1)
                dve.wait_ge(dve_own, own.next())

            dve.memset(ones[:], 1.0).then_inc(const_ones, 1)
            dve.wait_ge(wk_hi_done, 1)
            lo(wk_lo[:], wk_raw[:], wk_hi[:]).then_inc(wk_lo_done, 1)
            dve.wait_ge(txt_hi_done, 1)
            lo(txt_lo[:], txt_raw[0][:], txt_hi[:]).then_inc(txt_lo_done, 1)

            dve.wait_ge(d_x, 16)
            ln_sums(range(B))
            dve.tensor_scalar(lnx[:], mv[:, :, 1], LN_EPS, None, ALU.add).then_inc(ln0_var, 1)
            dve.wait_ge(ln0_root, 1)
            refine(rstd[:], lnr0[:], lna[:], lnx[:]).then_inc(dve_own, 1)
            dve.wait_ge(dve_own, own.next())
            dve.tensor_tensor(rm[:], rstd[:], mv[:, :, 0], ALU.mult).then_inc(dve_own, 1)
            dve.wait_ge(dve_own, own.next())
            dve.wait_ge(const_eye, 1)
            dve.tensor_tensor(rmask[:], eye8[:], rstd[:].unsqueeze(1).to_broadcast([S, B, B]), ALU.mult).then_inc(ln0_done, 1)
            dve.wait_ge(k_mm, 4)
            dve.wait_ge(txt_hi_done, 2)
            lo(txt_lo[:], txt_raw[1][:], txt_hi[:]).then_inc(txt_lo_done, 1)
            dve.wait_ge(w_hi_done, 1)
            lo(wki_lo[:], w_slot[0][:], wki_hi[:]).then_inc(w_lo_done, 1)
            dve.wait_ge(d_small, 16)
            dve.tensor_scalar(qscale[:], col[:, NQ:NQ + C], float(HD) ** -0.5, None, ALU.mult).then_inc(dve_own, 1)
            dve.wait_ge(dve_own, own.next())
            dve.tensor_tensor(vbsum[:], col[:, VB:VB + C], col[:, VIB:VIB + C], ALU.add).then_inc(dve_own, 1)
            dve.wait_ge(dve_own, own.next())
            dve.wait_ge(const_ident, 2)
            dve.tensor_copy(rep[:], ident[:].rearrange("p (g d) -> p g d", g=G).unsqueeze(2).to_broadcast([P, G, R, HD]))\
               .then_inc(mean_v_done, 1)
            dve.wait_ge(sums_mm, 1)
            dve.tensor_copy(mcorr[:], ps[0:B, 5, 0:1]).then_inc(dve_own, 1)
            dve.wait_ge(dve_own, own.next())
            dve.tensor_scalar(mean8[:], ps[0:B, 4, :], mcorr[:, 0:1], 1.0 / S, ALU.subtract, ALU.mult).then_inc(mean_done, 1)
            dve.wait_ge(turned_mean_mm, 1)
            dve.tensor_copy(meanT[:], ps[:, 6, 0:C * B].rearrange("p (c b) -> p c b", c=C)).then_inc(turned_mean_done, 1)
            dve.wait_ge(mean_v_mm, 1)
            dve.tensor_copy(vT[:], ps[:, 5, 0:B]).then_inc(mean_v_done, 1)
            dve.wait_ge(heads_mm, 1)
            dve.tensor_copy(vrep[:].rearrange("p g b -> p (g b)"), ps[:, 6, 0:G * B]).then_inc(heads_done, 1)
            dve.wait_ge(ctx_hi_done, 1)
            lo(ctx_lo[0][:], ctx_raw[0][:], ctx_hi[0][:]).then_inc(ctx_lo_done, 1)
            dve.wait_ge(attn_mm, 1)
            dve.tensor_tensor(o8[:], ps[0:B, 7, :], o8[:], ALU.add).then_inc(attn_done, 1)
            dve.wait_ge(attn_done, 1)
            dve.wait_ge(o8_hi_done, 1)
            lo(o8_lo[:], o8[:], o8_hi[:]).then_inc(o8_lo_done, 1)
            for b in range(B):
                dve.wait_ge(broadcast_mm, b + 1)
                dve.tensor_tensor(X[:, b, :], ps[0:S, 4 + b % 4, :], X[:, b, :], ALU.add).then_inc(x1_done, 1)
            def key_norm(b):
                dve.wait_ge(k_square_mm, b + 1)
                if due(b):
                    dve.wait_ge(k_root_done, b)
                dve.tensor_scalar(kx[:], ps[:, 7, 0:KEYS], 1.0 / D, RMS_EPS, ALU.mult, ALU.add).then_inc(k_mean_done, 1)
                dve.wait_ge(k_root_done, b + 1)
                refine(ka[:], kr0[:], ka[:], kx[:]).then_inc(dve_own, 1)
                dve.wait_ge(dve_own, own.next())
                for c in range(C):
                    for k0, k1, w in ((0, IMGP, NKI), (IMGP, KEYS, NK)):
                        kt = KT[:, c, ds(b, 1), k0:k1].rearrange("p a n -> p (a n)")
                        dve.scalar_tensor_tensor(kt, kt, col[:, w + c:w + c + 1], ka[:, k0:k1], ALU.mult, ALU.mult)\
                           .then_inc(k_fin, 1)

            def project(b, i, par, first=False, last=False):
                n = P if last else CKEYS
                dve.wait_ge(ctx_hi_done, b + 2)
                lo(ctx_lo[1 - par][:, :, 0:n], (last_raw if last else ctx_raw[1 - par])[:], ctx_hi[1 - par][:, :, 0:n])\
                    .then_inc(ctx_lo_done, 1)
                if not first:
                    if due(8 * (b - 1)):
                        dve.wait_ge(k_fin, 8 * (b - 1))
                    key_norm(b - 1)

            project(0, 0, 0, True)
            dve.wait_ge(x1_done, B)
            ln_sums(range(B))
            dve.tensor_scalar(lnx[:], mv[:, :, 1], LN_EPS, None, ALU.add).then_inc(ln1_var, 1)
            project(1, 0, 1)
            dve.wait_ge(ln1_root, 1)
            refine(rstd[:], lnr0[:], lna[:], lnx[:]).then_inc(dve_own, 1)
            dve.wait_ge(dve_own, own.next())
            with dve.Fori(1, B // 2 - 1) as i:
                own.enter(i, 1, 6)
                for par in range(2):
                    project(2 * i + par, i, par)
            own.leave(B // 2 - 2)
            project(B - 2, B // 2 - 1, 0)
            project(B - 1, B // 2 - 1, 1, last=True)
            def x1_norm(b):
                if due(b - 1):
                    dve.wait_ge(x1t_mm, b - 1)
                dve.tensor_scalar(xn1[b % 2][:], X[:, b, :], mv[:, b, 0:1], rstd[:, b:b + 1], ALU.subtract, ALU.mult)\
                   .then_inc(xn1_done, 1)

            def xt1_lo_part(b):
                dve.wait_ge(xt1_hi_done, b + 1)
                lo(xt1_lo[:, :, b * S:(b + 1) * S], ps[:, b % 2, 0:C * S].rearrange("p (c n) -> p c n", c=C),
                   xt1_hi[:, :, b * S:(b + 1) * S]).then_inc(xt1_lo_done, 1)

            dve.wait_ge(vlast_mm, 1)
            x1_norm(0)
            x1_norm(1)
            dve.wait_ge(wq_hi_done, 1)
            lo(wq_lo[:], wq_raw[:], wq_hi[:]).then_inc(wq_lo_done, 1)
            for b in range(B):
                xt1_lo_part(b)
                if b + 2 < B:
                    x1_norm(b + 2)
                if b == 3:
                    dve.wait_ge(k_fin, 8 * (B - 1))
                    key_norm(B - 1)

            def q_norm(h):
                dve.wait_ge(q_root_done, h + 1)
                refine(qa[:], qr0[:], qa[:], qx[:]).then_inc(dve_own, 1)
                dve.wait_ge(dve_own, own.next())
                for c in range(C):
                    qf = QF[:, c, h * HALF:(h + 1) * HALF]
                    dve.scalar_tensor_tensor(qf, qf, qscale[:, c:c + 1], qa[:], ALU.mult, ALU.mult).then_inc(q_fin, 1)

            def q_mean(h):
                dve.wait_ge(q_square_mm, h + 1)
                dve.tensor_scalar(qx[:], ps[:, 2 + 2 * h, 0:HALF], 1.0 / D, RMS_EPS, ALU.mult, ALU.add).then_inc(q_mean_done, 1)

            def split_q(b, g):
                n = 4 * b + g
                if due(2 * n - 2):
                    dve.wait_ge(score_mm, 2 * n - 2)
                q_ = QF[:, g, ds(b * S, S)]
                dve.tensor_copy(qh[g % 2][:, :], q_).then_inc(q_hi_done, 1)
                for r in range(R):
                    rows = slice(HD * r, HD * r + HD)
                    dve.tensor_copy(qs_hi[g % 2][rows, r, :], QF[rows, g, ds(b * S, S)]).then_inc(q_hi_done, 1)
                dve.wait_ge(q_hi_done, 5 * n + 1)
                lo(qs_lo[g % 2][:, :], q_, qh[g % 2][:, :]).then_inc(q_lo_done, 1)

            q_mean(0)
            q_norm(0)
            dve.wait_ge(q_evac, 2 * C - 1)
            dve.tensor_tensor(qsum2[:], QF[:, C - 2, HALF:NTOK], QF[:, C - 2, HALF:NTOK], ALU.mult).then_inc(dve_own, 1)
            dve.wait_ge(d_vlast, 16 * B)
            dve.wait_ge(qs_zero, 2)
            dve.wait_ge(q_fin, C)
            split_q(0, 0)
            dve.wait_ge(q_evac, 2 * C)
            dve.tensor_tensor(qsq2[:], QF[:, C - 1, HALF:NTOK], QF[:, C - 1, HALF:NTOK], ALU.mult).then_inc(dve_own, 1)
            own.next()
            dve.wait_ge(dve_own, own.next())
            dve.tensor_tensor(qsum2[:], qsum2[:], qsq2[:], ALU.add).then_inc(q_sum2, 1)

            def maxima(n, g, a):
                dve.wait_ge(score_mm, 2 * n + a + 1)
                for kind, (k0, k1) in enumerate(((0, IMG), (IMGP, KEYS))):
                    dve.tensor_reduce(nmax[:, g, 2 * a:2 * a + 2, kind], ps[0:S, 2 * a:2 * a + 2, k0:k1], AX.X, ALU.max,
                                      negate=True).then_inc(max_done, 1)

            def reciprocals(n, g, a):
                dve.wait_ge(exp_done, 8 * n + 4 * a + 4)
                dve.reciprocal(prec[:, g, 2 * a:2 * a + 2, :], psums[:, g, 2 * a:2 * a + 2, :]).then_inc(rec_done, 1)

            def pt_lo_part(n, g, t):
                m, k, s = 3 * n + t, TILE[t], (g + t) % 2
                dve.wait_ge(pt_hi_done, m + 1)
                lo(pt_lo[t][0:k, :], ps[0:k, 4 + s, 0:R * S], pt_hi[t][0:k, :]).then_inc(pt_lo_done, 1)

            def diagonal(b, g):
                n = 4 * b + g
                dve.wait_ge(pv_mm, 3 * n + 3)
                for r in range(R):
                    rows = slice(HD * r, HD * r + HD)
                    dve.tensor_scalar(QF[rows, g, ds(b * S, S)], ps[rows, 6 + g % 2, r * S:(r + 1) * S], vbsum[rows, g:g + 1],
                                      None, ALU.add).then_inc(diag_done, 1)

            def x2_sums(c):
                for i in (c, c + 1):
                    dve.wait_ge(o_mm, i + 1)
                    dve.tensor_tensor(X[:, i, :], ps[0:S, i % 4, :], X[:, i, :], ALU.add).then_inc(x2_done, 1)
                dve.wait_ge(x2_done, c + 2)
                ln_sums((c, c + 1))
                dve.tensor_scalar(lnx[:, c:c + 2], mv[:, c:c + 2, 1], LN_EPS, None, ALU.add).then_inc(ln2_var, 1)

            def x2_rstd(c):
                b = c + 2
                dve.wait_ge(ln2_root, b // 2)
                refine(rstd[:, c:b], lnr0[:, c:b], lna[:, c:b], lnx[:, c:b]).then_inc(dve_own, 1)
                dve.wait_ge(dve_own, own.next())
                dve.scalar_tensor_tensor(nmr[:, c:b], mv[:, c:b, 0], -1.0, rstd[:, c:b], ALU.mult, ALU.mult)\
                   .then_inc(ln2_done, 1)

            def attend(b, first=False, last=False):
                for g in range(G):
                    n = 4 * b + g
                    if not last or g + 1 < G:
                        reciprocals(n + 1, (g + 1) % G, 1)
                    if not last or g + 2 < G:
                        maxima(n + 2, (g + 2) % G, 0)
                    pt_lo_part(n, g, 0)
                    if last and g == 2:
                        dve.wait_ge(wo_hi_done, 1)
                        lo(wo_lo[:], wo_raw[:], wo_hi[:]).then_inc(wo_lo_done, 1)
                    pt_lo_part(n, g, 1)
                    if not last or g + 2 < G:
                        maxima(n + 2, (g + 2) % G, 1)
                    if not last or g + 3 < G:
                        split_q(b + (g + 3) // G, (g + 3) % G)
                    pt_lo_part(n, g, 2)
                    if not last or g + 2 < G:
                        reciprocals(n + 2, (g + 2) % G, 0)
                    if not (first and g == 0):
                        diagonal(b - (g == 0), (g - 1) % G)

            split_q(0, 1)
            for a in range(2):
                maxima(0, 0, a)
            q_mean(1)
            reciprocals(0, 0, 0)
            reciprocals(0, 0, 1)
            for a in range(2):
                maxima(1, 1, a)
            split_q(0, 2)
            reciprocals(1, 1, 0)
            q_norm(1)
            dve.wait_ge(q_fin, 2 * C)
            attend(0, first=True)
            with dve.Fori(1, B - 1) as b:
                attend(b)
            attend(B - 1, last=True)
            dve.wait_ge(score_mm, 2 * B * G)
            dve.memset(f(wr_hi[:]), 0.0).then_inc(dve_own, 1)
            dve.wait_ge(dve_own, own.next())
            dve.memset(f(wr_lo[:]), 0.0).then_inc(wr_zero, 1)
            x2_sums(0)
            diagonal(B - 1, 3)
            x2_rstd(0)

            for b in range(2, B + 4, 2):
                if b < B:
                    x2_sums(b)
                if b >= 4:
                    for t in (b - 4, b - 3):
                        dve.wait_ge(xt_hi_done, t + 1)
                        lo(xt_lo[:, :, t * S:(t + 1) * S], ps[:, 4 + t % 2, 0:C * S].rearrange("p (c n) -> p c n", c=C),
                           xt_hi[:, :, t * S:(t + 1) * S]).then_inc(xt_lo_done, 1)
                if b == B - 2:
                    dve.wait_ge(wr_hi_done, 1)
                    dve.wait_ge(wr_zero, 1)
                    lo(wr_lo[:, :, 0:E], wr_raw[:, :, :], wr_hi[:, :, 0:E]).then_inc(wr_lo_done, 1)
                if b < B:
                    x2_rstd(b)

            itemp = s2[:, 0:1]
            dve.reciprocal(itemp, col[:, TEMP:TEMP + 1]).then_inc(dve_own, 1)
            dve.wait_ge(dve_own, own.next())
            dve.wait_ge(turned_logit_mm, 1)
            dve.tensor_scalar(z[:].rearrange("p t e -> p (t e)"), ps[:, 6, 0:NT * E], itemp, None, ALU.mult).then_inc(router_dve, 1)
            dve.wait_ge(router_act, 1)
            dve.tensor_scalar(inh[:], inh[:], 1.0, None, ALU.add).then_inc(dve_own, 1)
            dve.wait_ge(dve_own, own.next())
            dve.reciprocal(inh[:], inh[:]).then_inc(dve_own, 1)
            dve.wait_ge(dve_own, own.next())
            dve.tensor_scalar(dist[:], inh[:], -ZONE_MID, None, ALU.add).then_inc(dve_own, 1)
            dve.wait_ge(dve_own, own.next())
            dve.tensor_scalar(rnk[:], dist[:], -1.0, None, ALU.mult).then_inc(dve_own, 1)
            dve.wait_ge(dve_own, own.next())
            dve.tensor_tensor(dist[:], dist[:], rnk[:], ALU.max).then_inc(router_dve, 1)
            dve.wait_ge(router_dve, 2)
            dve.tensor_scalar(rnk[:], inh[:], ZONE_LO, None, ALU.is_ge).then_inc(dve_own, 1)
            dve.wait_ge(dve_own, own.next())
            dve.scalar_tensor_tensor(rnk[:], inh[:], ZONE_HI, rnk[:], ALU.is_le, ALU.mult).then_inc(dve_own, 1)
            dve.wait_ge(dve_own, own.next())
            dve.wait_ge(router_act, 3)
            dve.tensor_tensor(wtok[:], zone[:], rnk[:], ALU.mult).then_inc(dve_own, 1)
            dve.wait_ge(dve_own, own.next())
            dve.tensor_reduce(s1[:], wtok[:], AX.X, ALU.add).then_inc(dve_own, 1)
            dve.wait_ge(dve_own, own.next())
            dve.tensor_scalar(s1[:], s1[:], 1e-8, None, ALU.is_lt).then_inc(dve_own, 1)
            dve.wait_ge(dve_own, own.next())
            fb_e = fb[:].unsqueeze(3).to_broadcast([P, NT, E, E])
            fb_j = fb[:].unsqueeze(2).to_broadcast([P, NT, E, E])
            dve.tensor_tensor(rank2[:], fb_j, fb_e, ALU.is_gt).then_inc(dve_own, 1)
            dve.wait_ge(dve_own, own.next())
            dve.tensor_reduce(rnk[:], rank2[:], AX.X, ALU.add).then_inc(dve_own, 1)
            dve.wait_ge(dve_own, own.next())
            dve.tensor_tensor(rank2[:], fb_j, fb_e, ALU.is_equal).then_inc(dve_own, 1)
            dve.wait_ge(dve_own, own.next())
            dve.wait_ge(const_ident, 3)
            dve.tensor_tensor(rank2[:], rank2[:], tril[:].unsqueeze(1).to_broadcast([P, NT, E, E]), ALU.mult).then_inc(dve_own, 1)
            dve.wait_ge(dve_own, own.next())
            dve.tensor_reduce(inh[:], rank2[:], AX.X, ALU.add).then_inc(dve_own, 1)
            dve.wait_ge(dve_own, own.next())
            dve.tensor_tensor(rnk[:], rnk[:], inh[:], ALU.add).then_inc(dve_own, 1)
            dve.wait_ge(dve_own, own.next())
            dve.scalar_tensor_tensor(fb[:], rnk[:], 1.5, fb[:], ALU.is_lt, ALU.mult).then_inc(dve_own, 1)
            dve.wait_ge(dve_own, own.next())

            def over_sum(t):
                dve.tensor_reduce(s2[:], t[:], AX.X, ALU.add).then_inc(dve_own, 1)
                dve.wait_ge(dve_own, own.next())
                dve.tensor_scalar(s2[:], s2[:], 1e-8, None, ALU.max).then_inc(dve_own, 1)
                dve.wait_ge(dve_own, own.next())
                dve.reciprocal(s2[:], s2[:]).then_inc(dve_own, 1)
                dve.wait_ge(dve_own, own.next())
                dve.tensor_tensor(t[:], t[:], s2[:].unsqueeze(2).to_broadcast([P, NT, E]), ALU.mult).then_inc(dve_own, 1)
                dve.wait_ge(dve_own, own.next())

            over_sum(fb)
            dve.tensor_tensor(fb[:], fb[:], s1[:].unsqueeze(2).to_broadcast([P, NT, E]), ALU.mult).then_inc(dve_own, 1)
            dve.wait_ge(dve_own, own.next())
            dve.tensor_scalar(s1[:], s1[:], -1.0, 1.0, ALU.mult, ALU.add).then_inc(dve_own, 1)
            dve.wait_ge(dve_own, own.next())
            dve.tensor_tensor(wtok[:], wtok[:], s1[:].unsqueeze(2).to_broadcast([P, NT, E]), ALU.mult).then_inc(dve_own, 1)
            dve.wait_ge(dve_own, own.next())
            dve.tensor_tensor(wtok[:], wtok[:], fb[:], ALU.add).then_inc(dve_own, 1)
            dve.wait_ge(dve_own, own.next())
            over_sum(wtok)

            def gate_up(e, part, c):
                n = 8 * e + 4 * part + c
                t0, nt = PART[part]
                dve.wait_ge(silu_done, n + 1)
                dve.wait_ge(up_mm, n + 1)
                if due(n - 1):
                    dve.wait_ge(h_hi_done, n - 1)
                    dve.wait_ge(h_lo_done, n - 1)
                dve.tensor_tensor(hf[c % 2][:, 0:nt], silu[c % 2][:, 0:nt], ps[:, unit_banks(e, part, c)[1], 0:nt], ALU.mult)\
                   .then_inc(hf_done, 1)
                dve.wait_ge(h_hi_done, n + 1)
                lo(h_lo[:, c, t0:t0 + nt], hf[c % 2][:, 0:nt], h_hi[:, c, t0:t0 + nt]).then_inc(h_lo_done, 1)

            def add(e, par, part):
                for j in range(4 * part, (4, NT)[part]):
                    d = NT * e + j
                    dve.wait_ge(down_mm, d + 1)
                    if due(d - NT + 1):
                        dve.wait_ge(acc_done, d - NT + 1)
                    dve.scalar_tensor_tensor(acc[:, j, :], ps[:, 4 + (par + j) % 2, :],
                                             wtok[:, j, ds(e, 1)], acc[:, j, :], ALU.mult, ALU.add)\
                       .then_inc(acc_done, 1)

            def expert(e, i, par, last=False):
                for c in range(1, FC):
                    gate_up(e, 0, c)
                gate_up(e, 1, 0)
                if last:
                    for c in range(1, FC):
                        gate_up(e, 1, c)
                add(e, par, 0)
                if not last:
                    for c in range(1, FC):
                        gate_up(e, 1, c)
                    gate_up(e + 1, 0, 0)
                add(e, par, 1)

            gate_up(0, 0, 0)
            expert(0, 0, 0)
            expert(1, 0, 1)
            pairs(dve, 1, E // 2 - 1, expert)
            expert(E - 2, 0, 0)
            expert(E - 1, 0, 1, True)

        @block.gpsimd
        def _(pool):
            own = Count()
            pool.memset(ident[:], 0.0).then_inc(pool_own, 1)
            pool.wait_ge(pool_own, own.next())
            pool.affine_select(out=ident[:], in_=ident[:], compare_op=ALU.not_equal, fill=1.0, base=0,
                               pattern=[[-1, P]], channel_multiplier=1).then_inc(const_ident, 2)
            pool.memset(f(sel[:]), 0.0).then_inc(pool_own, 1)
            pool.wait_ge(pool_own, own.next())
            pool.affine_select(out=sel[:], in_=sel[:], compare_op=ALU.not_equal, fill=1.0, base=0,
                               pattern=[[-1, B], [0, S]], channel_multiplier=1).then_inc(const_sel, 1)
            pool.memset(eye8[:], 0.0).then_inc(pool_own, 1)
            pool.wait_ge(pool_own, own.next())
            pool.affine_select(out=eye8[:], in_=eye8[:], compare_op=ALU.not_equal, fill=1.0, base=0,
                               pattern=[[1, B], [-1, B]], channel_multiplier=0).then_inc(const_eye, 1)
            pool.memset(tril[:], 1.0).then_inc(pool_own, 1)
            pool.wait_ge(pool_own, own.next())
            pool.affine_select(out=tril[:], in_=tril[:], compare_op=ALU.is_gt, fill=0.0, base=0,
                               pattern=[[1, E], [-1, E]], channel_multiplier=0).then_inc(const_ident, 1)

            pool.wait_ge(w_hi_done, 2)
            pool.tensor_tensor(wv_lo[:], w_slot[1][:], f(wv_hi[:]), ALU.subtract).then_inc(wv_lo_done, 1)
            pool.wait_ge(w_hi_done, 3)
            pool.tensor_tensor(wvi_lo[:], w_slot[0][:], f(wvi_hi[:]), ALU.subtract).then_inc(wv_lo_done, 1)

            pool.wait_ge(broadcast_mm, B)
            def square_sum(b):
                for c in range(C):
                    kt = KT[:, c, ds(b, 1), :].rearrange("p a n -> p (a n)")
                    pool.wait_ge(k_evac, 2 * C + C * b + c + 1)
                    if c == 0:
                        if due(b):
                            pool.wait_ge(k_square_mm, b)
                        pool.tensor_tensor(ksum[:], kt, kt, ALU.mult).then_inc(pool_own, 1)
                        pool.wait_ge(pool_own, own.next())
                    else:
                        pool.tensor_tensor(ksq[:], kt, kt, ALU.mult).then_inc(pool_own, 1)
                        pool.wait_ge(pool_own, own.next())
                        ins = pool.tensor_tensor(ksum[:], ksum[:], ksq[:], ALU.add)
                        if c < C - 1:
                            ins.then_inc(pool_own, 1)
                            pool.wait_ge(pool_own, own.next())
                        else:
                            ins.then_inc(k_sum, 1)

            square_sum(0)
            with pool.Fori(1, B) as b:
                own.enter(b, 1, 2 * C - 2)
                square_sum(b)
            own.leave(B - 1)

            def add_bias(b):
                pool.wait_ge(xn1_done, b + 1)
                pool.tensor_tensor(X[:, b, :], X[:, b, :], ob_sb[:], ALU.add).then_inc(ob_done, 1)

            pool.wait_ge(d_ob, 16)
            for b in range(6):
                add_bias(b)
            for u in range(C + 2):
                h, c = divmod(u, C)
                qf = QF[:, c, h * HALF:(h + 1) * HALF]
                pool.wait_ge(q_evac, u + 1)
                if c == 0:
                    if h == 1:
                        pool.wait_ge(q_square_mm, 1)
                    pool.tensor_tensor(qsum[:], qf, qf, ALU.mult).then_inc(pool_own, 1)
                    pool.wait_ge(pool_own, own.next())
                else:
                    pool.tensor_tensor(qsq[:], qf, qf, ALU.mult).then_inc(pool_own, 1)
                    pool.wait_ge(pool_own, own.next())
                    ins = pool.tensor_tensor(qsum[:], qsum[:], qsq[:], ALU.add)
                    if u in (C - 1, C + 1):
                        ins.then_inc(q_sum, 1)
                    else:
                        ins.then_inc(pool_own, 1)
                        pool.wait_ge(pool_own, own.next())
                if u == C - 1:
                    add_bias(B - 2)
                    add_bias(B - 1)
                    pool.wait_ge(wq_lo_done, 1)
                    pool.wait_ge(ob_done, B)
                    for i in range(2):
                        pool.memset(f(qs_hi[i][:]), 0.0).then_inc(qs_zero, 1)

            def k_lo(b, g):
                n = 4 * b + g
                pool.wait_ge(k_hi_done, n + 1)
                pool.tensor_tensor(ks_lo[g % 2][:, :], KT[:, g, ds(b, 1), :].rearrange("p a n -> p (a n)"),
                                   f(ks_hi[g % 2][:, :]), ALU.subtract).then_inc(k_lo_done, 1)

            def v_lo(b, g):
                n = 4 * b + g
                pool.wait_ge(vs_hi_done, n + 1)
                pool.tensor_tensor(vs_lo[g % 2][:, :, :], VV[:, ds(b, 1), :, g * P:(g + 1) * P].rearrange("p a t n -> p (a t) n"),
                                   f(vs_hi[g % 2][:, :, :]), ALU.subtract).then_inc(vs_lo_done, 1)

            def o_lo(b):
                pool.wait_ge(ot_hi_done, b + 1)
                pool.tensor_tensor(ot_lo[b % 4][:, :, :], QF[:, :, b * S:(b + 1) * S], f(ot_hi[b % 4][:, :, :]), ALU.subtract)\
                    .then_inc(ot_lo_done, 1)

            def normalise(n, g, a):
                pool.wait_ge(rec_done, 2 * n + a + 1)
                for kind, (k0, k1) in enumerate(((0, IMG), (IMGP, KEYS))):
                    p = prob[g][:, 2 * a:2 * a + 2, k0:k1]
                    pool.tensor_tensor(p, p, prec[:, g, 2 * a:2 * a + 2, kind:kind + 1].to_broadcast([S, 2, k1 - k0]), ALU.mult)\
                        .then_inc(norm_done, 1)

            def attend(b, last=False):
                for g in range(G):
                    n = 4 * b + g
                    v_lo(b, g)
                    if not last or g + 1 < G:
                        normalise(n + 1, (g + 1) % G, 1)
                    if not last or g + 3 < G:
                        k_lo(b + (g + 3) // G, (g + 3) % G)
                    if not last or g + 2 < G:
                        normalise(n + 2, (g + 2) % G, 0)
                    if last and g == G - 1:
                        for i in range(4):
                            o_lo(i)

            k_lo(0, 0)
            k_lo(0, 1)
            pool.wait_ge(q_mm, 2 * C)
            pool.wait_ge(q_sum, 2)
            pool.wait_ge(q_sum2, 1)
            for i in range(4):
                ins = pool.memset(prob[i][:, :, IMG:IMGP], 0.0)
            ins.then_inc(pool_own, 1)
            pool.wait_ge(pool_own, own.next())
            normalise(0, 0, 0)
            normalise(0, 0, 1)
            k_lo(0, 2)
            normalise(1, 1, 0)
            attend(0)
            with pool.Fori(1, B - 1) as b:
                attend(b)
            attend(B - 1, last=True)

            def e_lo(e, par):
                for k in range(3):
                    e_lo_part(e, par, k)

            def e_lo_part(e, par, k):
                w = (eg, eu, ed)[k]
                pool.wait_ge(e_hi_done, 3 * e + k + 1)
                pool.tensor_tensor(w[par][1][:], e_raw[k][:], f(w[par][0][:]), ALU.subtract).then_inc(e_lo_done, 1)

            for b in range(4, B):
                o_lo(b)
                if b == 5:
                    e_lo_part(0, 0, 0)
            e_lo_part(0, 0, 1)
            e_lo_part(0, 0, 2)
            e_lo(1, 1)
            pairs(pool, 1, E // 2, lambda e, i, par: e_lo(e, par))


NAMES = ("x", "ctxT", "ctx_txt", "ctx_last", "wkv", "wo_attn", "bo8", "wkT", "wkiT", "wvT", "wviT", "wqT", "woT", "ob",
         "cols", "wg", "wu", "wd", "wr")


def lay_out(i):
    c = np.asarray(i["ctx_2048"])
    t = c.transpose(0, 2, 1).reshape(B, C, P, CTX).transpose(0, 2, 1, 3)
    ctxT = np.zeros((B, P, C, CKEYS), c.dtype)
    ctxT[..., :IMG] = t[..., :IMG]
    ctxT[..., IMGP:KEYS] = t[..., IMG:]
    ctx_txt = t[..., IMG:].reshape(B // TB, TB, P, C, TXT).transpose(0, 2, 3, 1, 4).reshape(B // TB, P, C, TXTN)
    ctx_last = np.zeros((P, C, P), c.dtype)
    ctx_last[..., :B] = t[..., IMG - 1].transpose(1, 2, 0)

    def wT(w):
        return np.asarray(w).T.reshape(C, P, D).transpose(1, 0, 2)

    def vec(v):
        return np.asarray(v).reshape(C, P).T

    x = "L0_xattn_"
    temp = np.broadcast_to(np.asarray(i["L0_ffn_temperature"]).reshape(1, 1), (P, 1))
    cols = np.concatenate([vec(i[x + n]) for n in ("q_b", "k_b", "k_img_b", "v_b", "v_img_b", "norm_q_w", "norm_k_w",
                                                   "norm_k_img_w")] + [temp], axis=1)
    arrays = (i["x"], ctxT, ctx_txt, ctx_last, i["L0_attn_Wkv"], i["L0_attn_Wo"],
              np.broadcast_to(np.asarray(i["L0_attn_bo"]), (B, D)),
              wT(i[x + "k_w"]), wT(i[x + "k_img_w"]), wT(i[x + "v_w"]), wT(i[x + "v_img_w"]), wT(i[x + "q_w"]),
              wT(i[x + "o_w"]), np.broadcast_to(np.asarray(i[x + "o_b"]), (S, D)), cols,
              i["L0_ffn_Wg"], i["L0_ffn_Wu"], i["L0_ffn_Wd"], i["L0_ffn_Wr"])
    return {n: np.ascontiguousarray(a) for n, a in zip(NAMES, arrays)}


def kernel(**inputs):
    import concourse.bacc as bacc
    from concourse.bass_utils import run_bass_kernel_spmd

    nc = bacc.Bacc("TRN2", target_bir_lowering=False, num_devices=1)
    arrays = {f"in_{n}": a for n, a in lay_out(inputs).items()}
    args = [nc.dram_tensor(n, a.shape, mybir.dt.from_np(a.dtype), kind="ExternalInput").ap() for n, a in arrays.items()]
    out = nc.dram_tensor("out", (NTOK, D), F32, kind="ExternalOutput").ap()
    decoder(nc, *args, out)
    r = run_bass_kernel_spmd(nc, [arrays], core_ids=[0])
    return r.results[0]["out"].reshape(B, S, D)
```
